# Optimizing a Trainium2 kernel written in Bass

```python
import numpy as np
import jax
import jax.numpy as jnp

def _softmax(x, axis=-1):
    return jax.nn.softmax(x, axis=axis)

def _gelu(x):
    return jax.nn.gelu(x, approximate=True)

def _silu(x):
    return jax.nn.silu(x)

def _sigmoid(x):
    return jax.nn.sigmoid(x)

def _layernorm(x, axis=-1, eps=1e-05):
    m = jnp.mean(x, axis=axis, keepdims=True)
    v = jnp.var(x, axis=axis, keepdims=True)
    return (x - m) / jnp.sqrt(v + eps)

def _scatter_add(tgt, idx, src, axis=0):
    return tgt.at[idx].add(src)

def _segment_sum(src, seg, n):
    return jax.ops.segment_sum(src, seg, n)
kernel_name = 'mk_gnn_ffn_d2_gnn_r16_6e0166'

def setup_inputs(seed: int=0):
    np.random.seed(seed)
    _w = jnp.asarray

    def _rec_inputs():
        import jax
        import jax.numpy as jnp
        _gk = jax.random.key(seed)
        x = -0.0002117 + 1 * jax.random.normal(jax.random.fold_in(_gk, 1), (6250, 256), jnp.float32)
        src = jax.random.randint(jax.random.fold_in(_gk, 2), (100000,), 0, 6250, jnp.int32)
        dst = jnp.minimum((6250 * jax.random.uniform(jax.random.fold_in(_gk, 3), (100000,)) ** 2.0).astype(jnp.int32), 99999)
        _o = jnp.argsort(dst, stable=True)
        src = src[_o]
        dst = dst[_o]
        edge_attr_64 = 0.000189758 + 1.00013 * jax.random.normal(jax.random.fold_in(_gk, 13), (100000, 64), jnp.float32)
        edge_weight = jax.random.uniform(jax.random.fold_in(_gk, 15), (100000,), jnp.float32, 0.0, 1)
        return (x, src, dst, edge_attr_64, edge_weight)
    x, src, dst, edge_attr_64, edge_weight = _rec_inputs()

    def _L0_gnn_setup():
        import jax, jax.numpy as jnp
        import numpy as np
        N = 6250
        E = 200000
        D_IN = 256
        D_OUT = 256
        EPS = 1e-12
        key = jax.random.key(seed)
        k1, k2, k3, k4, k5, k6 = jax.random.split(key, 6)
        x = jax.random.normal(k1, (N, D_IN), dtype=jnp.float32)
        edge_src = jax.random.randint(k2, (E,), 0, N, dtype=jnp.int32)
        edge_dst = jax.random.randint(k3, (E,), 0, N, dtype=jnp.int32)
        edge_w = jax.random.uniform(k4, (E,), dtype=jnp.float32)
        w_self = jax.random.normal(k5, (D_OUT, D_IN), dtype=jnp.float32) * 0.05
        w_neigh = jax.random.normal(k6, (D_OUT, D_IN), dtype=jnp.float32) * 0.05
        return {'x': x, 'edge_src': edge_src, 'edge_dst': edge_dst, 'edge_w': edge_w, 'w_self': w_self, 'w_neigh': w_neigh}
    _L0_gnn_all = _L0_gnn_setup()
    _L0_gnn_in = {k: v for k, v in _L0_gnn_all.items() if k in ('w_self', 'w_neigh')}
    del _L0_gnn_all

    def _L0_ffn_setup():
        import jax, jax.numpy as jnp
        import numpy as np
        B, A = (256, 8)
        IN, OUT = (256, 256)
        SH1, SH2 = (256, 128)
        EH1, EH2 = (128, 64)
        E, TOPK = (4, 2)

        def _shared_mlp(x, W1, b1, W2, b2, W3, b3):
            h = jax.nn.relu(x @ W1 + b1)
            h = jax.nn.relu(h @ W2 + b2)
            return h @ W3 + b3

        def _experts_mlp(x, eW1, eb1, eW2, eb2, eW3, eb3):
            h = jax.nn.relu(jnp.einsum('baf,efh->ebah', x, eW1) + eb1[:, None, None, :])
            h = jax.nn.relu(jnp.einsum('ebah,ehg->ebag', h, eW2) + eb2[:, None, None, :])
            o = jnp.einsum('ebag,ego->ebao', h, eW3) + eb3[:, None, None, :]
            return jnp.moveaxis(o, 0, -1)
        key = jax.random.key(seed)
        ks = jax.random.split(key, 16)
        s = 0.05
        return {'x': jax.random.normal(ks[0], (B, A, IN), jnp.float32), 'sW1': jax.random.normal(ks[1], (IN, SH1), jnp.float32) * s, 'sb1': jnp.zeros((SH1,), jnp.float32), 'sW2': jax.random.normal(ks[2], (SH1, SH2), jnp.float32) * s, 'sb2': jnp.zeros((SH2,), jnp.float32), 'sW3': jax.random.normal(ks[3], (SH2, OUT), jnp.float32) * s, 'sb3': jnp.zeros((OUT,), jnp.float32), 'eW1': jax.random.normal(ks[4], (E, IN, EH1), jnp.float32) * s, 'eb1': jnp.zeros((E, EH1), jnp.float32), 'eW2': jax.random.normal(ks[5], (E, EH1, EH2), jnp.float32) * s, 'eb2': jnp.zeros((E, EH2), jnp.float32), 'eW3': jax.random.normal(ks[6], (E, EH2, OUT), jnp.float32) * s, 'eb3': jnp.zeros((E, OUT), jnp.float32), 'gW': jax.random.normal(ks[7], (IN, E), jnp.float32) * s, 'gb': jnp.zeros((E,), jnp.float32)}
    _L0_ffn_all = _L0_ffn_setup()
    _L0_ffn_in = {k: v for k, v in _L0_ffn_all.items() if k in ('sW1', 'sb1', 'sW2', 'sb2', 'sW3', 'sb3', 'eW1', 'eb1', 'eW2', 'eb2', 'eW3', 'eb3', 'gW', 'gb')}
    del _L0_ffn_all

    def _L1_gnn_setup():
        import jax, jax.numpy as jnp
        import numpy as np
        N_NODES = 3125
        N_EDGES = 50000
        NODE_IN = 256
        EDGE_OUT = 64
        GLOBAL_IN = 128
        NODE_OUT = 256
        HIDDEN = 512
        N_GRAPHS = 64
        key = jax.random.key(seed)
        ks = jax.random.split(key, 8)
        x = jax.random.normal(ks[0], (N_NODES, NODE_IN), dtype=jnp.float32)
        edge_index = jax.random.randint(ks[1], (2, N_EDGES), 0, N_NODES, dtype=jnp.int64)
        edge_attr = jax.random.normal(ks[2], (N_EDGES, EDGE_OUT), dtype=jnp.float32)
        u = jax.random.normal(ks[3], (N_GRAPHS, GLOBAL_IN), dtype=jnp.float32)
        batch = jnp.sort(jax.random.randint(ks[4], (N_NODES,), 0, N_GRAPHS, dtype=jnp.int64))
        in_dim = NODE_IN + EDGE_OUT + GLOBAL_IN
        b1s = 1.0 / np.sqrt(in_dim)
        b2s = 1.0 / np.sqrt(HIDDEN)
        W1 = jax.random.uniform(ks[5], (in_dim, HIDDEN), dtype=jnp.float32, minval=-b1s, maxval=b1s)
        b1 = jnp.zeros((HIDDEN,), dtype=jnp.float32)
        W2 = jax.random.uniform(ks[6], (HIDDEN, NODE_OUT), dtype=jnp.float32, minval=-b2s, maxval=b2s)
        b2 = jnp.zeros((NODE_OUT,), dtype=jnp.float32)
        return {'x': x, 'edge_index': edge_index, 'edge_attr': edge_attr, 'u': u, 'batch': batch, 'W1': W1, 'b1': b1, 'W2': W2, 'b2': b2}
    _L1_gnn_all = _L1_gnn_setup()
    _L1_gnn_in = {k: v for k, v in _L1_gnn_all.items() if k in ('u', 'W1', 'b1', 'W2', 'b2')}
    del _L1_gnn_all

    def _L1_ffn_setup():
        import jax, jax.numpy as jnp
        import numpy as np
        B, S, D, H, E, K = (8, 512, 256, 1024, 8, 2)
        key = jax.random.key(seed)
        ks = jax.random.split(key, 7)
        s_in = 1.0 / np.sqrt(D)
        s_hid = 1.0 / np.sqrt(H)
        return {'x': jax.random.normal(ks[0], (B, S, D), dtype=jnp.float32), 'Wg': jax.random.uniform(ks[1], (E, D), jnp.float32, -s_in, s_in), 'bg': jax.random.uniform(ks[2], (E,), jnp.float32, -s_in, s_in), 'W1': jax.random.uniform(ks[3], (E, H, D), jnp.float32, -s_in, s_in), 'b1': jax.random.uniform(ks[4], (E, H), jnp.float32, -s_in, s_in), 'W2': jax.random.uniform(ks[5], (E, D, H), jnp.float32, -s_hid, s_hid), 'b2': jax.random.uniform(ks[6], (E, D), jnp.float32, -s_hid, s_hid)}
    _L1_ffn_all = _L1_ffn_setup()
    _L1_ffn_in = {k: v for k, v in _L1_ffn_all.items() if k in ('Wg', 'bg', 'W1', 'b1', 'W2', 'b2')}
    del _L1_ffn_all
    return {'x': x, 'src': src, 'dst': dst, 'edge_attr_64': edge_attr_64, 'edge_weight': edge_weight, 'L0_gnn_w_self': _L0_gnn_in['w_self'], 'L0_gnn_w_neigh': _L0_gnn_in['w_neigh'], 'L0_ffn_sW1': _L0_ffn_in['sW1'], 'L0_ffn_sb1': _L0_ffn_in['sb1'], 'L0_ffn_sW2': _L0_ffn_in['sW2'], 'L0_ffn_sb2': _L0_ffn_in['sb2'], 'L0_ffn_sW3': _L0_ffn_in['sW3'], 'L0_ffn_sb3': _L0_ffn_in['sb3'], 'L0_ffn_eW1': _L0_ffn_in['eW1'], 'L0_ffn_eb1': _L0_ffn_in['eb1'], 'L0_ffn_eW2': _L0_ffn_in['eW2'], 'L0_ffn_eb2': _L0_ffn_in['eb2'], 'L0_ffn_eW3': _L0_ffn_in['eW3'], 'L0_ffn_eb3': _L0_ffn_in['eb3'], 'L0_ffn_gW': _L0_ffn_in['gW'], 'L0_ffn_gb': _L0_ffn_in['gb'], 'L1_gnn_u': _L1_gnn_in['u'], 'L1_gnn_W1': _L1_gnn_in['W1'], 'L1_gnn_b1': _L1_gnn_in['b1'], 'L1_gnn_W2': _L1_gnn_in['W2'], 'L1_gnn_b2': _L1_gnn_in['b2'], 'L1_ffn_Wg': _L1_ffn_in['Wg'], 'L1_ffn_bg': _L1_ffn_in['bg'], 'L1_ffn_W1': _L1_ffn_in['W1'], 'L1_ffn_b1': _L1_ffn_in['b1'], 'L1_ffn_W2': _L1_ffn_in['W2'], 'L1_ffn_b2': _L1_ffn_in['b2']}

def reference(x, src, dst, edge_attr_64, edge_weight, L0_gnn_w_self, L0_gnn_w_neigh, L0_ffn_sW1, L0_ffn_sb1, L0_ffn_sW2, L0_ffn_sb2, L0_ffn_sW3, L0_ffn_sb3, L0_ffn_eW1, L0_ffn_eb1, L0_ffn_eW2, L0_ffn_eb2, L0_ffn_eW3, L0_ffn_eb3, L0_ffn_gW, L0_ffn_gb, L1_gnn_u, L1_gnn_W1, L1_gnn_b1, L1_gnn_W2, L1_gnn_b2, L1_ffn_Wg, L1_ffn_bg, L1_ffn_W1, L1_ffn_b1, L1_ffn_W2, L1_ffn_b2):
    import jax
    import jax.numpy as jnp

    def _L0_gnn_ref(x, edge_src, edge_dst, edge_w, w_self, w_neigh):
        import jax, jax.numpy as jnp
        import numpy as np
        N = 6250
        E = 200000
        D_IN = 256
        D_OUT = 256
        EPS = 1e-12
        x_self = x @ w_self.T
        msgs = edge_w[:, None] * x[edge_src]
        x_neigh = jax.ops.segment_sum(msgs, edge_dst, num_segments=N)
        x_neigh = x_neigh @ w_neigh.T
        out = x_self + x_neigh
        norm = jnp.sqrt(jnp.sum(out * out, axis=1, keepdims=True))
        return out / jnp.maximum(norm, EPS)

    def _L0_ffn_ref(x, sW1, sb1, sW2, sb2, sW3, sb3, eW1, eb1, eW2, eb2, eW3, eb3, gW, gb):
        import jax, jax.numpy as jnp
        import numpy as np
        B, A = (256, 8)
        IN, OUT = (256, 256)
        SH1, SH2 = (256, 128)
        EH1, EH2 = (128, 64)
        E, TOPK = (4, 2)

        def _shared_mlp(x, W1, b1, W2, b2, W3, b3):
            h = jax.nn.relu(x @ W1 + b1)
            h = jax.nn.relu(h @ W2 + b2)
            return h @ W3 + b3

        def _experts_mlp(x, eW1, eb1, eW2, eb2, eW3, eb3):
            h = jax.nn.relu(jnp.einsum('baf,efh->ebah', x, eW1) + eb1[:, None, None, :])
            h = jax.nn.relu(jnp.einsum('ebah,ehg->ebag', h, eW2) + eb2[:, None, None, :])
            o = jnp.einsum('ebag,ego->ebao', h, eW3) + eb3[:, None, None, :]
            return jnp.moveaxis(o, 0, -1)
        all_out = _experts_mlp(x, eW1, eb1, eW2, eb2, eW3, eb3)
        shared = _shared_mlp(x, sW1, sb1, sW2, sb2, sW3, sb3)
        gates = jax.nn.softmax(x @ gW + gb, axis=-1)
        topv, topi = jax.lax.top_k(gates, TOPK)
        topw = jax.nn.softmax(topv, axis=-1)
        sel = jnp.take_along_axis(all_out, topi[:, :, None, :], axis=-1)
        gated = jnp.sum(sel * topw[:, :, None, :], axis=-1)
        return shared + gated

    def _L1_gnn_ref(x, edge_index, edge_attr, u, batch, W1, b1, W2, b2):
        import jax, jax.numpy as jnp
        import numpy as np
        N_NODES = 3125
        N_EDGES = 50000
        NODE_IN = 256
        EDGE_OUT = 64
        GLOBAL_IN = 128
        NODE_OUT = 256
        HIDDEN = 512
        N_GRAPHS = 64
        n = x.shape[0]
        src = edge_index[0]
        sums = jax.ops.segment_sum(edge_attr, src, num_segments=n)
        counts = jax.ops.segment_sum(jnp.ones((edge_attr.shape[0],), edge_attr.dtype), src, num_segments=n)
        edge_attr_agg = sums / jnp.maximum(counts, 1.0)[:, None]
        u_expanded = u[batch]
        combined = jnp.concatenate([x, edge_attr_agg, u_expanded], axis=1)
        h = jax.nn.relu(combined @ W1 + b1)
        return h @ W2 + b2

    def _L1_ffn_ref(x, Wg, bg, W1, b1, W2, b2):
        import jax, jax.numpy as jnp
        import numpy as np
        B, S, D, H, E, K = (8, 512, 256, 1024, 8, 2)
        gate_scores = jnp.einsum('bsd,ed->bse', x, Wg) + bg
        topk_scores, topk_idx = jax.lax.top_k(gate_scores, K)
        topk_probs = jax.nn.softmax(topk_scores, axis=-1)
        combine = jnp.sum(topk_probs[..., None] * jax.nn.one_hot(topk_idx, E, dtype=x.dtype), axis=-2)
        out = jnp.zeros_like(x)
        for e in range(E):
            h = jax.nn.relu(jnp.einsum('bsd,hd->bsh', x, W1[e]) + b1[e])
            y = jnp.einsum('bsh,dh->bsd', h, W2[e]) + b2[e]
            out = out + combine[..., e:e + 1] * y
        return out
    edge_index = jnp.stack([src, dst])
    batch0 = jnp.zeros((6250,), jnp.int32)
    x = x + _L0_gnn_ref(_layernorm(x, axis=-1), src, dst, edge_weight, L0_gnn_w_self, L0_gnn_w_neigh)
    x = x + _L0_ffn_ref(_layernorm(x, axis=-1)[None], L0_ffn_sW1, L0_ffn_sb1, L0_ffn_sW2, L0_ffn_sb2, L0_ffn_sW3, L0_ffn_sb3, L0_ffn_eW1, L0_ffn_eb1, L0_ffn_eW2, L0_ffn_eb2, L0_ffn_eW3, L0_ffn_eb3, L0_ffn_gW, L0_ffn_gb)[0]
    x = x + _L1_gnn_ref(_layernorm(x, axis=-1), edge_index, edge_attr_64, L1_gnn_u, batch0, L1_gnn_W1, L1_gnn_b1, L1_gnn_W2, L1_gnn_b2)
    x = x + _L1_ffn_ref(_layernorm(x, axis=-1)[None], L1_ffn_Wg, L1_ffn_bg, L1_ffn_W1, L1_ffn_b1, L1_ffn_W2, L1_ffn_b2)[0]
    return x

_drawn_inputs = setup_inputs


def setup_inputs(seed=0):
    import zlib

    import numpy as np

    out = dict(_drawn_inputs(seed))
    spreads = {'L0_ffn_sb1': (0.0, 0.282),
     'L0_ffn_sb2': (0.0, 0.1),
     'L0_ffn_sb3': (0.0, 0.1),
     'L0_ffn_eb1': (0.0, 0.55),
     'L0_ffn_eb2': (0.0, 0.325),
     'L0_ffn_eb3': (0.0, 0.1),
     'L0_ffn_gb': (0.0, 0.312),
     'L1_gnn_b1': (0.0, 0.1),
     'L1_gnn_b2': (0.0, 0.1)}
    factors = {'L1_ffn_b1': 5.726, 'L1_ffn_b2': 4.569}
    for name, (base, spread) in spreads.items():
        noise = np.random.default_rng([zlib.crc32(name.encode()), seed]).standard_normal(out[name].shape)
        drawn = base * np.exp(spread * noise) if base else spread * noise
        out[name] = jnp.asarray(drawn.astype(out[name].dtype))
    for name, factor in factors.items():
        out[name] = (out[name] * factor).astype(out[name].dtype)
    return out
```

```python
import concourse.bass as bass
from concourse import mybir
from contextlib import ExitStack

P = 128
D = 256
N = 6250
NT = -(-N // P)
NP = NT * P
G = 7
NG = NT // G
E = 100000
RUN = 4
NC = -(-E // (P * RUN)) * RUN
EP = NC * P
PAD_KEY = NP
NB = NT + 1
STEP = 16
NI = -(-(-(-E // P) + NT - 1) // STEP) * STEP
STEP4 = 8
NI4 = -(-(-(-E // (P * RUN)) + NT - 1) // STEP4) * STEP4
IJ = -(-NI // P)
EA = 64
ER = EA + 2
RING = 8
NX = 8
HX = 1024
NBLK = (2 * NP + NX * (P - 1)) // P
NBLK += NBLK % 2
LN_EPS = 1e-5

f32 = mybir.dt.float32
i32 = mybir.dt.int32
u8 = mybir.dt.uint8
ALU = mybir.AluOpType
ACT = mybir.ActivationFunctionType
AX = mybir.AxisListType
ds = bass.ds


class Chain:

    def __init__(self, engine, sem, base=0):
        self.engine, self.sem, self.base, self.n = engine, sem, base, 0

    def add(self, instruction):
        self.n += 1
        instruction.then_inc(self.sem, 1)

    def sync(self):
        self.engine.wait_ge(self.sem, self.base + self.n)


def wide(v, n):
    return v[:, :].unsqueeze(2).to_broadcast([P, G, n])


DENSE0_OWN = 44
DENSE1_OWN = 50
HALVES = ((0, 4 * P), (4 * P, G * P))
SC = 14
assert NC % (2 * SC) == 0


def build(nc, a, out):
    ctx = ExitStack()

    def sb(name, shape, dt=f32, scope=None):
        return (scope or ctx).enter_context(nc.sbuf_tensor(name, shape, dt))

    def sem(name):
        return ctx.enter_context(nc.semaphore(name))

    def dram(name, shape, dt=f32):
        return nc.dram_tensor(name, shape, dt, kind="Internal").ap()

    with ctx:
        xn_d = dram("xn_rows", [NP, D])
        edges_d = dram("sorted_edges", [EP, ER])
        item_d = dram("item_rows", [4, IJ * P], i32)
        xd_d = dram("dispatched", [(NBLK + 2) * P, D])
        yd_d = dram("expert_rows", [NBLK * P, D])
        psum = ctx.enter_context(nc.psum_tensor("psum", [P, 8, 512], f32))

        ident = sb("ident", [P, P])
        iota_r = sb("iota_r", [P, P])
        upper = sb("upper", [P, P])
        ones = sb("ones", [P, P])
        xr = sb("xr", [P, NT, D])
        rstd = sb("rstd", [P, NT])
        nmr = sb("nmr", [P, NT])
        mean_var = sb("mean_var", [P, NT, 2])
        sd = sb("sd", [P, NT])
        eps = sb("eps", [P, 1])
        early = ctx.enter_context(ExitStack())
        items = sb("items", [4, IJ * P], i32, early)
        pos_i = sb("pos_i", [P, NC], i32, early)
        acc = sb("acc", [P, NB, D], f32, early)

        s_const = sem("constants")
        s_x = sem("x_loaded")
        s_dst = sem("dst_loaded")
        s_src = sem("src_loaded")
        s_own = sem("vector_own")
        s_var = sem("variance_ready")
        s_sd = sem("deviation_ready")
        s_ln = sem("rstd_ready")
        s_xn = sem("xn_ready")
        s_xst = sem("xn_stored")
        s_cum = sem("counts_ready")
        s_off = sem("offsets_in_psum")
        s_base = sem("base_ready")
        s_tab = sem("tables_ready")
        s_tabT = sem("tables_transposed")
        s_row = sem("rows_ready")
        s_rst = sem("rows_stored")
        s_rld = sem("rows_loaded")
        s_cidx = sem("chunk_indices")
        s_pg = sem("item_rows_gathered")
        s_pf = sem("item_rows_ready")
        s_pt = sem("item_rows_transposed")
        s_pe = sem("item_columns_ready")
        s_z = sem("zero_ready")
        s_xdz = sem("dispatch_zeroed")

        s_turn_p = sem("turns_of_pool")
        s_turn_v = sem("turns_of_vector")
        s_turn_a = sem("turns_of_scalar")

        def alone(engine, turns):
            engine.sem_inc(turns, 1)

        def normalise(dve, own, x, g, ln, s_var, s_sd, s_rstd):
            nc.vector.memset(ln["nil"][:, 2:3], 0.0)
            for k in range(G):
                own.add(nc.vector.bn_stats(ln["stats"][:, k, :], x[:, ds(g * G + k, 1), :].squeeze(1)))
            own.sync()
            nc.vector.memset(ln["nil"][:, 0:1], 0.0)
            for k in range(G):
                own.add(nc.vector.bn_aggr(ln["mv"][:, k, :], ln["stats"][:, k, :]))
            own.sync()
            nc.vector.memset(ln["nil"][:, 1:2], 0.0).then_inc(s_var, 1)
            dve.wait_ge(s_sd, g + 1)
            own.add(nc.vector.reciprocal(ln["rstd"][:, :], ln["sd"][:, :]))
            own.sync()
            nc.vector.scalar_tensor_tensor(ln["nmr"][:, :], ln["mv"][:, :, 0], -1.0, ln["rstd"][:, :],
                                           ALU.mult, ALU.mult).then_inc(s_rstd, 1)

        def top_two(own, gt, g1, rev, n):
            for v, o, eq, sc, key, src in (("v1", "o1", "eq", "sc", "k1", "g"), ("v2", "o2", "eq2", "sc2", "k2", "g2")):
                if src == "g2":
                    own.add(nc.vector.scalar_tensor_tensor(gt["g2"][:, :, :], gt["o1"][:, :, :], -1e30, gt["g"][:, :, :], ALU.mult, ALU.add))
                    own.sync()
                own.add(nc.vector.tensor_reduce(g1[v][:, :], gt[src][:, :, :], AX.X, ALU.max))
                own.sync()
                own.add(nc.vector.tensor_tensor(gt[eq][:, :, :], gt[src][:, :, :], wide(g1[v], n), ALU.is_equal))
                own.sync()
                own.add(nc.vector.tensor_tensor(gt[sc][:, :, :], gt[eq][:, :, :], rev[:, 0:n].unsqueeze(1).to_broadcast([P, G, n]), ALU.mult))
                own.sync()
                own.add(nc.vector.tensor_reduce(g1[key][:, :], gt[sc][:, :, :], AX.X, ALU.max))
                own.sync()
                own.add(nc.vector.tensor_tensor(gt[o][:, :, :], gt[sc][:, :, :], wide(g1[key], n), ALU.is_equal))
                own.sync()

        def two_weights(own, g1):
            own.add(nc.vector.tensor_scalar(g1["t"][:, :], g1["x"][:, :], 1.0, None, ALU.add))
            own.sync()
            own.add(nc.vector.reciprocal(g1["w1"][:, :], g1["t"][:, :]))
            own.sync()
            own.add(nc.vector.tensor_tensor(g1["w2"][:, :], g1["x"][:, :], g1["w1"][:, :], ALU.mult))
            own.sync()

        with ExitStack() as ph:
            it_src = sb("it_src", [P, IJ * P], i32, ph)
            it_rel = sb("it_rel", [P, IJ * P], f32, ph)
            it_w = sb("it_w", [P, IJ * P], f32, ph)
            kb = sb("kb", [P, NC], f32, ph)
            base = sb("base", [P, NB + 2], f32, ph)
            bnum = sb("bnum", [P, NB + 2], f32, ph)
            with ExitStack() as ph1:
                iota_i = sb("iota_i", [P, P], i32, ph1)
                dst_i = sb("dst_i", [P, NC], i32, ph1)
                src_i = sb("src_i", [P, NC], i32, ph1)
                dst_f = sb("dst_f", [P, NC], f32, ph1)
                src_f = sb("src_f", [P, NC], f32, ph1)
                junk = sb("junk", [P, NC], f32, ph1)
                junk2 = sb("junk2", [P, NC], f32, ph1)
                nil = sb("nil", [P, 4], f32, ph1)
                thr = sb("thr", [P, NB], f32, ph1)
                thr_i = sb("thr_i", [P, NB + 2], i32, ph1)
                item_i = sb("item_i", [P, IJ], i32, ph1)
                item_f = sb("item_f", [P, IJ], f32, ph1)
                cum = sb("cum", [P, 2, NB + 1], f32, ph1)
                cnt = sb("cnt", [P, NB], f32, ph1)
                starts = sb("starts", [P, 2, NB + 1], f32, ph1)
                st_i = sb("st_i", [P, 2, NB + 1], i32, ph1)
                up_i = sb("up_i", [P, 2, NB + 1], i32, ph1)
                c0_i = sb("c0_i", [P, 2, NB + 1], i32, ph1)
                c1_i = sb("c1_i", [P, 2, NB + 1], i32, ph1)
                ni = sb("ni", [P, 2, NB], f32, ph1)
                nz = sb("nz", [P, 2, NB], f32, ph1)
                iend = sb("iend", [P, 2, NB], f32, ph1)
                dif = sb("dif", [P, 2, NB], f32, ph1)
                ddif = sb("ddif", [P, 2, NT], f32, ph1)
                geq = sb("geq", [P, IJ, NT], f32, ph1)
                prod = sb("prod", [P, IJ, NT], f32, ph1)
                tab = sb("tab", [P, 4, IJ], f32, ph1)
                cidx = sb("cidx", [P, IJ], i32, ph1)
                tabT = sb("tabT", [4 * IJ, P], i32, ph1)
                t128 = sb("t128", [P, IJ], f32, ph1)
                row_i = sb("row_i", [P, IJ, 2, P], i32, ph1)
                row_w = sb("row_w", [P, IJ, P], f32, ph1)
                row_f = sb("row_f", [P, IJ, 2, P], f32, ph1)
                stats = sb("stats", [P, G, 6], f32, ph1)
                mv = sb("mv", [P, G, 2], f32, ph1)
                xn_st = sb("xn_st", [P, G, D], f32, ph1)
                zero = sb("zero", [P, 2 * D], f32, ph1)

                with nc.Block() as block:

                    @block.sync
                    def _(sp):
                        sp.dma_start(dst_i[:, :], a["dst"].rearrange("(p c) -> p c", p=P)).then_inc(s_dst, 16)
                        sp.dma_start(src_i[:, :], a["src"].rearrange("(p c) -> p c", p=P)).then_inc(s_src, 16)
                        sp.dma_start(xr[:, :, :], a["x"].rearrange("(t p) d -> p t d", p=P)).then_inc(s_x, 16)
                        with sp.Fori(0, NG) as g:
                            sp.wait_ge(s_xn, G * g + G)
                            sp.dma_start(
                                xn_d[ds(g * (G * P), G * P), :].rearrange("(t p) d -> p t d", p=P),
                                xn_st[:, :, :]).then_inc(s_xst, 16)
                        sp.wait_ge(s_xst, 16 * NG)

                    @block.gpsimd
                    def _(pool):
                        own = Chain(pool, s_const)
                        own.add(pool.memset(ident[:, :], 0.0))
                        own.add(pool.memset(ones[:, :], 1.0))
                        own.add(pool.iota(iota_i[:, :], pattern=[[1, P]], base=0, channel_multiplier=0))
                        own.add(pool.iota(thr_i[:, :], pattern=[[P, NB + 2]], base=0, channel_multiplier=0))
                        own.add(pool.memset(acc[:, :, :], 0.0))
                        own.add(pool.memset(eps[:, :], LN_EPS))
                        own.add(pool.iota(item_i[:, :], pattern=[[P, IJ]], base=0, channel_multiplier=1))
                        own.sync()
                        own.add(pool.affine_select(out=ident[:, :], in_=ident[:, :], compare_op=ALU.not_equal,
                                                   fill=1.0, base=0, pattern=[[-1, P]], channel_multiplier=1))
                        own.add(pool.affine_select(out=upper[:, :], in_=ones[:, :], compare_op=ALU.is_gt,
                                                   fill=0.0, base=0, pattern=[[1, P]], channel_multiplier=-1))
                        pool.wait_ge(s_cidx, 1)
                        for j in range(IJ):
                            off = bass.IndirectOffsetOnAxis(ap=cidx[:, j:j + 1], axis=0)
                            for n, name in enumerate(("src", "dst")):
                                pool.indirect_dma_start(
                                    out=row_i[:, j, n, :], out_offset=None,
                                    in_=a[name].rearrange("(c p) -> c p", p=P), in_offset=off).then_inc(s_pg, 16)
                            pool.indirect_dma_start(
                                out=row_w[:, j, :], out_offset=None,
                                in_=a["w"].rearrange("(c p) -> c p", p=P), in_offset=off).then_inc(s_pg, 16)

                    @block.scalar
                    def _(act):
                        act.wait_ge(s_z, 1)
                        act.dma_start(xd_d.rearrange("(p r c) d -> p r (c d)", p=P, c=2),
                                      zero[:, :].unsqueeze(1).to_broadcast([P, NBLK // 2 + 1, 2 * D])).then_inc(s_xdz, 16)
                        act.wait_ge(s_var, 1)
                        nc.scalar.activation(sd[:, :], mean_var[:, :, 1], ACT.Sqrt, bias=eps[:, :]).then_inc(s_sd, 1)
                        act.wait_ge(s_ln, 1)
                        with act.Fori(0, NG) as g:
                            act.wait_ge(s_xst, 16 * g)
                            for k in range(G):
                                t = g * G + k
                                nc.scalar.activation(xn_st[:, k, :], xr[:, ds(t, 1), :], ACT.Identity,
                                                     bias=nmr[:, ds(t, 1)], scale=rstd[:, ds(t, 1)]).then_inc(s_xn, 1)
                        act.wait_ge(s_xdz, 16)

                    @block.vector
                    def _(dve):
                        own = Chain(dve, s_own)
                        nc.vector.memset(zero[:, :], 0.0).then_inc(s_z, 1)
                        dve.wait_ge(s_const, 9)
                        own.add(nc.vector.tensor_copy(iota_r[:, :], iota_i[:, :]))
                        own.add(nc.vector.tensor_copy(thr[:, :], thr_i[:, 1:NB + 1]))
                        own.add(nc.vector.tensor_copy(item_f[:, :], item_i[:, :]))
                        own.add(nc.vector.memset(cum[:, :, 0:1], 0.0))
                        dve.wait_ge(s_dst, 16)
                        own.add(nc.vector.tensor_copy(dst_f[:, :], dst_i[:, :]))
                        dve.wait_ge(s_src, 16)
                        own.add(nc.vector.tensor_copy(src_f[:, :], src_i[:, :]))
                        own.sync()
                        own.add(nc.vector.tensor_scalar(dst_i[:, :], src_i[:, :], 7, None, ALU.arith_shift_right))
                        own.sync()
                        own.add(nc.vector.tensor_copy(kb[:, :], dst_i[:, :]))
                        own.add(nc.vector.tensor_scalar(bnum[:, :], thr_i[:, :], 1.0 / P, None, ALU.mult))
                        with dve.Fori(0, NB) as b:
                            dve.wait_ge(s_own, own.n - 1 + 2 * b)
                            nc.vector.tensor_scalar(junk[:, :], dst_f[:, :], thr[:, ds(b, 1)], None,
                                                    ALU.is_lt, ALU.add, accum_out=cum[:, 0, ds(b + 1, 1)]).then_inc(s_own, 1)
                            dve.wait_ge(s_own, own.n + 2 * b)
                            nc.vector.tensor_scalar(junk2[:, :], src_f[:, :], thr[:, ds(b, 1)], None,
                                                    ALU.is_lt, ALU.add, accum_out=cum[:, 1, ds(b + 1, 1)]).then_inc(s_own, 1)
                        own.n += 2 * NB
                        own.sync()
                        own.add(nc.vector.tensor_tensor(cnt[:, :], cum[:, 1, 1:NB + 1], cum[:, 1, 0:NB], ALU.subtract))
                        own.sync()
                        nc.vector.memset(t128[:, :], 0.0).then_inc(s_cum, 1)
                        dve.wait_ge(s_off, 1)
                        own.add(nc.vector.tensor_copy(starts[:, :, :], psum[:, 0, 0:2 * (NB + 1)].rearrange("p (k b) -> p k b", k=2)))
                        own.sync()
                        own.add(nc.vector.tensor_copy(st_i[:, :, :], starts[:, :, :]))
                        for k, size in enumerate((P, P * RUN)):
                            own.add(nc.vector.tensor_scalar(up_i[:, k, :], starts[:, k, :], float(size - 1), None, ALU.add))
                        own.add(nc.vector.tensor_tensor(base[:, 0:NB], psum[:, 1, 0:NB], starts[:, 1, 0:NB], ALU.add))
                        own.sync()
                        for k, size in enumerate((P, P * RUN)):
                            shift = size.bit_length() - 1
                            own.add(nc.vector.tensor_scalar(c0_i[:, k, :], st_i[:, k, :], shift, None, ALU.arith_shift_right))
                            own.add(nc.vector.tensor_scalar(c1_i[:, k, :], up_i[:, k, :], shift, None, ALU.arith_shift_right))
                        own.add(nc.vector.tensor_tensor(nz[:, :, :], starts[:, :, 1:NB + 1], starts[:, :, 0:NB], ALU.is_gt))
                        own.add(nc.vector.tensor_scalar(base[:, 0:NB], base[:, 0:NB], 1.0, None, ALU.subtract))
                        own.sync()
                        own.add(nc.vector.tensor_tensor(ni[:, :, :], c1_i[:, :, 1:NB + 1], c0_i[:, :, 0:NB], ALU.subtract))
                        own.sync()
                        own.add(nc.vector.tensor_tensor(ni[:, :, :], ni[:, :, :], nz[:, :, :], ALU.mult))
                        own.sync()
                        for k in range(2):
                            own.add(nc.vector.tensor_tensor_scan(iend[:, k, :], ni[:, k, :], ni[:, k, :], 0.0, ALU.add, ALU.bypass))
                        own.sync()
                        own.add(nc.vector.tensor_tensor(dif[:, :, :], ni[:, :, :], iend[:, :, :], ALU.subtract))
                        own.sync()
                        own.add(nc.vector.tensor_tensor(dif[:, :, :], dif[:, :, :], c0_i[:, :, 0:NB], ALU.add))
                        own.sync()
                        own.add(nc.vector.tensor_tensor(ddif[:, :, :], dif[:, :, 1:NB], dif[:, :, 0:NT], ALU.subtract))
                        own.sync()
                        for k in range(2):
                            own.add(nc.vector.tensor_tensor(geq[:, :, :], iend[:, k, 0:NT].unsqueeze(1).to_broadcast([P, IJ, NT]),
                                                            item_f[:, :].unsqueeze(2).to_broadcast([P, IJ, NT]), ALU.is_le))
                            own.sync()
                            own.add(nc.vector.tensor_reduce(tab[:, k, :], geq[:, :, :], AX.X, ALU.add))
                            own.add(nc.vector.tensor_tensor(prod[:, :, :], geq[:, :, :],
                                                            ddif[:, k, :].unsqueeze(1).to_broadcast([P, IJ, NT]), ALU.mult))
                            own.sync()
                            own.add(nc.vector.tensor_reduce(tab[:, 2 + k, :], prod[:, :, :], AX.X, ALU.add))
                            own.sync()
                            own.add(nc.vector.tensor_tensor(tab[:, 2 + k, :], tab[:, 2 + k, :], item_f[:, :], ALU.add))
                            own.sync()
                            own.add(nc.vector.tensor_scalar(tab[:, 2 + k, :], tab[:, 2 + k, :], float(NC // (RUN if k else 1) - 1), None, ALU.min))
                            own.sync()
                        nc.vector.tensor_copy(cidx[:, :], tab[:, 2, :]).then_inc(s_cidx, 1)
                        nc.vector.tensor_scalar(t128[:, :], tab[:, 0, :], float(P), None, ALU.mult).then_inc(s_tab, 1)
                        dve.wait_ge(s_tabT, 1)
                        nc.vector.tensor_copy(tabT[:, :], psum[0:4 * IJ, 2, 0:P]).then_inc(s_row, 1)
                        own.add(nc.vector.memset(base[:, NB:NB + 2], 0.0))
                        dve.wait_ge(s_x, 16)
                        n1 = own.n
                        with dve.Fori(0, NG) as g:
                            own = Chain(dve, s_own, g * (2 * G + 1) + n1)
                            own.sync()
                            for k in range(G):
                                own.add(nc.vector.bn_stats(stats[:, k, :], xr[:, ds(g * G + k, 1), :].squeeze(1)))
                            own.sync()
                            nc.vector.memset(nil[:, 0:1], 0.0)
                            for k in range(G):
                                own.add(nc.vector.bn_aggr(mv[:, k, :], stats[:, k, :]))
                            own.sync()
                            own.add(nc.vector.tensor_copy(mean_var[:, ds(g * G, G), :], mv[:, :, :]))
                            assert own.n == 2 * G + 1
                        own = Chain(dve, s_own, n1 + NG * (2 * G + 1))
                        own.sync()
                        nc.vector.memset(nil[:, 1:2], 0.0).then_inc(s_var, 1)
                        dve.wait_ge(s_sd, 1)
                        own.add(nc.vector.reciprocal(rstd[:, :], sd[:, :]))
                        own.sync()
                        nc.vector.scalar_tensor_tensor(nmr[:, :], mean_var[:, :, 0], -1.0, rstd[:, :], ALU.mult, ALU.mult).then_inc(s_ln, 1)
                        dve.wait_ge(s_pg, 3 * 16 * IJ)
                        own.add(nc.vector.tensor_copy(row_f[:, :, :, :], row_i[:, :, :, :]))
                        own.sync()
                        nc.vector.tensor_tensor(row_f[:, :, 1, :], row_f[:, :, 1, :], t128[:, :].unsqueeze(2).to_broadcast([P, IJ, P]),
                                                ALU.subtract).then_inc(s_pf, 1)
                        for j in range(IJ):
                            dve.wait_ge(s_pt, j + 1)
                            nc.vector.tensor_scalar(it_src[:, j * P:(j + 1) * P], psum[:, 3 + j % 2, 0:P], float(NP - 1), None,
                                                    ALU.min).then_inc(s_pe, 1)
                            nc.vector.tensor_copy(it_rel[:, j * P:(j + 1) * P], psum[:, 3 + j % 2, P:2 * P]).then_inc(s_pe, 1)
                            nc.vector.tensor_copy(it_w[:, j * P:(j + 1) * P], psum[:, 3 + j % 2, 2 * P:3 * P]).then_inc(s_pe, 1)

                    @block.tensor
                    def _(pe):
                        pe.wait_ge(s_const, 9)
                        pe.wait_ge(s_cum, 1)
                        nc.tensor.matmul(psum[:, 0, 0:2 * (NB + 1)], ones[:, :], cum[:, :, :].rearrange("p k b -> p (k b)"),
                                         start=True, stop=True)
                        nc.tensor.matmul(psum[:, 1, 0:NB], upper[:, :], cnt[:, :], start=True, stop=True).then_inc(s_off, 1)
                        pe.wait_ge(s_tab, 1)
                        nc.tensor.transpose(psum[0:4 * IJ, 2, 0:P], tab[:, :, :].rearrange("p k j -> p (k j)"), ident[:, :]).then_inc(s_tabT, 1)
                        pe.wait_ge(s_pf, 1)
                        for j in range(IJ):
                            if j >= 2:
                                pe.wait_ge(s_pe, 3 * (j - 1))
                            nc.tensor.transpose(psum[:, 3 + j % 2, 0:P], row_f[:, j, 0, :], ident[:, :])
                            nc.tensor.transpose(psum[:, 3 + j % 2, P:2 * P], row_f[:, j, 1, :], ident[:, :])
                            nc.tensor.transpose(psum[:, 3 + j % 2, 2 * P:3 * P], row_w[:, j, :], ident[:, :]).then_inc(s_pt, 1)

                with nc.Block() as block:

                    @block.sync
                    def _(sp):
                        sp.dma_start(item_d.rearrange("k (j p) -> (k j) p", p=P), tabT[:, :]).then_inc(s_rst, 16)
                        sp.wait_ge(s_rst, 16)
                        sp.dma_start(items[:, :], item_d).then_inc(s_rld, 16)
                        sp.wait_ge(s_rld, 16)

            s_hot = sem("l0_onehot_ready")
            s_mm = sem("l0_products")
            s_acc = sem("l0_added")
            s_gat = [sem(f"l0_gathered{u}") for u in range(RING)]
            s_idx = sem("l0_indices_ready")
            s_rank = sem("ranked")
            with ExitStack() as ph2:
                idx = sb("idx", [P, 2, RING], i32, ph2)
                rows = sb("rows", [P, RING, D], f32, ph2)
                hot = sb("hot", [P, RING, P], f32, ph2)
                mask = sb("mask", [P, NC], f32, ph2)
                rank = sb("rank", [P, NC], f32, ph2)
                pos = sb("pos", [P, NC], f32, ph2)
                with nc.Block() as block:

                    @block.scalar
                    def _(act):
                        for h in range(2):
                            nc.scalar.activation(idx[:, h, :], it_src[:, h * RING:(h + 1) * RING], ACT.Copy).then_inc(s_idx, 1)
                        with act.Fori(0, NI // STEP - 1) as it:
                            for h in range(2):
                                act.wait_ge(s_mm, RING + it * STEP + (h + 1) * RING)
                                nc.scalar.activation(idx[:, h, :], it_src[:, ds((it + 1) * STEP + h * RING, RING)],
                                                     ACT.Copy).then_inc(s_idx, 1)

                    @block.gpsimd
                    def _(pool):
                        with pool.Fori(0, NI // STEP) as it:
                            for u in range(STEP):
                                if u % RING == 0:
                                    pool.wait_ge(s_idx, it * 2 + u // RING + 1)
                                pool.wait_ge(s_mm, it * STEP + u + 1)
                                alone(pool, s_turn_p)
                                pool.indirect_dma_start(
                                    out=rows[:, u % RING, :], out_offset=None, in_=xn_d,
                                    in_offset=bass.IndirectOffsetOnAxis(ap=idx[:, u // RING, u % RING:u % RING + 1], axis=0),
                                ).then_inc(s_gat[u % RING], 16)

                    @block.tensor
                    def _(pe):
                        pe.sem_inc(s_mm, RING)
                        with pe.Fori(0, NI // STEP) as it:
                            for u in range(STEP):
                                pe.wait_ge(s_hot, it * STEP + u + 1)
                                pe.wait_ge(s_gat[u % RING], it * (16 * STEP // RING) + 16 * (u // RING + 1))
                                pe.wait_ge(s_acc, it * STEP + u + 1)
                                nc.tensor.matmul(psum[:, u % RING, 0:D], hot[:, u % RING, :], rows[:, u % RING, :],
                                                 start=True, stop=True).then_inc(s_mm, 1)

                    @block.vector
                    def _(dve):
                        dve.sem_inc(s_acc, RING)
                        nc.vector.memset(pos[:, :], 0.0).then_inc(s_rank, 1)
                        with dve.Fori(0, NI // STEP) as it:

                            def onehot(u):
                                dve.wait_ge(s_mm, it * STEP + u + 1)
                                nc.vector.tensor_scalar(hot[:, u % RING, :], iota_r[:, :], it_rel[:, ds(it * STEP + u, 1)],
                                                        it_w[:, ds(it * STEP + u, 1)], ALU.is_equal, ALU.mult).then_inc(s_hot, 1)

                            for u in range(RING):
                                onehot(u)
                            dve.wait_ge(s_rank, it * 3 + 1)
                            nc.vector.tensor_scalar(mask[:, :], kb[:, :], bnum[:, ds(it, 1)], None, ALU.is_equal).then_inc(s_rank, 1)
                            dve.wait_ge(s_rank, it * 3 + 2)
                            nc.vector.tensor_tensor_scan(rank[:, :], mask[:, :], mask[:, :], base[:, ds(it, 1)],
                                                         ALU.add, ALU.bypass).then_inc(s_rank, 1)
                            dve.wait_ge(s_rank, it * 3 + 3)
                            alone(dve, s_turn_v)
                            nc.vector.copy_predicated(pos[:, :], mask[:, :].bitcast(i32), rank[:, :]).then_inc(s_rank, 1)
                            for half in range(2):
                                tiles = nc.values_load_multi_w_load_instructions(
                                    items[0:1, ds(it * STEP + half * RING, RING)], [mybir.EngineType.DVE], min_val=0, max_val=NB - 1,
                                    skip_runtime_bounds_check_because="a tile's number is a count of at most NB - 1 buckets")[1]
                                for k in range(RING):
                                    u = half * RING + k
                                    dve.wait_ge(s_mm, RING + it * STEP + u + 1)
                                    dve.wait_ge(s_acc, RING + it * STEP + u)
                                    there = acc[:, ds(tiles[k], 1), :].squeeze(1)
                                    nc.vector.tensor_tensor(there, there, psum[:, u % RING, 0:D], ALU.add).then_inc(s_acc, 1)
                                    if half == 0:
                                        onehot(u + RING)
                        dve.wait_ge(s_rank, 3 * (NI // STEP) + 1)
                        nc.vector.tensor_copy(pos_i[:, :], pos[:, :]).then_inc(s_rank, 1)

        with ExitStack() as ph3:
            stage = sb("stage", [P, 2, SC, ER], f32, ph3)
            sidx = sb("sidx", [P, 2, SC], i32, ph3)
            src3 = sb("src3", [P, NC], i32, ph3)
            w_self = sb("w_self", [P, 2, D], f32, ph3)
            w_neigh = sb("w_neigh", [P, 2, D], f32, ph3)
            w1 = sb("w1", [P, 2, 6, P], f32, ph3)
            b1 = sb("b1", [P, 6], f32, ph3)
            w2s = sb("w2s", [P, 2, P], f32, ph3)
            w2e = sb("w2e", [P, 4, P // 2], f32, ph3)
            b2 = sb("b2", [P, 3], f32, ph3)
            w3 = sb("w3", [P, 3, D], f32, ph3)
            b3 = sb("b3", [5, D], f32, ph3)
            gw = sb("gw", [P, 2, 4], f32, ph3)
            gb = sb("gb", [1, 4], f32, ph3)
            pair = sb("pair", [4, 2, P], f32, ph3)
            rev = sb("rev", [P, 8], f32, ph3)
            rev_i = sb("rev_i", [P, 8], i32, ph3)
            xs = sb("xs", [P, G, 2 * D], f32, ph3)
            tT = sb("tT", [P, 2, 4, P], f32, ph3)
            sq = sb("sq", [P, D], f32, ph3)
            ss = sb("ss", [P, G], f32, ph3)
            nrm = sb("nrm", [P, G], f32, ph3)
            rn = sb("rn", [P, G], f32, ph3)
            ln = {n: sb("ln_" + n, s, f32, ph3) for n, s in
                  (("stats", [P, G, 6]), ("mv", [P, G, 2]), ("sd", [P, G]), ("rstd", [P, G]), ("nmr", [P, G]), ("nil", [P, 4]))}
            yT = sb("yT", [P, 2, G * P], f32, ph3)
            h1 = sb("h1", [P, 6, G * P], f32, ph3)
            h2 = sb("h2", [P, 3, G * P], f32, ph3)
            gt = {n: sb("gt_" + n, [P, G, 4], f32, ph3) for n in ("l", "e", "g", "eq", "sc", "o1", "g2", "eq2", "sc2", "o2")}
            g1 = {n: sb("g1_" + n, [P, G], f32, ph3) for n in ("m", "s", "r", "v1", "k1", "v2", "k2", "d", "x", "t", "w1", "w2")}
            cf = sb("cf", [P, G, 5], f32, ph3)
            cfT = sb("cfT", [5, G * P], f32, ph3)

            s_w3 = sem("l0_weights")
            s_att = [sem(f"attributes_loaded{h}") for h in range(2)]
            s_side = sem("scatter_sides_ready")
            s_own3 = sem("l0_vector_own")
            s_sca = [sem(f"scattered{h}") for h in range(2)]
            s_c3 = sem("l0_constants")
            s_a = sem("l0_normalised")
            s_t1 = sem("l0_transposed")
            s_t1c = sem("l0_columns")
            s_gnn = sem("l0_gnn_products")
            s_ss = sem("l0_squares")
            s_nrm = sem("l0_norms")
            s_v3 = sem("l0_variance")
            s_sd3 = sem("l0_deviation")
            s_ln3 = sem("l0_rstd")
            s_y = sem("l0_ffn_rows")
            s_t2 = sem("l0_ffn_transposed")
            s_yT = sem("l0_ffn_columns")
            s_h1 = sem("l0_hidden1_products")
            s_h1c = sem("l0_hidden1")
            s_h2 = sem("l0_hidden2_products")
            s_h2c = sem("l0_hidden2")
            s_lg = sem("l0_logits")
            s_mx = sem("l0_shifted")
            s_ex = sem("l0_exponentials")
            s_df = sem("l0_gate_gap")
            s_ex2 = sem("l0_gate_ratio")
            s_cf = sem("l0_coefficients")
            s_cT = sem("l0_coefficients_transposed")
            s_cTc = sem("l0_coefficient_columns")
            s_gbr = sem("l0_gates_spread")
            s_h2g = sem("l0_hidden2_gated")
            s_y3 = sem("l0_ffn_products")
            s_x2 = sem("l0_rows_done")

            with nc.Block() as block:

                @block.sync
                def _(sp):
                    for dst, src in (
                        (w_self[:, :, :], a["w_self"].rearrange("(c p) n -> p c n", p=P)),
                        (w_neigh[:, :, :], a["w_neigh"].rearrange("(c p) n -> p c n", p=P)),
                        (w1[:, :, 0:2, :], a["sW1"].rearrange("(c p) (m n) -> p c m n", p=P, n=P)),
                        (w2s[:, :, :], a["sW2"].rearrange("(c p) n -> p c n", p=P)),
                        (w2e[:, :, :], a["eW2"].rearrange("e p n -> p e n")),
                        (w3[:, 0, :], a["sW3"]),
                        (w3[:, 1:3, :], a["eW3"].rearrange("(q e) k n -> (e k) q n", q=2)),
                        (b3[0:4, :], a["eb3"]),
                        (b3[4:5, :], a["sb3"].unsqueeze(0)),
                        (gw[:, :, :], a["gW"].rearrange("(c p) n -> p c n", p=P)),
                        (gb[:, :], a["gb"].unsqueeze(0)),
                        (b1[:, 0:2], a["sb1"].rearrange("(m p) -> p m", p=P)),
                        (b1[:, 2:6], a["eb1"].rearrange("e p -> p e")),
                        (b2[:, 0:1], a["sb2"].unsqueeze(1)),
                        (b2[:, 1:3], a["eb2"].rearrange("(q e) k -> (e k) q", q=2)),
                        (src3[:, :], a["src"].rearrange("(p c) -> p c", p=P)),
                    ):
                        with nc.allow_non_contiguous_dma(reason="a few hundred biases"):
                            sp.dma_start(dst, src).then_inc(s_w3, 16)
                    for c in range(2):
                        sp.dma_start(w1[:, c, 2:6, :], a["eW1"][:, c * P:(c + 1) * P, :].rearrange("e p n -> p e n")).then_inc(s_w3, 16)
                    attr = a["attr"].rearrange("(p c) f -> p c f", p=P)
                    for h in range(2):
                        sp.dma_start(stage[:, h, :, 0:EA], attr[:, h * SC:(h + 1) * SC, :]).then_inc(s_att[h], 16)
                    with sp.Fori(0, NC // SC // 2 - 1) as it:
                        for h in range(2):
                            sp.wait_ge(s_sca[h], (it + 1) * (16 * SC))
                            sp.dma_start(stage[:, h, :, 0:EA], attr[:, ds((it + 1) * (2 * SC) + h * SC, SC), :]).then_inc(s_att[h], 16)

                @block.gpsimd
                def _(pool):
                    own = Chain(pool, s_c3)
                    own.add(pool.iota(rev_i[:, :], pattern=[[-1, 8]], base=8, channel_multiplier=0))
                    own.add(pool.memset(pair[:, :, :], 0.0))
                    own.add(pool.memset(stage[:, :, :, EA:EA + 1], 1.0))
                    own.add(pool.memset(cf[:, :, 4:5], 1.0))
                    own.sync()
                    for m in range(4):
                        own.add(pool.affine_select(out=pair[:, m // 2, m % 2 * (P // 2):(m % 2 + 1) * (P // 2)],
                                                   in_=pair[:, m // 2, m % 2 * (P // 2):(m % 2 + 1) * (P // 2)],
                                                   compare_op=ALU.not_equal, fill=1.0, base=-m,
                                                   pattern=[[0, P // 2]], channel_multiplier=1))
                    own.sync()
                    with pool.Fori(0, NC // SC // 2) as it:
                        for h in range(2):
                            pool.wait_ge(s_sca[h], it * (16 * SC))
                            alone(pool, s_turn_p)
                            at = ds(it * (2 * SC) + h * SC, SC)
                            pool.tensor_copy(sidx[:, h, :], pos_i[:, at]).then_inc(s_side, 1)
                            pool.wait_ge(s_att[h], it * 16 + 16)
                            alone(pool, s_turn_p)
                            pool.tensor_copy(stage[:, h, :, EA + 1], src3[:, at]).then_inc(s_side, 1)
                            pool.wait_ge(s_side, it * 4 + 2 * h + 2)
                            alone(pool, s_turn_p)
                            for c in range(SC):
                                pool.indirect_dma_start(
                                    out=edges_d, out_offset=bass.IndirectOffsetOnAxis(ap=sidx[:, h, c:c + 1], axis=0),
                                    in_=stage[:, h, c, :], in_offset=None).then_inc(s_sca[h], 16)
                    for h in range(2):
                        pool.wait_ge(s_sca[h], 16 * SC * (NC // SC // 2))

                @block.scalar
                def _(act):
                    act.wait_ge(s_w3, 16 * 18)
                    act.wait_ge(s_c3, 8)
                    with act.Fori(0, NG) as g:
                        act.wait_ge(s_t2, g * G)
                        alone(act, s_turn_a)
                        for k in range(G):
                            t = g * G + k
                            nc.scalar.activation(xs[:, k, 0:D], xr[:, ds(t, 1), :].squeeze(1), ACT.Identity,
                                                 bias=nmr[:, ds(t, 1)], scale=rstd[:, ds(t, 1)])
                            nc.scalar.activation(xs[:, k, D:2 * D], acc[:, ds(t, 1), :].squeeze(1), ACT.Copy).then_inc(s_a, 1)
                        for k in range(G):
                            act.wait_ge(s_gnn, g * G + min(k | 1, G - 1) + 1)
                            act.wait_ge(s_ss, g * G + k)
                            nc.scalar.activation(sq[:, :], psum[:, k // 2, k % 2 * D:(k % 2 + 1) * D], ACT.Square,
                                                 accum_out=ss[:, k:k + 1]).then_inc(s_ss, 1)
                        act.wait_ge(s_ss, g * G + G)
                        nc.scalar.activation(nrm[:, :], ss[:, :], ACT.Sqrt).then_inc(s_nrm, 1)
                        act.wait_ge(s_v3, g + 1)
                        nc.scalar.activation(ln["sd"][:, :], ln["mv"][:, :, 1], ACT.Sqrt, bias=eps[:, :]).then_inc(s_sd3, 1)
                        act.wait_ge(s_ln3, g + 1)
                        alone(act, s_turn_a)
                        for k in range(G):
                            nc.scalar.activation(xs[:, k, 0:D], xr[:, ds(g * G + k, 1), :].squeeze(1), ACT.Identity,
                                                 bias=ln["nmr"][:, k:k + 1], scale=ln["rstd"][:, k:k + 1]).then_inc(s_y, 1)
                        act.wait_ge(s_mx, g + 1)
                        nc.scalar.activation(gt["e"][:, :, :], gt["l"][:, :, :], ACT.Exp).then_inc(s_ex, 1)
                        for n in range(12):
                            m, (c0, c1) = n // 2, HALVES[n % 2]
                            act.wait_ge(s_h1, g * 12 + n + 1)
                            nc.scalar.activation(h1[:, m, c0:c1], psum[:, 4 + n % 4, 0:c1 - c0], ACT.Relu,
                                                 bias=b1[:, m:m + 1]).then_inc(s_h1c, 1)
                        act.wait_ge(s_df, g + 1)
                        nc.scalar.activation(g1["x"][:, :], g1["d"][:, :], ACT.Exp).then_inc(s_ex2, 1)
                        for n in range(6):
                            m, (c0, c1) = n // 2, HALVES[n % 2]
                            act.wait_ge(s_h2, g * 6 + n + 1)
                            nc.scalar.activation(h2[:, m, c0:c1], psum[:, 4 + n % 4, 0:c1 - c0], ACT.Relu,
                                                 bias=b2[:, m:m + 1]).then_inc(s_h2c, 1)

                @block.tensor
                def _(pe):
                    pe.wait_ge(s_w3, 16 * 18)
                    pe.wait_ge(s_c3, 8)
                    with pe.Fori(0, NG) as g:

                        def products(k):
                            pe.wait_ge(s_t1c, g * G + k + 1)
                            for c in range(4):
                                w = (w_self if c < 2 else w_neigh)[:, c % 2, :]
                                last = nc.tensor.matmul(psum[:, k // 2, k % 2 * D:(k % 2 + 1) * D], tT[:, k % 2, c, :], w,
                                                        start=c == 0, stop=c == 3)
                            last.then_inc(s_gnn, 1)

                        pe.wait_ge(s_x2, g * G)
                        for k in range(G):
                            pe.wait_ge(s_a, g * G + k + 1)
                            if k >= 2:
                                pe.wait_ge(s_t1c, g * G + k - 1)
                            for c in range(4):
                                last = nc.tensor.transpose(psum[:, 4 + k % 2, c * P:(c + 1) * P], xs[:, k, c * P:(c + 1) * P], ident[:, :])
                            last.then_inc(s_t1, 1)
                            if k:
                                products(k - 1)
                        products(G - 1)
                        for k in range(G):
                            pe.wait_ge(s_y, g * G + k + 1)
                            if k >= 2:
                                pe.wait_ge(s_yT, g * G + k - 1)
                            for c in range(2):
                                last = nc.tensor.transpose(psum[:, 4 + k % 2, c * P:(c + 1) * P], xs[:, k, c * P:(c + 1) * P], ident[:, :])
                            last.then_inc(s_t2, 1)
                        pe.wait_ge(s_yT, g * G + G)
                        for k in range(G):
                            for c in range(2):
                                nc.tensor.matmul(psum[:, 6, k * 4:k * 4 + 4], yT[:, c, k * P:(k + 1) * P], gw[:, c, :],
                                                 start=c == 0, stop=False)
                            last = nc.tensor.matmul(psum[:, 6, k * 4:k * 4 + 4], ones[0:1, :], gb[:, :], start=False, stop=True)
                        last.then_inc(s_lg, 1)
                        for n in range(12):
                            m, (c0, c1) = n // 2, HALVES[n % 2]
                            if n >= 4:
                                pe.wait_ge(s_h1c, g * 12 + n - 3)
                            if n == 2:
                                pe.wait_ge(s_mx, g + 1)
                            for c in range(2):
                                last = nc.tensor.matmul(psum[:, 4 + n % 4, 0:c1 - c0], w1[:, c, m, :], yT[:, c, c0:c1],
                                                        start=c == 0, stop=c == 1)
                            last.then_inc(s_h1, 1)
                        for n in range(6):
                            m, (c0, c1) = n // 2, HALVES[n % 2]
                            pe.wait_ge(s_h1c, g * 12 + 12)
                            if n >= 4:
                                pe.wait_ge(s_h2c, g * 6 + n - 3)
                            for c in range(2):
                                if m == 0:
                                    last = nc.tensor.matmul(psum[:, 4 + n % 4, 0:c1 - c0], w2s[:, c, :], h1[:, c, c0:c1],
                                                            start=c == 0, stop=c == 1)
                                else:
                                    e = 2 * (m - 1) + c
                                    last = nc.tensor.matmul(psum[c * (P // 2):(c + 1) * (P // 2), 4 + n % 4, 0:c1 - c0],
                                                            w2e[:, e, :], h1[:, 2 + e, c0:c1], start=True, stop=True)
                            last.then_inc(s_h2, 1)
                        pe.wait_ge(s_cf, g + 1)
                        for n, (c0, c1) in enumerate(HALVES):
                            for k in range(c0 // P, c1 // P):
                                last = nc.tensor.transpose(psum[0:5, n, k * P - c0:(k + 1) * P - c0], cf[:, k, :], ident[:, :])
                            last.then_inc(s_cT, 1)
                        pe.wait_ge(s_cTc, g * 2 + 2)
                        for n in range(4):
                            q, (c0, c1) = n // 2, HALVES[n % 2]
                            nc.tensor.matmul(psum[:, n, 0:c1 - c0], pair[:, q, :], cfT[0:4, c0:c1], start=True, stop=True).then_inc(s_gbr, 1)
                        for k in range(G):
                            if k == 0:
                                pe.wait_ge(s_h2c, g * 6 + 6)
                            pe.wait_ge(s_h2g, g * 4 + (3 if k < 4 else 4))
                            if k >= 4:
                                pe.wait_ge(s_x2, g * G + k - 3)
                            for m in range(3):
                                nc.tensor.matmul(psum[:, 4 + k % 4, 0:D], h2[:, m, k * P:(k + 1) * P], w3[:, m, :], start=m == 0, stop=False)
                            nc.tensor.matmul(psum[:, 4 + k % 4, 0:D], cfT[:, k * P:(k + 1) * P], b3[:, :], start=False, stop=True).then_inc(s_y3, 1)

                @block.vector
                def _(dve):
                    dve.wait_ge(s_c3, 8)
                    nc.vector.tensor_copy(rev[:, :], rev_i[:, :]).then_inc(s_own3, 1)
                    with dve.Fori(0, NG) as g:
                        own = Chain(dve, s_own3, 1 + g * DENSE0_OWN)
                        for k in range(G):
                            dve.wait_ge(s_t1, g * G + k + 1)
                            if k >= 2:
                                dve.wait_ge(s_gnn, g * G + k - 1)
                            nc.vector.tensor_copy(tT[:, k % 2, :, :].rearrange("p c n -> p (c n)"), psum[:, 4 + k % 2, :]).then_inc(s_t1c, 1)
                        dve.wait_ge(s_nrm, g + 1)
                        own.add(nc.vector.tensor_scalar(nrm[:, :], nrm[:, :], 1e-12, None, ALU.max))
                        own.sync()
                        own.add(nc.vector.reciprocal(rn[:, :], nrm[:, :]))
                        own.sync()
                        for k in range(G):
                            x = xr[:, ds(g * G + k, 1), :].squeeze(1)
                            own.add(nc.vector.scalar_tensor_tensor(x, psum[:, k // 2, k % 2 * D:(k % 2 + 1) * D], rn[:, k:k + 1], x,
                                                                   ALU.mult, ALU.add))
                        own.sync()
                        normalise(dve, own, xr, g, ln, s_v3, s_sd3, s_ln3)
                        for k in range(G):
                            dve.wait_ge(s_t2, g * G + k + 1)
                            nc.vector.tensor_copy(yT[:, :, k * P:(k + 1) * P],
                                                  psum[:, 4 + k % 2, 0:2 * P].rearrange("p (c n) -> p c n", c=2)).then_inc(s_yT, 1)
                        dve.wait_ge(s_lg, g + 1)
                        logits = psum[:, 6, 0:4 * G].rearrange("p (k e) -> p k e", e=4)
                        own.add(nc.vector.tensor_reduce(g1["m"][:, :], logits, AX.X, ALU.max))
                        own.sync()
                        nc.vector.tensor_tensor(gt["l"][:, :, :], logits, wide(g1["m"], 4), ALU.subtract).then_inc(s_mx, 1)
                        dve.wait_ge(s_ex, g + 1)
                        own.add(nc.vector.tensor_reduce(g1["s"][:, :], gt["e"][:, :, :], AX.X, ALU.add))
                        own.sync()
                        own.add(nc.vector.reciprocal(g1["r"][:, :], g1["s"][:, :]))
                        own.sync()
                        own.add(nc.vector.tensor_tensor(gt["g"][:, :, :], gt["e"][:, :, :], wide(g1["r"], 4), ALU.mult))
                        own.sync()
                        top_two(own, gt, g1, rev, 4)
                        nc.vector.tensor_tensor(g1["d"][:, :], g1["v2"][:, :], g1["v1"][:, :], ALU.subtract).then_inc(s_df, 1)
                        dve.wait_ge(s_ex2, g + 1)
                        two_weights(own, g1)
                        own.add(nc.vector.tensor_tensor(gt["g2"][:, :, :], gt["o1"][:, :, :], wide(g1["w1"], 4), ALU.mult))
                        own.add(nc.vector.tensor_tensor(gt["e"][:, :, :], gt["o2"][:, :, :], wide(g1["w2"], 4), ALU.mult))
                        own.sync()
                        nc.vector.tensor_tensor(cf[:, :, 0:4], gt["g2"][:, :, :], gt["e"][:, :, :], ALU.add).then_inc(s_cf, 1)
                        for n, (c0, c1) in enumerate(HALVES):
                            dve.wait_ge(s_cT, g * 2 + n + 1)
                            nc.vector.tensor_copy(cfT[:, c0:c1], psum[0:5, n, 0:c1 - c0]).then_inc(s_cTc, 1)
                        for n in (0, 2, 1, 3):
                            q, (c0, c1) = n // 2, HALVES[n % 2]
                            dve.wait_ge(s_gbr, g * 4 + n + 1)
                            dve.wait_ge(s_h2c, g * 6 + 2 * (q + 1) + n % 2 + 1)
                            nc.vector.tensor_tensor(h2[:, 1 + q, c0:c1], h2[:, 1 + q, c0:c1], psum[:, n, 0:c1 - c0], ALU.mult).then_inc(s_h2g, 1)
                        for k in range(G):
                            dve.wait_ge(s_y3, g * G + k + 1)
                            x = xr[:, ds(g * G + k, 1), :].squeeze(1)
                            nc.vector.tensor_tensor(x, psum[:, 4 + k % 4, 0:D], x, ALU.add).then_inc(s_x2, 1)
                        assert own.n == DENSE0_OWN, own.n

        early.close()
        out1 = sb("out1", [P, NT, NX])
        out2 = sb("out2", [P, NT, NX])
        wt1 = sb("wt1", [P, NT])
        wt2 = sb("wt2", [P, NT])
        rstd4 = sb("rstd4", [P, NT])
        nmr4 = sb("nmr4", [P, NT])

        with ExitStack() as ph4:
            agg = sb("agg", [P, NB, EA + 1], f32, ph4)
            rcount = sb("rcount", [P, NB], f32, ph4)
            s_own4 = sem("l1_vector_own")
            s_one = sem("l1_onehot_ready")
            s_prd = sem("l1_products")
            s_add = sem("l1_added")
            s_row4 = [sem(f"l1_rows_loaded{u}") for u in range(STEP4)]
            s_it4 = sem("l1_tiles_loaded")
            with ExitStack() as ph5:
                items4 = sb("items4", [4, IJ * P], i32, ph5)
                tile_bi = sb("tile_bi", [P, IJ * P], i32, ph5)
                tile_b = sb("tile_b", [P, IJ * P], f32, ph5)
                rows4 = sb("rows4", [P, STEP4, RUN, ER], f32, ph5)
                hot4 = sb("hot4", [P, STEP4, RUN, P], f32, ph5)
                rel4 = sb("rel4", [P, STEP4, RUN], f32, ph5)
                with nc.Block() as block:

                    @block.sync
                    def _(sp):
                        sp.dma_start(tile_bi[:, :], item_d[1:2, :].partition_broadcast(P).squeeze(1)).then_inc(s_it4, 16)
                        sp.dma_start(items4[:, :], item_d).then_inc(s_it4, 16)
                        sp.wait_ge(s_it4, 32)
                        with sp.Fori(0, NI4 // STEP4) as it:
                            runs = nc.values_load_multi_w_load_instructions(
                                items4[3:4, ds(it * STEP4, STEP4)], [mybir.EngineType.SP], min_val=0, max_val=NC // RUN - 1,
                                skip_runtime_bounds_check_because="a run's number is clamped to the last")[1]
                            for u in range(STEP4):
                                sp.wait_ge(s_prd, it * STEP4 + u + 1)
                                sp.dma_start(rows4[:, u, :, :], edges_d[ds(runs[u] * (P * RUN), P * RUN), :].rearrange(
                                    "(p c) f -> p c f", c=RUN)).then_inc(s_row4[u], 16)

                    @block.tensor
                    def _(pe):
                        pe.sem_inc(s_prd, STEP4)
                        with pe.Fori(0, NI4 // STEP4) as it:
                            for u in range(STEP4):
                                pe.wait_ge(s_one, it * STEP4 + u + 1)
                                pe.wait_ge(s_add, it * STEP4 + u + 1)
                                for c in range(RUN):
                                    last = nc.tensor.matmul(psum[:, u, 0:EA + 1], hot4[:, u, c, :], rows4[:, u, c, 0:EA + 1],
                                                            start=c == 0, stop=c == RUN - 1)
                                last.then_inc(s_prd, 1)

                    @block.vector
                    def _(dve):
                        dve.sem_inc(s_add, STEP4)
                        own = Chain(dve, s_own4)
                        own.add(nc.vector.memset(agg[:, :, :], 0.0))
                        dve.wait_ge(s_it4, 32)
                        own.add(nc.vector.tensor_scalar(tile_b[:, :], tile_bi[:, :], float(P), None, ALU.mult))
                        own.sync()
                        half4 = STEP4 // 2
                        with dve.Fori(0, NI4 // STEP4) as it:
                            for half in range(2):
                                at = slice(half * half4, (half + 1) * half4)
                                for u in range(half * half4, (half + 1) * half4):
                                    dve.wait_ge(s_row4[u], it * 16 + 16)
                                dve.wait_ge(s_prd, it * STEP4 + (half + 1) * half4)
                                alone(dve, s_turn_v)
                                first = tile_b[:, ds(it * STEP4 + half * half4, half4)].unsqueeze(2).to_broadcast([P, half4, RUN])
                                nc.vector.tensor_tensor(rel4[:, at, :], rows4[:, at, :, EA + 1], first, ALU.subtract).then_inc(s_own4, 1)
                                dve.wait_ge(s_own4, own.n + it * 2 + half + 1)
                                for u in range(half * half4, (half + 1) * half4):
                                    for c in range(RUN):
                                        last = nc.vector.tensor_scalar(hot4[:, u, c, :], iota_r[:, :], rel4[:, u, c:c + 1], None, ALU.is_equal)
                                    last.then_inc(s_one, 1)
                            tiles = nc.values_load_multi_w_load_instructions(
                                items4[1:2, ds(it * STEP4, STEP4)], [mybir.EngineType.DVE], min_val=0, max_val=NB - 1,
                                skip_runtime_bounds_check_because="a tile's number is a count of at most NB - 1 buckets")[1]
                            for u in range(STEP4):
                                dve.wait_ge(s_prd, STEP4 + it * STEP4 + u + 1)
                                dve.wait_ge(s_add, STEP4 + it * STEP4 + u)
                                there = agg[:, ds(tiles[u], 1), :].squeeze(1)
                                nc.vector.tensor_tensor(there, there, psum[:, u, 0:EA + 1], ALU.add).then_inc(s_add, 1)
                        dve.wait_ge(s_add, STEP4 + NI4)
                        nc.vector.tensor_scalar(rcount[:, :], agg[:, :, EA], 1.0, None, ALU.max).then_inc(s_own4, 1)
                        dve.wait_ge(s_own4, own.n + 2 * (NI4 // STEP4) + 1)
                        nc.vector.reciprocal(rcount[:, :], rcount[:, :]).then_inc(s_own4, 1)

            with ExitStack() as ph6:
                gw1 = sb("gw1", [P, 2, 4, P], f32, ph6)
                gw1e = sb("gw1e", [EA, 4, P], f32, ph6)
                gw1u = sb("gw1u", [P, 4, P], f32, ph6)
                u0 = sb("u0", [P, 1], f32, ph6)
                gb1 = sb("gb1", [P, 4], f32, ph6)
                hbias = sb("hbias", [P, 4], f32, ph6)
                gw2 = sb("gw2", [P, 4, D], f32, ph6)
                gb2 = sb("gb2", [1, D], f32, ph6)
                fg = sb("fg", [P, 2, NX], f32, ph6)
                fbg = sb("fbg", [1, NX], f32, ph6)
                rev5 = sb("rev5", [P, NX], f32, ph6)
                rev5_i = sb("rev5_i", [P, NX], i32, ph6)
                xs5 = sb("xs5", [P, G, D + EA], f32, ph6)
                xT5 = sb("xT5", [P, 2, G * P], f32, ph6)
                aT5 = sb("aT5", [EA, G * P], f32, ph6)
                h5 = sb("h5", [P, 4, G * P], f32, ph6)
                yT5 = sb("yT5", [P, 2, G * P], f32, ph6)
                ln5, ln6 = ({n: sb(f"ln{m}_" + n, s, f32, ph6) for n, s in
                             (("stats", [P, G, 6]), ("mv", [P, G, 2]), ("sd", [P, G]), ("rstd", [P, G]), ("nmr", [P, G]), ("nil", [P, 4]))}
                            for m in (5, 6))
                gt5 = {n: sb("gt5_" + n, [P, G, NX], f32, ph6) for n in ("g", "eq", "sc", "o1", "g2", "eq2", "sc2", "o2")}
                g5 = {n: sb("g5_" + n, [P, G], f32, ph6) for n in ("v1", "k1", "v2", "k2", "d", "x", "t", "w1", "w2")}
                s_w5 = sem("l1_weights")
                s_c5 = sem("l1_constants")
                s_own5 = sem("l1_dense_vector_own")
                s_u5 = sem("l1_global_product")
                s_v5 = sem("l1_variance")
                s_sd5 = sem("l1_deviation")
                s_ln5 = sem("l1_rstd")
                s_a5 = sem("l1_normalised")
                s_t5 = sem("l1_transposed")
                s_tc5 = sem("l1_columns")
                s_h5 = sem("l1_hidden_products")
                s_hc5 = sem("l1_hidden")
                s_o5 = sem("l1_node_products")
                s_x3 = sem("l1_rows_done")
                s_v6 = sem("moe_variance")
                s_sd6 = sem("moe_deviation")
                s_ln6 = sem("moe_rstd")
                s_y6 = sem("moe_normalised")
                s_t6 = sem("moe_transposed")
                s_tc6 = sem("moe_columns")
                s_lg6 = sem("moe_logits")
                s_gl6 = sem("moe_logits_copied")
                s_df6 = sem("moe_gate_gap")
                s_ex6 = sem("moe_gate_ratio")
                with nc.Block() as block:

                    @block.sync
                    def _(sp):
                        with nc.allow_non_contiguous_dma(reason="a few hundred biases"):
                            for dst, src in (
                                (gw1[:, :, :, :], a["g_W1"][0:D, :].rearrange("(c p) (m n) -> p c m n", p=P, n=P)),
                                (gw1e[:, :, :], a["g_W1"][D:D + EA, :].rearrange("p (m n) -> p m n", n=P)),
                                (gw1u[:, :, :], a["g_W1"][D + EA:D + EA + P, :].rearrange("p (m n) -> p m n", n=P)),
                                (u0[:, :], a["g_u"][0, :].unsqueeze(1)),
                                (gb1[:, :], a["g_b1"].rearrange("(m p) -> p m", p=P)),
                                (gw2[:, :, :], a["g_W2"].rearrange("(m p) n -> p m n", p=P)),
                                (gb2[:, :], a["g_b2"].unsqueeze(0)),
                                (fg[:, :, :], a["f_Wg"].rearrange("(c p) e -> p c e", p=P)),
                                (fbg[:, :], a["f_bg"].unsqueeze(0)),
                            ):
                                sp.dma_start(dst, src).then_inc(s_w5, 16)
                        sp.wait_ge(s_w5, 16 * 9)

                    @block.gpsimd
                    def _(pool):
                        pool.iota(rev5_i[:, :], pattern=[[-1, NX]], base=NX, channel_multiplier=0).then_inc(s_c5, 1)

                    @block.scalar
                    def _(act):
                        act.wait_ge(s_w5, 16 * 9)
                        with act.Fori(0, NG) as g:
                            act.wait_ge(s_v5, g + 1)
                            nc.scalar.activation(ln5["sd"][:, :], ln5["mv"][:, :, 1], ACT.Sqrt, bias=eps[:, :]).then_inc(s_sd5, 1)
                            act.wait_ge(s_ln5, g + 1)
                            alone(act, s_turn_a)
                            for k in range(G):
                                t = g * G + k
                                nc.scalar.activation(xs5[:, k, 0:D], xr[:, ds(t, 1), :].squeeze(1), ACT.Identity,
                                                     bias=ln5["nmr"][:, k:k + 1], scale=ln5["rstd"][:, k:k + 1])
                                nc.scalar.activation(xs5[:, k, D:D + EA], agg[:, ds(t, 1), 0:EA].squeeze(1), ACT.Copy,
                                                     scale=rcount[:, ds(t, 1)]).then_inc(s_a5, 1)
                            for n in range(8):
                                m, (c0, c1) = n // 2, HALVES[n % 2]
                                act.wait_ge(s_h5, g * 8 + n + 1)
                                nc.scalar.activation(h5[:, m, c0:c1], psum[:, 4 + n % 4, 0:c1 - c0], ACT.Relu,
                                                     bias=hbias[:, m:m + 1]).then_inc(s_hc5, 1)
                            act.wait_ge(s_v6, g + 1)
                            nc.scalar.activation(ln6["sd"][:, :], ln6["mv"][:, :, 1], ACT.Sqrt, bias=eps[:, :]).then_inc(s_sd6, 1)
                            act.wait_ge(s_ln6, g + 1)
                            alone(act, s_turn_a)
                            for k in range(G):
                                nc.scalar.activation(xs5[:, k, 0:D], xr[:, ds(g * G + k, 1), :].squeeze(1), ACT.Identity,
                                                     bias=ln6["nmr"][:, k:k + 1], scale=ln6["rstd"][:, k:k + 1]).then_inc(s_y6, 1)
                            act.wait_ge(s_df6, g + 1)
                            nc.scalar.activation(g5["x"][:, :], g5["d"][:, :], ACT.Exp).then_inc(s_ex6, 1)

                    @block.tensor
                    def _(pe):
                        pe.wait_ge(s_w5, 16 * 9)
                        for m in range(4):
                            last = nc.tensor.matmul(psum[:, 0, m:m + 1], gw1u[:, m, :], u0[:, :], start=True, stop=True)
                        last.then_inc(s_u5, 1)
                        with pe.Fori(0, NG) as g:
                            for k in range(G):
                                pe.wait_ge(s_a5, g * G + k + 1)
                                if k >= 2:
                                    pe.wait_ge(s_tc5, g * G + k - 1)
                                elif k == 0:
                                    pe.wait_ge(s_gl6, g + 1)
                                for c in range(2):
                                    nc.tensor.transpose(psum[:, k % 2, c * P:(c + 1) * P], xs5[:, k, c * P:(c + 1) * P], ident[:, :])
                                nc.tensor.transpose(psum[0:EA, k % 2, 2 * P:3 * P], xs5[:, k, D:D + EA], ident[:, :]).then_inc(s_t5, 1)
                            pe.wait_ge(s_tc5, g * G + G)
                            pe.wait_ge(s_x3, g * G)
                            for n in range(8):
                                m, (c0, c1) = n // 2, HALVES[n % 2]
                                if n >= 4:
                                    pe.wait_ge(s_hc5, g * 8 + n - 3)
                                for c in range(2):
                                    nc.tensor.matmul(psum[:, 4 + n % 4, 0:c1 - c0], gw1[:, c, m, :], xT5[:, c, c0:c1], start=c == 0, stop=False)
                                nc.tensor.matmul(psum[:, 4 + n % 4, 0:c1 - c0], gw1e[:, m, :], aT5[:, c0:c1], start=False, stop=True).then_inc(s_h5, 1)
                            pe.wait_ge(s_hc5, g * 8 + 8)
                            for k in range(G):
                                if k >= 4:
                                    pe.wait_ge(s_x3, g * G + k - 3)
                                for m in range(4):
                                    nc.tensor.matmul(psum[:, 4 + k % 4, 0:D], h5[:, m, k * P:(k + 1) * P], gw2[:, m, :], start=m == 0, stop=False)
                                nc.tensor.matmul(psum[:, 4 + k % 4, 0:D], ones[0:1, :], gb2[:, :], start=False, stop=True).then_inc(s_o5, 1)
                            for k in range(G):
                                pe.wait_ge(s_y6, g * G + k + 1)
                                if k >= 2:
                                    pe.wait_ge(s_tc6, g * G + k - 1)
                                for c in range(2):
                                    last = nc.tensor.transpose(psum[:, k % 2, c * P:(c + 1) * P], xs5[:, k, c * P:(c + 1) * P], ident[:, :])
                                last.then_inc(s_t6, 1)
                            pe.wait_ge(s_tc6, g * G + G)
                            for k in range(G):
                                for c in range(2):
                                    nc.tensor.matmul(psum[:, 2, k * NX:(k + 1) * NX], yT5[:, c, k * P:(k + 1) * P], fg[:, c, :], start=c == 0, stop=False)
                                last = nc.tensor.matmul(psum[:, 2, k * NX:(k + 1) * NX], ones[0:1, :], fbg[:, :], start=False, stop=True)
                            last.then_inc(s_lg6, 1)

                    @block.vector
                    def _(dve):
                        own = Chain(dve, s_own5)
                        dve.wait_ge(s_c5, 1)
                        own.add(nc.vector.tensor_copy(rev5[:, :], rev5_i[:, :]))
                        dve.wait_ge(s_u5, 1)
                        nc.vector.tensor_tensor(hbias[:, :], psum[:, 0, 0:4], gb1[:, :], ALU.add).then_inc(s_gl6, 1)
                        with dve.Fori(0, NG) as g:
                            own = Chain(dve, s_own5, 1 + g * DENSE1_OWN)
                            normalise(dve, own, xr, g, ln5, s_v5, s_sd5, s_ln5)
                            for k in range(G):
                                dve.wait_ge(s_t5, g * G + k + 1)
                                at = slice(k * P, (k + 1) * P)
                                nc.vector.tensor_copy(xT5[:, :, at], psum[:, k % 2, 0:2 * P].rearrange("p (c n) -> p c n", c=2))
                                nc.vector.tensor_copy(aT5[:, at], psum[0:EA, k % 2, 2 * P:3 * P]).then_inc(s_tc5, 1)
                            for k in range(G):
                                dve.wait_ge(s_o5, g * G + k + 1)
                                x = xr[:, ds(g * G + k, 1), :].squeeze(1)
                                nc.vector.tensor_tensor(x, psum[:, 4 + k % 4, 0:D], x, ALU.add).then_inc(s_x3, 1)
                            dve.wait_ge(s_x3, g * G + G)
                            normalise(dve, own, xr, g, ln6, s_v6, s_sd6, s_ln6)
                            dve.wait_ge(s_ln6, g + 1)
                            own.add(nc.vector.tensor_copy(rstd4[:, ds(g * G, G)], ln6["rstd"][:, :]))
                            own.add(nc.vector.tensor_copy(nmr4[:, ds(g * G, G)], ln6["nmr"][:, :]))
                            for k in range(G):
                                dve.wait_ge(s_t6, g * G + k + 1)
                                nc.vector.tensor_copy(yT5[:, :, k * P:(k + 1) * P],
                                                      psum[:, k % 2, 0:2 * P].rearrange("p (c n) -> p c n", c=2)).then_inc(s_tc6, 1)
                            dve.wait_ge(s_lg6, g + 1)
                            nc.vector.tensor_copy(gt5["g"][:, :, :], psum[:, 2, 0:NX * G].rearrange("p (k e) -> p k e", e=NX)).then_inc(s_gl6, 1)
                            dve.wait_ge(s_gl6, g + 2)
                            top_two(own, gt5, g5, rev5, NX)
                            nc.vector.tensor_tensor(g5["d"][:, :], g5["v2"][:, :], g5["v1"][:, :], ALU.subtract).then_inc(s_df6, 1)
                            dve.wait_ge(s_ex6, g + 1)
                            two_weights(own, g5)
                            for to, of in ((wt1, "w1"), (wt2, "w2")):
                                own.add(nc.vector.tensor_copy(to[:, ds(g * G, G)], g5[of][:, :]))
                            for to, of in ((out1, "o1"), (out2, "o2")):
                                own.add(nc.vector.tensor_copy(to[:, ds(g * G, G), :], gt5[of][:, :, :]))
                            own.sync()
                            assert own.n == DENSE1_OWN, own.n

        with ExitStack() as ph7:
            place_i = sb("place_i", [P, 2, NT], i32, ph7)
            etab = sb("etab", [1, NBLK + 2], i32, ph7)
            weights = ph7.enter_context(ExitStack())
            fw1 = sb("fw1", [P, NX, 2, HX], f32, weights)
            fw2 = sb("fw2", [P, NX, HX // P, D], f32, weights)
            fb1 = sb("fb1", [P, NX, HX // P], f32, weights)
            fb2 = sb("fb2", [P, NX, D], f32, weights)
            s_w7 = sem("moe_weights")
            s_own7 = sem("moe_vector_own")
            s_n7 = sem("moe_counts")
            s_o7 = sem("moe_offsets")
            s_pl7 = sem("moe_places")
            s_st7 = sem("moe_staged")
            s_id7 = sem("moe_place_copied")
            s_dp = [sem(f"moe_dispatched{k}") for k in range(G)]
            with ExitStack() as ph8:
                st8 = sb("st8", [P, G, D], f32, ph8)
                id8 = sb("id8", [P, 2, G], i32, ph8)
                both = sb("both", [P, NT, NX], f32, ph8)
                pos8 = sb("pos8", [P, NT, NX], f32, ph8)
                pl8 = sb("pl8", [P, 2, NT], f32, ph8)
                cnt8 = sb("cnt8", [P, NX], f32, ph8)
                nb8_i = sb("nb8_i", [P, NX], i32, ph8)
                nb8s = sb("nb8s", [P, NX], i32, ph8)
                nb8 = sb("nb8", [P, NX], f32, ph8)
                end8 = sb("end8", [P, NX], f32, ph8)
                bas8 = sb("bas8", [P, NX], f32, ph8)
                blk_f = sb("blk_f", [1, NBLK + 2], f32, ph8)
                ge8 = sb("ge8", [1, NBLK + 2, NX - 1], f32, ph8)
                with nc.Block() as block:

                    @block.sync
                    def _(sp):
                        for e in range(NX):
                            sp.dma_start(fw1[:, e, :, :], a["f_W1"][e].rearrange("(c p) n -> p c n", p=P)).then_inc(s_w7, 16)
                        for e in range(NX):
                            sp.dma_start(fw2[:, e, :, :], a["f_W2"][e].rearrange("(m p) n -> p m n", p=P)).then_inc(s_w7, 16)
                        with nc.allow_non_contiguous_dma(reason="the experts' biases by hidden unit"):
                            sp.dma_start(fb1[:, :, :], a["f_b1"].rearrange("e (m p) -> p e m", p=P)).then_inc(s_w7, 16)
                        sp.dma_start(fb2[:, :, :], a["f_b2"].partition_broadcast(P)).then_inc(s_w7, 16)
                        sp.wait_ge(s_w7, 16 * (2 * NX + 2))

                    @block.vector
                    def _(dve):
                        own = Chain(dve, s_own7)
                        own.add(nc.vector.tensor_tensor(both[:, :, :], out1[:, :, :], out2[:, :, :], ALU.add))
                        dve.wait_ge(s_pl7, 1)
                        own.add(nc.vector.tensor_copy(blk_f[:, :], etab[:, :]))
                        own.sync()
                        nc.vector.tensor_reduce(cnt8[:, :], both[:, :, :].rearrange("p t e -> p e t"), AX.X, ALU.add).then_inc(s_n7, 1)
                        dve.wait_ge(s_o7, 1)
                        own.add(nc.vector.tensor_scalar(nb8_i[:, :], psum[:, 0, 0:NX], float(P - 1), None, ALU.add))
                        own.sync()
                        own.add(nc.vector.tensor_scalar(nb8s[:, :], nb8_i[:, :], 7, None, ALU.arith_shift_right))
                        own.sync()
                        own.add(nc.vector.tensor_copy(nb8[:, :], nb8s[:, :]))
                        own.sync()
                        own.add(nc.vector.tensor_tensor_scan(end8[:, :], nb8[:, :], nb8[:, :], 0.0, ALU.add, ALU.bypass))
                        own.sync()
                        own.add(nc.vector.tensor_tensor(bas8[:, :], end8[:, :], nb8[:, :], ALU.subtract))
                        own.sync()
                        own.add(nc.vector.tensor_scalar(bas8[:, :], bas8[:, :], float(P), -1.0, ALU.mult, ALU.add))
                        own.sync()
                        own.add(nc.vector.tensor_tensor(bas8[:, :], bas8[:, :], psum[:, 0, NX:2 * NX], ALU.add))
                        own.sync()
                        for e in range(NX):
                            own.add(nc.vector.tensor_tensor_scan(pos8[:, :, e], both[:, :, e], both[:, :, e], bas8[:, e:e + 1], ALU.add, ALU.bypass))
                        own.sync()
                        for n, o in enumerate((out1, out2)):
                            own.add(nc.vector.tensor_tensor(both[:, :, :], o[:, :, :], pos8[:, :, :], ALU.mult))
                            own.sync()
                            own.add(nc.vector.tensor_reduce(pl8[:, n, :], both[:, :, :], AX.X, ALU.add))
                            own.sync()
                        nc.vector.tensor_copy(place_i[:, :, :], pl8[:, :, :]).then_inc(s_pl7, 1)
                        own.add(nc.vector.tensor_tensor(ge8[:, :, :], end8[0:1, 0:NX - 1].unsqueeze(1).to_broadcast([1, NBLK + 2, NX - 1]),
                                                        blk_f[:, :].unsqueeze(2).to_broadcast([1, NBLK + 2, NX - 1]), ALU.is_le))
                        own.sync()
                        own.add(nc.vector.tensor_reduce(blk_f[:, :], ge8[:, :, :], AX.X, ALU.add))
                        own.sync()
                        own.add(nc.vector.tensor_copy(etab[:, :], blk_f[:, :]))
                        own.sync()

                    @block.tensor
                    def _(pe):
                        pe.wait_ge(s_n7, 1)
                        nc.tensor.matmul(psum[:, 0, 0:NX], ones[:, :], cnt8[:, :], start=True, stop=True)
                        nc.tensor.matmul(psum[:, 0, NX:2 * NX], upper[:, :], cnt8[:, :], start=True, stop=True).then_inc(s_o7, 1)

                    @block.scalar
                    def _(act):
                        with act.Fori(0, NG) as g:
                            for k in range(G):
                                act.wait_ge(s_dp[k], g * 32)
                                alone(act, s_turn_a)
                                t = g * G + k
                                nc.scalar.activation(st8[:, k, :], xr[:, ds(t, 1), :].squeeze(1), ACT.Identity,
                                                     bias=nmr4[:, ds(t, 1)], scale=rstd4[:, ds(t, 1)]).then_inc(s_st7, 1)

                    @block.gpsimd
                    def _(pool):
                        pool.iota(etab[:, :], pattern=[[1, NBLK + 2]], base=0, channel_multiplier=0).then_inc(s_pl7, 1)
                        pool.wait_ge(s_pl7, 2)
                        with pool.Fori(0, NG) as g:
                            for k in range(G):
                                pool.wait_ge(s_dp[k], g * 32)
                            alone(pool, s_turn_p)
                            pool.tensor_copy(id8[:, :, :], place_i[:, :, ds(g * G, G)]).then_inc(s_id7, 1)
                            pool.wait_ge(s_id7, g + 1)
                            for k in range(G):
                                pool.wait_ge(s_st7, g * G + k + 1)
                                alone(pool, s_turn_p)
                                for n in range(2):
                                    pool.indirect_dma_start(
                                        out=xd_d, out_offset=bass.IndirectOffsetOnAxis(ap=id8[:, n, k:k + 1], axis=0),
                                        in_=st8[:, k, :], in_offset=None).then_inc(s_dp[k], 16)
                        for k in range(G):
                            pool.wait_ge(s_dp[k], NG * 32)

            with ExitStack() as ph9:
                xb = sb("xb", [P, 2, D], f32, ph9)
                xbT = sb("xbT", [P, 2, 2, P], f32, ph9)
                hs = sb("hs", [P, HX], f32, ph9)
                hT = sb("hT", [P, HX // P, P], f32, ph9)
                yb = sb("yb", [P, 2, D], f32, ph9)
                s_in = [sem(f"block_loaded{u}") for u in range(2)]
                s_xt = sem("block_transposed")
                s_xc = sem("block_columns")
                s_m1 = sem("block_hidden_products")
                s_hsa = sem("block_hidden_half_a")
                s_hsd = sem("block_hidden_half_d")
                s_ht = sem("block_hidden_transposed")
                s_hta = sem("block_relu_a")
                s_htd = sem("block_relu_d")
                s_m2 = sem("block_products")
                s_yb = sem("block_rows")
                s_yo = [sem(f"block_stored{u}") for u in range(2)]
                M = HX // P
                with nc.Block() as block:

                    @block.sync
                    def _(sp):
                        for u in range(2):
                            sp.dma_start(xb[:, u, :], xd_d[u * P:(u + 1) * P, :]).then_inc(s_in[u], 16)
                        with sp.Fori(0, NBLK // 2) as it:
                            for u in range(2):
                                sp.wait_ge(s_xt, it * 2 + u + 1)
                                sp.dma_start(xb[:, u, :], xd_d[ds(it * (2 * P) + (u + 2) * P, P), :]).then_inc(s_in[u], 16)

                    @block.tensor
                    def _(pe):
                        def transpose_x(j, u, n):
                            pe.wait_ge(s_in[u], n)
                            pe.wait_ge(s_xc, j)
                            for c in range(2):
                                last = nc.tensor.transpose(psum[:, 0, c * P:(c + 1) * P], xb[:, u, c * P:(c + 1) * P], ident[:, :])
                            last.then_inc(s_xt, 1)

                        def hidden(j, u, e):
                            pe.wait_ge(s_xc, j + 1)
                            for half in range(2):
                                for c in range(2):
                                    last = nc.tensor.matmul(psum[:, 1 + half, :], xbT[:, u, c, :],
                                                            fw1[:, ds(e, 1), c, half * 512:(half + 1) * 512].squeeze(1), start=c == 0, stop=c == 1)
                                last.then_inc(s_m1, 1)

                        def expert(j):
                            return pe.value_load(etab[0:1, ds(j, 1)], min_val=0, max_val=NX - 1)

                        transpose_x(0, 0, 16)
                        transpose_x(1, 1, 16)
                        e0 = expert(0)
                        hidden(0, 0, e0)
                        with pe.Fori(0, NBLK // 2) as it:
                            for u in range(2):
                                j = it * 2 + u
                                pe.wait_ge(s_hsa, j + 1)
                                pe.wait_ge(s_hsd, j + 1)
                                for m in range(M):
                                    last = nc.tensor.transpose(psum[:, 3 + m // 4, m % 4 * P:(m % 4 + 1) * P], hs[:, m * P:(m + 1) * P], ident[:, :])
                                    if m % 4 == 3:
                                        last.then_inc(s_ht, 1)
                                transpose_x(j + 2, u, it * 16 + 32)
                                nxt = expert(j + 1)
                                hidden(j + 1, 1 - u, nxt)
                                now = expert(j)
                                pe.wait_ge(s_hta, j * 4 + 4)
                                pe.wait_ge(s_htd, j * 4 + 4)
                                pe.wait_ge(s_yb, j)
                                for m in range(M):
                                    last = nc.tensor.matmul(psum[:, 5, 0:D], hT[:, m, :], fw2[:, ds(now, 1), m, :].squeeze(1), start=m == 0, stop=m == M - 1)
                                last.then_inc(s_m2, 1)

                    @block.scalar
                    def _(act):
                        def copy_hidden(j):
                            act.wait_ge(s_m1, 2 * j + 1)
                            nc.scalar.activation(hs[:, 0:512], psum[:, 1, :], ACT.Copy).then_inc(s_hsa, 1)

                        copy_hidden(0)
                        with act.Fori(0, NBLK // 2) as it:
                            for u in range(2):
                                j = it * 2 + u
                                e = act.value_load(etab[0:1, ds(j, 1)], min_val=0, max_val=NX - 1)
                                act.wait_ge(s_ht, 2 * j + 1)
                                act.wait_ge(s_m2, j)
                                alone(act, s_turn_a)
                                for m in range(4):
                                    nc.scalar.activation(hT[:, m, :], psum[:, 3, m * P:(m + 1) * P], ACT.Relu,
                                                         bias=fb1[:, ds(e, 1), m]).then_inc(s_hta, 1)
                                act.wait_ge(s_ht, 2 * j + 2)
                                copy_hidden(j + 1)
                                act.wait_ge(s_yb, j + 1)
                                act.dma_start(yd_d[ds(it * (2 * P) + u * P, P), :], yb[:, u, :]).then_inc(s_yo[u], 16)
                        for u in range(2):
                            act.wait_ge(s_yo[u], 16 * (NBLK // 2))

                    @block.vector
                    def _(dve):
                        def columns(j, u):
                            dve.wait_ge(s_xt, j + 1)
                            nc.vector.tensor_copy(xbT[:, u, :, :].rearrange("p c n -> p (c n)"), psum[:, 0, 0:2 * P]).then_inc(s_xc, 1)

                        def copy_hidden(j):
                            dve.wait_ge(s_m1, 2 * j + 2)
                            nc.vector.tensor_copy(hs[:, 512:1024], psum[:, 2, :]).then_inc(s_hsd, 1)

                        columns(0, 0)
                        columns(1, 1)
                        copy_hidden(0)
                        with dve.Fori(0, NBLK // 2) as it:
                            for u in range(2):
                                j = it * 2 + u
                                e = dve.value_load(etab[0:1, ds(j, 1)], min_val=0, max_val=NX - 1)
                                dve.wait_ge(s_ht, 2 * j + 2)
                                dve.wait_ge(s_m2, j)
                                alone(dve, s_turn_v)
                                for m in range(4, M):
                                    nc.vector.tensor_scalar(hT[:, m, :], psum[:, 4, (m - 4) * P:(m - 3) * P], fb1[:, ds(e, 1), m], 0.0,
                                                            ALU.add, ALU.max).then_inc(s_htd, 1)
                                columns(j + 2, u)
                                copy_hidden(j + 1)
                                dve.wait_ge(s_m2, j + 1)
                                dve.wait_ge(s_yo[u], it * 16)
                                nc.vector.tensor_tensor(yb[:, u, :], psum[:, 5, 0:D], fb2[:, ds(e, 1), :].squeeze(1), ALU.add).then_inc(s_yb, 1)

            weights.close()
            with ExitStack() as ph10:
                yg = sb("yg", [P, G, 2, D], f32, ph10)
                id10 = sb("id10", [P, 2, G], i32, ph10)
                fin = sb("fin", [P, G, D], f32, ph10)
                s_id10 = sem("gather_places_copied")
                s_yg = [sem(f"results_gathered{k}") for k in range(G)]
                s_p1 = sem("first_result_added")
                s_fin = sem("rows_finished")
                s_out = sem("rows_stored_out")
                s_out2 = sem("last_rows_stored_out")
                with nc.Block() as block:

                    @block.gpsimd
                    def _(pool):
                        with pool.Fori(0, NG) as g:
                            pool.wait_ge(s_fin, g * G)
                            alone(pool, s_turn_p)
                            pool.tensor_copy(id10[:, :, :], place_i[:, :, ds(g * G, G)]).then_inc(s_id10, 1)
                            pool.wait_ge(s_id10, g + 1)
                            alone(pool, s_turn_p)
                            for k in range(G):
                                for n in range(2):
                                    pool.indirect_dma_start(
                                        out=yg[:, k, n, :], out_offset=None, in_=yd_d,
                                        in_offset=bass.IndirectOffsetOnAxis(ap=id10[:, n, k:k + 1], axis=0)).then_inc(s_yg[k], 16)

                    @block.vector
                    def _(dve):
                        with dve.Fori(0, NG) as g:
                            dve.wait_ge(s_out, g * 16)
                            for k in range(G):
                                t = g * G + k
                                dve.wait_ge(s_yg[k], g * 32 + 32)
                                alone(dve, s_turn_v)
                                nc.vector.scalar_tensor_tensor(fin[:, k, :], yg[:, k, 0, :], wt1[:, ds(t, 1)], xr[:, ds(t, 1), :].squeeze(1),
                                                               ALU.mult, ALU.add).then_inc(s_p1, 1)
                                dve.wait_ge(s_p1, t + 1)
                                alone(dve, s_turn_v)
                                nc.vector.scalar_tensor_tensor(fin[:, k, :], yg[:, k, 1, :], wt2[:, ds(t, 1)], fin[:, k, :],
                                                               ALU.mult, ALU.add).then_inc(s_fin, 1)

                    @block.sync
                    def _(sp):
                        y = out["y"]
                        with sp.Fori(0, NG - 1) as g:
                            sp.wait_ge(s_fin, g * G + G)
                            sp.dma_start(y[ds(g * (G * P), G * P), :].rearrange("(t p) d -> p t d", p=P), fin[:, :, :]).then_inc(s_out, 16)
                        sp.wait_ge(s_fin, NT)
                        first = (NG - 1) * G * P
                        sp.dma_start(y[first:first + (G - 1) * P, :].rearrange("(t p) d -> p t d", p=P), fin[:, 0:G - 1, :]).then_inc(s_out2, 16)
                        sp.dma_start(y[first + (G - 1) * P:N, :], fin[0:N - first - (G - 1) * P, G - 1, :]).then_inc(s_out2, 16)
                        sp.wait_ge(s_out, 16 * (NG - 1))
                        sp.wait_ge(s_out2, 32)


def kernel(**inputs):
    import numpy as _np
    import concourse.bacc as _bacc
    from concourse import mybir as _mybir
    from concourse.bass_utils import run_bass_kernel_spmd as _run

    given = {name: _np.asarray(v) for name, v in inputs.items()}
    arrays = {
        "x": _np.pad(given["x"], ((0, NP - N), (0, 0))),
        "src": _np.pad(given["src"], (0, EP - E), constant_values=PAD_KEY),
        "dst": _np.pad(given["dst"], (0, EP - E), constant_values=PAD_KEY),
        "w": _np.pad(given["edge_weight"], (0, EP - E)),
        "attr": _np.pad(given["edge_attr_64"], ((0, EP - E), (0, 0))),
        "w_self": given["L0_gnn_w_self"].transpose(1, 0),
        "w_neigh": given["L0_gnn_w_neigh"].transpose(1, 0),
        "f_Wg": given["L1_ffn_Wg"].transpose(1, 0),
        "f_W1": given["L1_ffn_W1"].transpose(0, 2, 1),
        "f_W2": given["L1_ffn_W2"].transpose(0, 2, 1),
    }
    for name in ("sW1", "sb1", "sW2", "sb2", "sW3", "sb3", "eW1", "eb1", "eW2", "eb2", "eW3", "eb3", "gW", "gb"):
        arrays[name] = given["L0_ffn_" + name]
    for name in ("u", "W1", "b1", "W2", "b2"):
        arrays["g_" + name] = given["L1_gnn_" + name]
    for name in ("bg", "b1", "b2"):
        arrays["f_" + name] = given["L1_ffn_" + name]

    nc = _bacc.Bacc("TRN2", target_bir_lowering=False, num_devices=1)
    laid, aps = {}, {}
    for name, v in arrays.items():
        v = _np.ascontiguousarray(v)
        laid[f"in_{name}_dram"] = v
        aps[name] = nc.dram_tensor(f"in_{name}_dram", v.shape, _mybir.dt.from_np(v.dtype), kind="ExternalInput").ap()
    y = nc.dram_tensor("out_y_dram", (N, D), _mybir.dt.from_np(_np.dtype("float32")), kind="ExternalOutput").ap()
    build(nc, aps, {"y": y})
    r = _run(nc, [laid], core_ids=[0])
    return r.results[0]["out_y_dram"]
```

```python
import concourse.bass as bass
from concourse import mybir
from contextlib import ExitStack

P = 128
D = 256
N = 6250
NT = -(-N // P)
NP = NT * P
G = 7
NG = NT // G
E = 100000
RUN = 4
NC = -(-E // (P * RUN)) * RUN
EP = NC * P
PAD_KEY = NP
NB = NT + 1
STEP = 16
NI = -(-(-(-E // P) + NT - 1) // STEP) * STEP
STEP4 = 16
HALF4 = 4
NI4 = -(-(-(-E // (P * RUN)) + NT - 1) // STEP4) * STEP4
IJ = -(-NI // P)
EA = 64
ER = EA + 2
RING = 8
NX = 8
HX = 1024
NBLK = (2 * NP + NX * (P - 1)) // P
NBLK += NBLK % 2
DISPATCHED = 32 * NG
LN_EPS = 1e-5

f32 = mybir.dt.float32
i32 = mybir.dt.int32
bf16 = mybir.dt.bfloat16
u8 = mybir.dt.uint8
ALU = mybir.AluOpType
ACT = mybir.ActivationFunctionType
AX = mybir.AxisListType
ds = bass.ds


class Chain:

    def __init__(self, engine, sem, base=0):
        self.engine, self.sem, self.base, self.n = engine, sem, base, 0

    def add(self, instruction):
        self.n += 1
        instruction.then_inc(self.sem, 1)

    def sync(self):
        self.engine.wait_ge(self.sem, self.base + self.n)


def wide(v, n):
    return v[:, :].unsqueeze(2).to_broadcast([P, G, n])


LN_OWN = 2 * G + 2
DENSE0_OWN = 44
XN_PARTS = (range(0, 4), range(4, G))
assert NB % 5 == 0
DENSE1_OWN = 50
HALVES = ((0, 4 * P), (4 * P, G * P))
SC = 14
assert NC % (2 * SC) == 0


def build(nc, a, out):
    ctx = ExitStack()

    def sb(name, shape, dt=f32, scope=None):
        return (scope or ctx).enter_context(nc.sbuf_tensor(name, shape, dt))

    def sem(name):
        return ctx.enter_context(nc.semaphore(name))

    def dram(name, shape, dt=f32):
        return nc.dram_tensor(name, shape, dt, kind="Internal").ap()

    with ctx:
        xn_d = dram("xn_rows", [NP, D])
        edges_d = dram("sorted_edges", [EP, ER])
        item_d = dram("item_rows", [4, IJ * P], i32)
        xd_d = dram("dispatched", [(NBLK + 2) * P, D])
        yd_d = dram("expert_rows", [NBLK * P, D])
        psum = ctx.enter_context(nc.psum_tensor("psum", [P, 8, 512], f32))

        ident = sb("ident", [P, P])
        iota_r = sb("iota_r", [P, P])
        upper = sb("upper", [P, P])
        ones = sb("ones", [P, P])
        xr = sb("xr", [P, NT, D])
        rstd = sb("rstd", [P, NT])
        nmr = sb("nmr", [P, NT])
        sd = sb("sd", [P, G])
        eps = sb("eps", [P, 1])
        early = ctx.enter_context(ExitStack())
        items = sb("items", [4, IJ * P], i32, early)
        pos_i = sb("pos_i", [P, NC], i32, early)
        acc = sb("acc", [P, NB, D], f32, early)

        s_const = sem("constants")
        s_x = sem("x_loaded")
        s_dst = sem("dst_loaded")
        s_src = sem("src_loaded")
        s_own = sem("vector_own")
        s_sgn = sem("source_counts")
        s_var = sem("variance_ready")
        s_sd = sem("deviation_ready")
        s_ln = sem("rstd_ready")
        s_xn = sem("xn_ready")
        s_xst = [sem(f"xn_stored{h}") for h in range(2)]
        s_cum = sem("counts_ready")
        s_off = sem("offsets_in_psum")
        s_base = sem("base_ready")
        s_tab = sem("tables_ready")
        s_tabT = sem("tables_transposed")
        s_row = sem("rows_ready")
        s_rst = sem("rows_stored")
        s_rld = sem("rows_loaded")
        s_cidx = sem("chunk_indices")
        s_pg = sem("item_rows_gathered")
        s_pf = sem("item_rows_ready")
        s_pt = sem("item_rows_transposed")
        s_pe = sem("item_columns_ready")
        s_z = sem("zero_ready")
        s_xdz = sem("dispatch_zeroed")

        s_turn = sem("turns")

        def alone(engine):
            engine.sem_inc(s_turn, 1)

        def normalise(dve, own, x, g, ln, s_var, s_sd, s_rstd):
            nc.vector.memset(ln["nil"][:, 2:3], 0.0)
            for k in range(G):
                own.add(nc.vector.bn_stats(ln["stats"][:, k, :], x[:, ds(g * G + k, 1), :].squeeze(1)))
            own.sync()
            nc.vector.memset(ln["nil"][:, 0:1], 0.0)
            for k in range(G):
                own.add(nc.vector.bn_aggr(ln["mv"][:, k, :], ln["stats"][:, k, :]))
            own.sync()
            nc.vector.memset(ln["nil"][:, 1:2], 0.0).then_inc(s_var, 1)
            dve.wait_ge(s_sd, g + 1)
            own.add(nc.vector.reciprocal(ln["rstd"][:, :], ln["sd"][:, :]))
            own.sync()
            nc.vector.scalar_tensor_tensor(ln["nmr"][:, :], ln["mv"][:, :, 0], -1.0, ln["rstd"][:, :],
                                           ALU.mult, ALU.mult).then_inc(s_rstd, 1)

        def top_two(own, gt, g1, rev, n):
            for v, o, eq, sc, key, src in (("v1", "o1", "eq", "sc", "k1", "g"), ("v2", "o2", "eq2", "sc2", "k2", "g2")):
                if src == "g2":
                    own.add(nc.vector.scalar_tensor_tensor(gt["g2"][:, :, :], gt["o1"][:, :, :], -1e30, gt["g"][:, :, :], ALU.mult, ALU.add))
                    own.sync()
                own.add(nc.vector.tensor_reduce(g1[v][:, :], gt[src][:, :, :], AX.X, ALU.max))
                own.sync()
                own.add(nc.vector.tensor_tensor(gt[eq][:, :, :], gt[src][:, :, :], wide(g1[v], n), ALU.is_equal))
                own.sync()
                own.add(nc.vector.tensor_tensor(gt[sc][:, :, :], gt[eq][:, :, :], rev[:, 0:n].unsqueeze(1).to_broadcast([P, G, n]), ALU.mult))
                own.sync()
                own.add(nc.vector.tensor_reduce(g1[key][:, :], gt[sc][:, :, :], AX.X, ALU.max))
                own.sync()
                own.add(nc.vector.tensor_tensor(gt[o][:, :, :], gt[sc][:, :, :], wide(g1[key], n), ALU.is_equal))
                own.sync()

        def two_weights(own, g1):
            own.add(nc.vector.tensor_scalar(g1["t"][:, :], g1["x"][:, :], 1.0, None, ALU.add))
            own.sync()
            own.add(nc.vector.reciprocal(g1["w1"][:, :], g1["t"][:, :]))
            own.sync()
            own.add(nc.vector.tensor_tensor(g1["w2"][:, :], g1["x"][:, :], g1["w1"][:, :], ALU.mult))
            own.sync()

        with ExitStack() as ph:
            it_src = sb("it_src", [P, IJ * P], i32, ph)
            it_rel = sb("it_rel", [P, IJ * P], f32, ph)
            it_w = sb("it_w", [P, IJ * P], f32, ph)
            kb = sb("kb", [P, NC], f32, ph)
            base = sb("base", [P, NB + 2], f32, ph)
            bnum = sb("bnum", [P, NB + 2], f32, ph)
            with ExitStack() as ph1:
                iota_i = sb("iota_i", [P, P], i32, ph1)
                dst_i = sb("dst_i", [P, NC], i32, ph1)
                src_i = sb("src_i", [P, NC], i32, ph1)
                dst_f = sb("dst_f", [P, NC], f32, ph1)
                src_f = sb("src_f", [P, NC], f32, ph1)
                junk = sb("junk", [P, NC], f32, ph1)
                junk2 = sb("junk2", [P, NC], f32, ph1)
                nil = sb("nil", [P, 4], f32, ph1)
                thr = sb("thr", [P, NB], f32, ph1)
                thr_h = sb("thr_h", [P, NB], f32, ph1)
                thr_i = sb("thr_i", [P, NB + 2], i32, ph1)
                item_i = sb("item_i", [P, IJ], i32, ph1)
                item_f = sb("item_f", [P, IJ], f32, ph1)
                cum = sb("cum", [P, 2, NB + 1], f32, ph1)
                cnt = sb("cnt", [P, NB], f32, ph1)
                starts = sb("starts", [P, 2, NB + 1], f32, ph1)
                st_i = sb("st_i", [P, 2, NB + 1], i32, ph1)
                up_i = sb("up_i", [P, 2, NB + 1], i32, ph1)
                c0_i = sb("c0_i", [P, 2, NB + 1], i32, ph1)
                c1_i = sb("c1_i", [P, 2, NB + 1], i32, ph1)
                ni = sb("ni", [P, 2, NB], f32, ph1)
                nz = sb("nz", [P, 2, NB], f32, ph1)
                iend = sb("iend", [P, 2, NB], f32, ph1)
                dif = sb("dif", [P, 2, NB], f32, ph1)
                ddif = sb("ddif", [P, 2, NT], f32, ph1)
                geq = sb("geq", [P, IJ, NT], f32, ph1)
                prod = sb("prod", [P, IJ, NT], f32, ph1)
                tab = sb("tab", [P, 4, IJ], f32, ph1)
                cidx = sb("cidx", [P, IJ], i32, ph1)
                tabT = sb("tabT", [4 * IJ, P], i32, ph1)
                t128 = sb("t128", [P, IJ], f32, ph1)
                row_i = sb("row_i", [P, IJ, 2, P], i32, ph1)
                row_w = sb("row_w", [P, IJ, P], f32, ph1)
                row_f = sb("row_f", [P, IJ, 2, P], f32, ph1)
                stats = sb("stats", [P, G, 6], f32, ph1)
                mv = sb("mv", [P, G, 2], f32, ph1)
                xn_st = sb("xn_st", [P, G, D], f32, ph1)
                zero = sb("zero", [P, 2 * D], f32, ph1)

                with nc.Block() as block:

                    @block.sync
                    def _(sp):
                        sp.dma_start(dst_i[:, :], a["dst"].rearrange("(p c) -> p c", p=P)).then_inc(s_dst, 16)
                        sp.dma_start(src_i[:, :], a["src"].rearrange("(p c) -> p c", p=P)).then_inc(s_src, 16)
                        sp.dma_start(xr[:, :, :], a["x"].rearrange("(t p) d -> p t d", p=P)).then_inc(s_x, 16)
                        sp.wait_ge(s_row, 1)
                        sp.dma_start(item_d.rearrange("k (j p) -> (k j) p", p=P), tabT[:, :]).then_inc(s_rst, 16)
                        sp.wait_ge(s_rst, 16)
                        sp.dma_start(items[:, :], item_d).then_inc(s_rld, 16)
                        with sp.Fori(0, NG) as g:
                            for h, tiles in enumerate(XN_PARTS):
                                sp.wait_ge(s_xn, g * G + tiles[-1] + 1)
                                sp.dma_start(
                                    xn_d[ds(g * (G * P) + tiles[0] * P, len(tiles) * P), :].rearrange("(t p) d -> p t d", p=P),
                                    xn_st[:, tiles[0]:tiles[-1] + 1, :]).then_inc(s_xst[h], 16)
                        for h in range(2):
                            sp.wait_ge(s_xst[h], 16 * NG + 1)
                        sp.wait_ge(s_rld, 16)

                    @block.gpsimd
                    def _(pool):
                        own = Chain(pool, s_const)
                        own.add(pool.memset(ident[:, :], 0.0))
                        own.add(pool.memset(ones[:, :], 1.0))
                        own.add(pool.iota(iota_i[:, :], pattern=[[1, P]], base=0, channel_multiplier=0))
                        own.add(pool.iota(thr_i[:, :], pattern=[[P, NB + 2]], base=0, channel_multiplier=0))
                        own.add(pool.memset(eps[:, :], LN_EPS))
                        own.add(pool.iota(item_i[:, :], pattern=[[P, IJ]], base=0, channel_multiplier=1))
                        own.sync()
                        own.add(pool.affine_select(out=ident[:, :], in_=ident[:, :], compare_op=ALU.not_equal,
                                                   fill=1.0, base=0, pattern=[[-1, P]], channel_multiplier=1))
                        own.add(pool.affine_select(out=upper[:, :], in_=ones[:, :], compare_op=ALU.is_gt,
                                                   fill=0.0, base=0, pattern=[[1, P]], channel_multiplier=-1))
                        own.add(pool.memset(acc[:, :, :], 0.0))
                        pool.wait_ge(s_cidx, 1)
                        for j in range(IJ):
                            off = bass.IndirectOffsetOnAxis(ap=cidx[:, j:j + 1], axis=0)
                            for n, name in enumerate(("src", "dst")):
                                pool.indirect_dma_start(
                                    out=row_i[:, j, n, :], out_offset=None,
                                    in_=a[name].rearrange("(c p) -> c p", p=P), in_offset=off).then_inc(s_pg, 16)
                            pool.indirect_dma_start(
                                out=row_w[:, j, :], out_offset=None,
                                in_=a["w"].rearrange("(c p) -> c p", p=P), in_offset=off).then_inc(s_pg, 16)

                    @block.scalar
                    def _(act):
                        for h in range(2):
                            act.sem_inc(s_xst[h], 1)
                        act.wait_ge(s_z, 1)
                        act.dma_start(xd_d.rearrange("(p r c) d -> p r (c d)", p=P, c=2),
                                      zero[:, :].unsqueeze(1).to_broadcast([P, NBLK // 2 + 1, 2 * D])).then_inc(s_xdz, 16)
                        act.wait_ge(s_sgn, 1)
                        with act.Fori(0, NB // 5) as it:
                            for k in range(5):
                                act.wait_ge(s_sgn, it * 5 + k + 1)
                                alone(act)
                                nc.scalar.activation(junk2[:, :], src_f[:, :], ACT.Sign, scale=-1.0, bias=thr_h[:, ds(it * 5 + k, 1)],
                                                     accum_out=cum[:, 1, ds(it * 5 + k + 1, 1)]).then_inc(s_sgn, 1)

                        def deviation(g):
                            act.wait_ge(s_var, g + 1)
                            nc.scalar.activation(sd[:, :], mv[:, :, 1], ACT.Sqrt, bias=eps[:, :]).then_inc(s_sd, 1)

                        def rows(g):
                            act.wait_ge(s_ln, g + 1)
                            for h, tiles in enumerate(XN_PARTS):
                                act.wait_ge(s_xst[h], 16 * g + 1)
                                alone(act)
                                for k in tiles:
                                    t = g * G + k
                                    nc.scalar.activation(xn_st[:, k, :], xr[:, ds(t, 1), :], ACT.Identity,
                                                         bias=nmr[:, ds(t, 1)], scale=rstd[:, ds(t, 1)]).then_inc(s_xn, 1)

                        deviation(0)
                        with act.Fori(0, NG - 1) as g:
                            deviation(g + 1)
                            rows(g)
                        rows(NG - 1)
                        act.wait_ge(s_xdz, 16)

                    @block.vector
                    def _(dve):
                        own = Chain(dve, s_own)
                        nc.vector.memset(zero[:, :], 0.0).then_inc(s_z, 1)
                        dve.wait_ge(s_const, 8)
                        own.add(nc.vector.tensor_copy(iota_r[:, :], iota_i[:, :]))
                        own.add(nc.vector.tensor_copy(thr[:, :], thr_i[:, 1:NB + 1]))
                        own.add(nc.vector.tensor_copy(item_f[:, :], item_i[:, :]))
                        own.add(nc.vector.memset(cum[:, :, 0:1], 0.0))
                        dve.wait_ge(s_dst, 16)
                        own.add(nc.vector.tensor_copy(dst_f[:, :], dst_i[:, :]))
                        dve.wait_ge(s_src, 16)
                        own.add(nc.vector.tensor_copy(src_f[:, :], src_i[:, :]))
                        own.add(nc.vector.tensor_scalar(thr_h[:, :], thr_i[:, 1:NB + 1], -0.5, None, ALU.add))
                        own.sync()
                        nc.vector.memset(nil[:, 2:3], 0.0).then_inc(s_sgn, 1)
                        with dve.Fori(0, NB) as b:
                            dve.wait_ge(s_own, own.n + b)
                            nc.vector.tensor_scalar(junk[:, :], dst_f[:, :], thr[:, ds(b, 1)], None,
                                                    ALU.is_lt, ALU.add, accum_out=cum[:, 0, ds(b + 1, 1)]).then_inc(s_own, 1)
                        own.n += NB
                        dve.wait_ge(s_sgn, NB + 1)
                        own.add(nc.vector.tensor_scalar(cum[:, 1, 1:NB + 1], cum[:, 1, 1:NB + 1], float(NC), 0.5, ALU.add, ALU.mult))
                        own.sync()
                        own.add(nc.vector.tensor_tensor(cnt[:, :], cum[:, 1, 1:NB + 1], cum[:, 1, 0:NB], ALU.subtract))
                        own.sync()
                        nc.vector.memset(t128[:, :], 0.0).then_inc(s_cum, 1)
                        dve.wait_ge(s_off, 1)
                        own.add(nc.vector.tensor_copy(starts[:, :, :], psum[:, 0, 0:2 * (NB + 1)].rearrange("p (k b) -> p k b", k=2)))
                        own.sync()
                        own.add(nc.vector.tensor_copy(st_i[:, :, :], starts[:, :, :]))
                        for k, size in enumerate((P, P * RUN)):
                            own.add(nc.vector.tensor_scalar(up_i[:, k, :], starts[:, k, :], float(size - 1), None, ALU.add))
                        own.add(nc.vector.tensor_tensor(base[:, 0:NB], psum[:, 1, 0:NB], starts[:, 1, 0:NB], ALU.add))
                        own.sync()
                        for k, size in enumerate((P, P * RUN)):
                            shift = size.bit_length() - 1
                            own.add(nc.vector.tensor_scalar(c0_i[:, k, :], st_i[:, k, :], shift, None, ALU.arith_shift_right))
                            own.add(nc.vector.tensor_scalar(c1_i[:, k, :], up_i[:, k, :], shift, None, ALU.arith_shift_right))
                        own.add(nc.vector.tensor_tensor(nz[:, :, :], starts[:, :, 1:NB + 1], starts[:, :, 0:NB], ALU.is_gt))
                        own.add(nc.vector.tensor_scalar(base[:, 0:NB], base[:, 0:NB], 1.0, None, ALU.subtract))
                        own.sync()
                        own.add(nc.vector.tensor_tensor(ni[:, :, :], c1_i[:, :, 1:NB + 1], c0_i[:, :, 0:NB], ALU.subtract))
                        own.sync()
                        own.add(nc.vector.tensor_tensor(ni[:, :, :], ni[:, :, :], nz[:, :, :], ALU.mult))
                        own.sync()
                        for k in range(2):
                            own.add(nc.vector.tensor_tensor_scan(iend[:, k, :], ni[:, k, :], ni[:, k, :], 0.0, ALU.add, ALU.bypass))
                        own.sync()
                        own.add(nc.vector.tensor_tensor(dif[:, :, :], ni[:, :, :], iend[:, :, :], ALU.subtract))
                        own.sync()
                        own.add(nc.vector.tensor_tensor(dif[:, :, :], dif[:, :, :], c0_i[:, :, 0:NB], ALU.add))
                        own.sync()
                        own.add(nc.vector.tensor_tensor(ddif[:, :, :], dif[:, :, 1:NB], dif[:, :, 0:NT], ALU.subtract))
                        own.sync()
                        for k in range(2):
                            own.add(nc.vector.tensor_tensor(geq[:, :, :], iend[:, k, 0:NT].unsqueeze(1).to_broadcast([P, IJ, NT]),
                                                            item_f[:, :].unsqueeze(2).to_broadcast([P, IJ, NT]), ALU.is_le))
                            own.sync()
                            own.add(nc.vector.tensor_reduce(tab[:, k, :], geq[:, :, :], AX.X, ALU.add))
                            own.add(nc.vector.tensor_tensor(prod[:, :, :], geq[:, :, :],
                                                            ddif[:, k, :].unsqueeze(1).to_broadcast([P, IJ, NT]), ALU.mult))
                            own.sync()
                            own.add(nc.vector.tensor_reduce(tab[:, 2 + k, :], prod[:, :, :], AX.X, ALU.add))
                            own.sync()
                            own.add(nc.vector.tensor_tensor(tab[:, 2 + k, :], tab[:, 2 + k, :], item_f[:, :], ALU.add))
                            own.sync()
                            own.add(nc.vector.tensor_scalar(tab[:, 2 + k, :], tab[:, 2 + k, :], float(NC // (RUN if k else 1) - 1), None, ALU.min))
                            own.sync()
                        nc.vector.tensor_copy(cidx[:, :], tab[:, 2, :]).then_inc(s_cidx, 1)
                        nc.vector.tensor_scalar(t128[:, :], tab[:, 0, :], float(P), None, ALU.mult).then_inc(s_tab, 1)
                        dve.wait_ge(s_tabT, 1)
                        nc.vector.tensor_copy(tabT[:, :], psum[0:4 * IJ, 2, 0:P]).then_inc(s_row, 1)
                        own.add(nc.vector.memset(base[:, NB:NB + 2], 0.0))
                        own.add(nc.vector.tensor_scalar(dst_i[:, :], src_i[:, :], 7, None, ALU.arith_shift_right))
                        own.sync()
                        own.add(nc.vector.tensor_copy(kb[:, :], dst_i[:, :]))
                        own.add(nc.vector.tensor_scalar(bnum[:, :], thr_i[:, :], 1.0 / P, None, ALU.mult))
                        dve.wait_ge(s_x, 16)
                        n1 = own.n
                        with dve.Fori(0, NG) as g:
                            own = Chain(dve, s_own, g * LN_OWN + n1)
                            own.sync()
                            nc.vector.memset(nil[:, 2:3], 0.0)
                            for k in range(G):
                                own.add(nc.vector.bn_stats(stats[:, k, :], xr[:, ds(g * G + k, 1), :].squeeze(1)))
                            own.sync()
                            nc.vector.memset(nil[:, 0:1], 0.0)
                            for k in range(G):
                                own.add(nc.vector.bn_aggr(mv[:, k, :], stats[:, k, :]))
                            own.sync()
                            nc.vector.memset(nil[:, 1:2], 0.0).then_inc(s_var, 1)
                            dve.wait_ge(s_sd, g + 1)
                            alone(dve)
                            own.add(nc.vector.reciprocal(rstd[:, ds(g * G, G)], sd[:, :]))
                            own.sync()
                            alone(dve)
                            own.add(nc.vector.scalar_tensor_tensor(nmr[:, ds(g * G, G)], mv[:, :, 0], -1.0, rstd[:, ds(g * G, G)], ALU.mult, ALU.mult))
                            own.sync()
                            nc.vector.memset(nil[:, 3:4], 0.0).then_inc(s_ln, 1)
                            assert own.n == LN_OWN, own.n
                        own = Chain(dve, s_own, n1 + NG * LN_OWN)
                        own.sync()
                        dve.wait_ge(s_pg, 3 * 16 * IJ)
                        own.add(nc.vector.tensor_copy(row_f[:, :, :, :], row_i[:, :, :, :]))
                        own.sync()
                        nc.vector.tensor_tensor(row_f[:, :, 1, :], row_f[:, :, 1, :], t128[:, :].unsqueeze(2).to_broadcast([P, IJ, P]),
                                                ALU.subtract).then_inc(s_pf, 1)
                        for j in range(IJ):
                            dve.wait_ge(s_pt, j + 1)
                            nc.vector.tensor_scalar(it_src[:, j * P:(j + 1) * P], psum[:, 3 + j % 2, 0:P], float(NP - 1), None,
                                                    ALU.min).then_inc(s_pe, 1)
                            nc.vector.tensor_copy(it_rel[:, j * P:(j + 1) * P], psum[:, 3 + j % 2, P:2 * P]).then_inc(s_pe, 1)
                            nc.vector.tensor_copy(it_w[:, j * P:(j + 1) * P], psum[:, 3 + j % 2, 2 * P:3 * P]).then_inc(s_pe, 1)

                    @block.tensor
                    def _(pe):
                        pe.wait_ge(s_const, 8)
                        pe.wait_ge(s_cum, 1)
                        nc.tensor.matmul(psum[:, 0, 0:2 * (NB + 1)], ones[:, :], cum[:, :, :].rearrange("p k b -> p (k b)"),
                                         start=True, stop=True)
                        nc.tensor.matmul(psum[:, 1, 0:NB], upper[:, :], cnt[:, :], start=True, stop=True).then_inc(s_off, 1)
                        pe.wait_ge(s_tab, 1)
                        nc.tensor.transpose(psum[0:4 * IJ, 2, 0:P], tab[:, :, :].rearrange("p k j -> p (k j)"), ident[:, :]).then_inc(s_tabT, 1)
                        pe.wait_ge(s_pf, 1)
                        for j in range(IJ):
                            if j >= 2:
                                pe.wait_ge(s_pe, 3 * (j - 1))
                            nc.tensor.transpose(psum[:, 3 + j % 2, 0:P], row_f[:, j, 0, :], ident[:, :])
                            nc.tensor.transpose(psum[:, 3 + j % 2, P:2 * P], row_f[:, j, 1, :], ident[:, :])
                            nc.tensor.transpose(psum[:, 3 + j % 2, 2 * P:3 * P], row_w[:, j, :], ident[:, :]).then_inc(s_pt, 1)

            s_hot = sem("l0_onehot_ready")
            s_mm = sem("l0_products")
            s_acc = sem("l0_added")
            s_gat = [sem(f"l0_gathered{u}") for u in range(RING)]
            s_idx = sem("l0_indices_ready")
            s_rank = sem("ranked")
            with ExitStack() as ph2:
                idx = sb("idx", [P, 2, RING], i32, ph2)
                rows = sb("rows", [P, RING, D], f32, ph2)
                hot = sb("hot", [P, RING, P], f32, ph2)
                mask = sb("mask", [P, NC], f32, ph2)
                rank = sb("rank", [P, NC], f32, ph2)
                pos = sb("pos", [P, NC], f32, ph2)
                with nc.Block() as block:

                    @block.scalar
                    def _(act):
                        for h in range(2):
                            nc.scalar.activation(idx[:, h, :], it_src[:, h * RING:(h + 1) * RING], ACT.Copy).then_inc(s_idx, 1)
                        with act.Fori(0, NI // STEP - 1) as it:
                            for h in range(2):
                                act.wait_ge(s_mm, RING + it * STEP + (h + 1) * RING)
                                nc.scalar.activation(idx[:, h, :], it_src[:, ds((it + 1) * STEP + h * RING, RING)],
                                                     ACT.Copy).then_inc(s_idx, 1)

                    @block.gpsimd
                    def _(pool):
                        with pool.Fori(0, NI // STEP) as it:
                            for u in range(STEP):
                                if u % RING == 0:
                                    pool.wait_ge(s_idx, it * 2 + u // RING + 1)
                                pool.wait_ge(s_mm, it * STEP + u + 1)
                                alone(pool)
                                pool.indirect_dma_start(
                                    out=rows[:, u % RING, :], out_offset=None, in_=xn_d,
                                    in_offset=bass.IndirectOffsetOnAxis(ap=idx[:, u // RING, u % RING:u % RING + 1], axis=0),
                                ).then_inc(s_gat[u % RING], 16)

                    @block.tensor
                    def _(pe):
                        pe.sem_inc(s_mm, RING)
                        with pe.Fori(0, NI // STEP) as it:
                            for u in range(STEP):
                                pe.wait_ge(s_hot, it * STEP + u + 1)
                                pe.wait_ge(s_gat[u % RING], it * (16 * STEP // RING) + 16 * (u // RING + 1))
                                pe.wait_ge(s_acc, it * STEP + u + 1)
                                nc.tensor.matmul(psum[:, u % RING, 0:D], hot[:, u % RING, :], rows[:, u % RING, :],
                                                 start=True, stop=True).then_inc(s_mm, 1)

                    @block.vector
                    def _(dve):
                        dve.sem_inc(s_acc, RING)
                        nc.vector.memset(pos[:, :], 0.0).then_inc(s_rank, 1)
                        with dve.Fori(0, NI // STEP) as it:

                            def onehot(u):
                                dve.wait_ge(s_mm, it * STEP + u + 1)
                                nc.vector.tensor_scalar(hot[:, u % RING, :], iota_r[:, :], it_rel[:, ds(it * STEP + u, 1)],
                                                        it_w[:, ds(it * STEP + u, 1)], ALU.is_equal, ALU.mult).then_inc(s_hot, 1)

                            for u in range(RING):
                                onehot(u)
                            dve.wait_ge(s_rank, it * 3 + 1)
                            nc.vector.tensor_scalar(mask[:, :], kb[:, :], bnum[:, ds(it, 1)], None, ALU.is_equal).then_inc(s_rank, 1)
                            dve.wait_ge(s_rank, it * 3 + 2)
                            nc.vector.tensor_tensor_scan(rank[:, :], mask[:, :], mask[:, :], base[:, ds(it, 1)],
                                                         ALU.add, ALU.bypass).then_inc(s_rank, 1)
                            dve.wait_ge(s_rank, it * 3 + 3)
                            alone(dve)
                            nc.vector.copy_predicated(pos[:, :], mask[:, :].bitcast(i32), rank[:, :]).then_inc(s_rank, 1)
                            for half in range(2):
                                tiles = nc.values_load_multi_w_load_instructions(
                                    items[0:1, ds(it * STEP + half * RING, RING)], [mybir.EngineType.DVE], min_val=0, max_val=NB - 1,
                                    skip_runtime_bounds_check_because="a tile's number is a count of at most NB - 1 buckets")[1]
                                for k in range(RING):
                                    u = half * RING + k
                                    dve.wait_ge(s_mm, RING + it * STEP + u + 1)
                                    dve.wait_ge(s_acc, RING + it * STEP + u)
                                    there = acc[:, ds(tiles[k], 1), :].squeeze(1)
                                    nc.vector.tensor_tensor(there, there, psum[:, u % RING, 0:D], ALU.add).then_inc(s_acc, 1)
                                    if half == 0:
                                        onehot(u + RING)
                        dve.wait_ge(s_rank, 3 * (NI // STEP) + 1)
                        nc.vector.tensor_copy(pos_i[:, :], pos[:, :]).then_inc(s_rank, 1)

        with ExitStack() as ph3:
            stage = sb("stage", [P, 2, SC, ER], f32, ph3)
            sidx = sb("sidx", [P, 2, SC], i32, ph3)
            src3 = sb("src3", [P, NC], i32, ph3)
            w_self = sb("w_self", [P, 2, D], f32, ph3)
            w_neigh = sb("w_neigh", [P, 2, D], f32, ph3)
            w1 = sb("w1", [P, 2, 6, P], f32, ph3)
            b1 = sb("b1", [P, 6], f32, ph3)
            w2s = sb("w2s", [P, 2, P], f32, ph3)
            w2e = sb("w2e", [P, 4, P // 2], f32, ph3)
            b2 = sb("b2", [P, 3], f32, ph3)
            w3 = sb("w3", [P, 3, D], f32, ph3)
            b3 = sb("b3", [5, D], f32, ph3)
            gw = sb("gw", [P, 2, 4], f32, ph3)
            gb = sb("gb", [1, 4], f32, ph3)
            pair = sb("pair", [4, 2, P], f32, ph3)
            rev = sb("rev", [P, 8], f32, ph3)
            rev_i = sb("rev_i", [P, 8], i32, ph3)
            xs = sb("xs", [P, G, 2 * D], f32, ph3)
            tT = sb("tT", [P, 2, 4, P], f32, ph3)
            sq = sb("sq", [P, D], f32, ph3)
            ss = sb("ss", [P, G], f32, ph3)
            nrm = sb("nrm", [P, G], f32, ph3)
            rn = sb("rn", [P, G], f32, ph3)
            ln = {n: sb("ln_" + n, s, f32, ph3) for n, s in
                  (("stats", [P, G, 6]), ("mv", [P, G, 2]), ("sd", [P, G]), ("rstd", [P, G]), ("nmr", [P, G]), ("nil", [P, 4]))}
            yT = sb("yT", [P, 2, G * P], f32, ph3)
            h1 = sb("h1", [P, 6, G * P], f32, ph3)
            h2 = sb("h2", [P, 3, G * P], f32, ph3)
            gt = {n: sb("gt_" + n, [P, G, 4], f32, ph3) for n in ("l", "e", "g", "eq", "sc", "o1", "g2", "eq2", "sc2", "o2")}
            g1 = {n: sb("g1_" + n, [P, G], f32, ph3) for n in ("m", "s", "r", "v1", "k1", "v2", "k2", "d", "x", "t", "w1", "w2")}
            cf = sb("cf", [P, G, 5], f32, ph3)
            cfT = sb("cfT", [5, G * P], f32, ph3)

            s_w3 = sem("l0_weights")
            s_att = [sem(f"attributes_loaded{h}") for h in range(2)]
            s_side = sem("scatter_sides_ready")
            s_own3 = sem("l0_vector_own")
            s_sca = [sem(f"scattered{h}") for h in range(2)]
            s_c3 = sem("l0_constants")
            s_a = sem("l0_normalised")
            s_t1 = sem("l0_transposed")
            s_t1c = sem("l0_columns")
            s_gnn = sem("l0_gnn_products")
            s_ss = sem("l0_squares")
            s_nrm = sem("l0_norms")
            s_v3 = sem("l0_variance")
            s_sd3 = sem("l0_deviation")
            s_ln3 = sem("l0_rstd")
            s_y = sem("l0_ffn_rows")
            s_t2 = sem("l0_ffn_transposed")
            s_yT = sem("l0_ffn_columns")
            s_h1 = sem("l0_hidden1_products")
            s_h1c = sem("l0_hidden1")
            s_h2 = sem("l0_hidden2_products")
            s_h2c = sem("l0_hidden2")
            s_lg = sem("l0_logits")
            s_mx = sem("l0_shifted")
            s_ex = sem("l0_exponentials")
            s_df = sem("l0_gate_gap")
            s_ex2 = sem("l0_gate_ratio")
            s_cf = sem("l0_coefficients")
            s_cT = sem("l0_coefficients_transposed")
            s_cTc = sem("l0_coefficient_columns")
            s_gbr = sem("l0_gates_spread")
            s_h2g = sem("l0_hidden2_gated")
            s_y3 = sem("l0_ffn_products")
            s_x2 = sem("l0_rows_done")

            with nc.Block() as block:

                @block.sync
                def _(sp):
                    for dst, src in (
                        (w_self[:, :, :], a["w_self"].rearrange("(c p) n -> p c n", p=P)),
                        (w_neigh[:, :, :], a["w_neigh"].rearrange("(c p) n -> p c n", p=P)),
                        (w1[:, :, 0:2, :], a["sW1"].rearrange("(c p) (m n) -> p c m n", p=P, n=P)),
                        (w2s[:, :, :], a["sW2"].rearrange("(c p) n -> p c n", p=P)),
                        (w2e[:, :, :], a["eW2"].rearrange("e p n -> p e n")),
                        (w3[:, 0, :], a["sW3"]),
                        (w3[:, 1:3, :], a["eW3"].rearrange("(q e) k n -> (e k) q n", q=2)),
                        (b3[0:4, :], a["eb3"]),
                        (b3[4:5, :], a["sb3"].unsqueeze(0)),
                        (gw[:, :, :], a["gW"].rearrange("(c p) n -> p c n", p=P)),
                        (gb[:, :], a["gb"].unsqueeze(0)),
                        (b1[:, 0:2], a["sb1"].rearrange("(m p) -> p m", p=P)),
                        (b1[:, 2:6], a["eb1"].rearrange("e p -> p e")),
                        (b2[:, 0:1], a["sb2"].unsqueeze(1)),
                        (b2[:, 1:3], a["eb2"].rearrange("(q e) k -> (e k) q", q=2)),
                        (src3[:, :], a["src"].rearrange("(p c) -> p c", p=P)),
                    ):
                        with nc.allow_non_contiguous_dma(reason="a few hundred biases"):
                            sp.dma_start(dst, src).then_inc(s_w3, 16)
                    for c in range(2):
                        sp.dma_start(w1[:, c, 2:6, :], a["eW1"][:, c * P:(c + 1) * P, :].rearrange("e p n -> p e n")).then_inc(s_w3, 16)
                    attr = a["attr"].rearrange("(p c) f -> p c f", p=P)
                    for h in range(2):
                        sp.dma_start(stage[:, h, :, 0:EA], attr[:, h * SC:(h + 1) * SC, :]).then_inc(s_att[h], 16)
                    with sp.Fori(0, NC // SC // 2 - 1) as it:
                        for h in range(2):
                            sp.wait_ge(s_sca[h], (it + 1) * (16 * SC))
                            sp.dma_start(stage[:, h, :, 0:EA], attr[:, ds((it + 1) * (2 * SC) + h * SC, SC), :]).then_inc(s_att[h], 16)

                @block.gpsimd
                def _(pool):
                    own = Chain(pool, s_c3)
                    own.add(pool.iota(rev_i[:, :], pattern=[[-1, 8]], base=8, channel_multiplier=0))
                    own.add(pool.memset(pair[:, :, :], 0.0))
                    own.add(pool.memset(stage[:, :, :, EA:EA + 1], 1.0))
                    own.add(pool.memset(cf[:, :, 4:5], 1.0))
                    own.sync()
                    for m in range(4):
                        own.add(pool.affine_select(out=pair[:, m // 2, m % 2 * (P // 2):(m % 2 + 1) * (P // 2)],
                                                   in_=pair[:, m // 2, m % 2 * (P // 2):(m % 2 + 1) * (P // 2)],
                                                   compare_op=ALU.not_equal, fill=1.0, base=-m,
                                                   pattern=[[0, P // 2]], channel_multiplier=1))
                    own.sync()
                    with pool.Fori(0, NC // SC // 2) as it:
                        for h in range(2):
                            pool.wait_ge(s_att[h], it * 16 + 16)
                            alone(pool)
                            at = ds(it * (2 * SC) + h * SC, SC)
                            pool.tensor_copy(sidx[:, h, :], pos_i[:, at]).then_inc(s_side, 1)
                            pool.tensor_copy(stage[:, h, :, EA + 1], src3[:, at]).then_inc(s_side, 1)
                            pool.wait_ge(s_side, it * 4 + 2 * h + 2)
                            alone(pool)
                            for c in range(SC):
                                pool.indirect_dma_start(
                                    out=edges_d, out_offset=bass.IndirectOffsetOnAxis(ap=sidx[:, h, c:c + 1], axis=0),
                                    in_=stage[:, h, c, :], in_offset=None).then_inc(s_sca[h], 16)
                    for h in range(2):
                        pool.wait_ge(s_sca[h], 16 * SC * (NC // SC // 2))

                @block.scalar
                def _(act):
                    act.wait_ge(s_w3, 16 * 18)
                    act.wait_ge(s_c3, 8)
                    act.sem_inc(s_t2, 1)
                    act.sem_inc(s_ss, 1)
                    with act.Fori(0, NG) as g:
                        act.wait_ge(s_t2, g * G + 1)
                        alone(act)
                        for k in range(G):
                            t = g * G + k
                            nc.scalar.activation(xs[:, k, 0:D], xr[:, ds(t, 1), :].squeeze(1), ACT.Identity,
                                                 bias=nmr[:, ds(t, 1)], scale=rstd[:, ds(t, 1)])
                            nc.scalar.activation(xs[:, k, D:2 * D], acc[:, ds(t, 1), :].squeeze(1), ACT.Copy).then_inc(s_a, 1)
                        for k in range(G):
                            act.wait_ge(s_gnn, g * G + min(k | 1, G - 1) + 1)
                            act.wait_ge(s_ss, g * G + k + 1)
                            nc.scalar.activation(sq[:, :], psum[:, k // 2, k % 2 * D:(k % 2 + 1) * D], ACT.Square,
                                                 accum_out=ss[:, k:k + 1]).then_inc(s_ss, 1)
                        act.wait_ge(s_ss, g * G + G + 1)
                        nc.scalar.activation(nrm[:, :], ss[:, :], ACT.Sqrt).then_inc(s_nrm, 1)
                        act.wait_ge(s_v3, g + 1)
                        nc.scalar.activation(ln["sd"][:, :], ln["mv"][:, :, 1], ACT.Sqrt, bias=eps[:, :]).then_inc(s_sd3, 1)
                        act.wait_ge(s_ln3, g + 1)
                        alone(act)
                        for k in range(G):
                            nc.scalar.activation(xs[:, k, 0:D], xr[:, ds(g * G + k, 1), :].squeeze(1), ACT.Identity,
                                                 bias=ln["nmr"][:, k:k + 1], scale=ln["rstd"][:, k:k + 1]).then_inc(s_y, 1)
                        act.wait_ge(s_mx, g + 1)
                        nc.scalar.activation(gt["e"][:, :, :], gt["l"][:, :, :], ACT.Exp).then_inc(s_ex, 1)
                        for n in range(12):
                            m, (c0, c1) = n // 2, HALVES[n % 2]
                            act.wait_ge(s_h1, g * 12 + n + 1)
                            nc.scalar.activation(h1[:, m, c0:c1], psum[:, 4 + n % 4, 0:c1 - c0], ACT.Relu,
                                                 bias=b1[:, m:m + 1]).then_inc(s_h1c, 1)
                        act.wait_ge(s_df, g + 1)
                        nc.scalar.activation(g1["x"][:, :], g1["d"][:, :], ACT.Exp).then_inc(s_ex2, 1)
                        for n in range(6):
                            m, (c0, c1) = n // 2, HALVES[n % 2]
                            act.wait_ge(s_h2, g * 6 + n + 1)
                            nc.scalar.activation(h2[:, m, c0:c1], psum[:, 4 + n % 4, 0:c1 - c0], ACT.Relu,
                                                 bias=b2[:, m:m + 1]).then_inc(s_h2c, 1)

                @block.tensor
                def _(pe):
                    pe.wait_ge(s_w3, 16 * 18)
                    pe.wait_ge(s_c3, 8)
                    pe.sem_inc(s_x2, 1)
                    with pe.Fori(0, NG) as g:

                        def products(k):
                            pe.wait_ge(s_t1c, g * G + k + 1)
                            for c in range(4):
                                w = (w_self if c < 2 else w_neigh)[:, c % 2, :]
                                last = nc.tensor.matmul(psum[:, k // 2, k % 2 * D:(k % 2 + 1) * D], tT[:, k % 2, c, :], w,
                                                        start=c == 0, stop=c == 3)
                            last.then_inc(s_gnn, 1)

                        pe.wait_ge(s_x2, g * G + 1)
                        for k in range(G):
                            pe.wait_ge(s_a, g * G + k + 1)
                            if k >= 2:
                                pe.wait_ge(s_t1c, g * G + k - 1)
                            for c in range(4):
                                last = nc.tensor.transpose(psum[:, 4 + k % 2, c * P:(c + 1) * P], xs[:, k, c * P:(c + 1) * P], ident[:, :])
                            last.then_inc(s_t1, 1)
                            if k:
                                products(k - 1)
                        products(G - 1)
                        for k in range(G):
                            pe.wait_ge(s_y, g * G + k + 1)
                            if k >= 2:
                                pe.wait_ge(s_yT, g * G + k - 1)
                            for c in range(2):
                                last = nc.tensor.transpose(psum[:, 4 + k % 2, c * P:(c + 1) * P], xs[:, k, c * P:(c + 1) * P], ident[:, :])
                            last.then_inc(s_t2, 1)
                        pe.wait_ge(s_yT, g * G + G)
                        for k in range(G):
                            for c in range(2):
                                nc.tensor.matmul(psum[:, 6, k * 4:k * 4 + 4], yT[:, c, k * P:(k + 1) * P], gw[:, c, :],
                                                 start=c == 0, stop=False)
                            last = nc.tensor.matmul(psum[:, 6, k * 4:k * 4 + 4], ones[0:1, :], gb[:, :], start=False, stop=True)
                        last.then_inc(s_lg, 1)
                        for n in range(12):
                            m, (c0, c1) = n // 2, HALVES[n % 2]
                            if n >= 4:
                                pe.wait_ge(s_h1c, g * 12 + n - 3)
                            if n == 2:
                                pe.wait_ge(s_mx, g + 1)
                            for c in range(2):
                                last = nc.tensor.matmul(psum[:, 4 + n % 4, 0:c1 - c0], w1[:, c, m, :], yT[:, c, c0:c1],
                                                        start=c == 0, stop=c == 1)
                            last.then_inc(s_h1, 1)
                        for n in range(6):
                            m, (c0, c1) = n // 2, HALVES[n % 2]
                            pe.wait_ge(s_h1c, g * 12 + 12)
                            if n >= 4:
                                pe.wait_ge(s_h2c, g * 6 + n - 3)
                            for c in range(2):
                                if m == 0:
                                    last = nc.tensor.matmul(psum[:, 4 + n % 4, 0:c1 - c0], w2s[:, c, :], h1[:, c, c0:c1],
                                                            start=c == 0, stop=c == 1)
                                else:
                                    e = 2 * (m - 1) + c
                                    last = nc.tensor.matmul(psum[c * (P // 2):(c + 1) * (P // 2), 4 + n % 4, 0:c1 - c0],
                                                            w2e[:, e, :], h1[:, 2 + e, c0:c1], start=True, stop=True)
                            last.then_inc(s_h2, 1)
                        pe.wait_ge(s_cf, g + 1)
                        for n, (c0, c1) in enumerate(HALVES):
                            for k in range(c0 // P, c1 // P):
                                last = nc.tensor.transpose(psum[0:5, n, k * P - c0:(k + 1) * P - c0], cf[:, k, :], ident[:, :])
                            last.then_inc(s_cT, 1)
                        pe.wait_ge(s_cTc, g * 2 + 2)
                        for n in range(4):
                            q, (c0, c1) = n // 2, HALVES[n % 2]
                            nc.tensor.matmul(psum[:, n, 0:c1 - c0], pair[:, q, :], cfT[0:4, c0:c1], start=True, stop=True).then_inc(s_gbr, 1)
                        for k in range(G):
                            if k == 0:
                                pe.wait_ge(s_h2c, g * 6 + 6)
                            pe.wait_ge(s_h2g, g * 4 + (3 if k < 4 else 4))
                            if k >= 4:
                                pe.wait_ge(s_x2, g * G + k - 2)
                            for m in range(3):
                                nc.tensor.matmul(psum[:, 4 + k % 4, 0:D], h2[:, m, k * P:(k + 1) * P], w3[:, m, :], start=m == 0, stop=False)
                            nc.tensor.matmul(psum[:, 4 + k % 4, 0:D], cfT[:, k * P:(k + 1) * P], b3[:, :], start=False, stop=True).then_inc(s_y3, 1)

                @block.vector
                def _(dve):
                    dve.wait_ge(s_c3, 8)
                    nc.vector.tensor_copy(rev[:, :], rev_i[:, :]).then_inc(s_own3, 1)
                    with dve.Fori(0, NG) as g:
                        own = Chain(dve, s_own3, 1 + g * DENSE0_OWN)
                        for k in range(G):
                            dve.wait_ge(s_t1, g * G + k + 1)
                            if k >= 2:
                                dve.wait_ge(s_gnn, g * G + k - 1)
                            nc.vector.tensor_copy(tT[:, k % 2, :, :].rearrange("p c n -> p (c n)"), psum[:, 4 + k % 2, :]).then_inc(s_t1c, 1)
                        dve.wait_ge(s_nrm, g + 1)
                        own.add(nc.vector.tensor_scalar(nrm[:, :], nrm[:, :], 1e-12, None, ALU.max))
                        own.sync()
                        own.add(nc.vector.reciprocal(rn[:, :], nrm[:, :]))
                        own.sync()
                        for k in range(G):
                            x = xr[:, ds(g * G + k, 1), :].squeeze(1)
                            own.add(nc.vector.scalar_tensor_tensor(x, psum[:, k // 2, k % 2 * D:(k % 2 + 1) * D], rn[:, k:k + 1], x,
                                                                   ALU.mult, ALU.add))
                        own.sync()
                        normalise(dve, own, xr, g, ln, s_v3, s_sd3, s_ln3)
                        for k in range(G):
                            dve.wait_ge(s_t2, g * G + k + 2)
                            nc.vector.tensor_copy(yT[:, :, k * P:(k + 1) * P],
                                                  psum[:, 4 + k % 2, 0:2 * P].rearrange("p (c n) -> p c n", c=2)).then_inc(s_yT, 1)
                        dve.wait_ge(s_lg, g + 1)
                        logits = psum[:, 6, 0:4 * G].rearrange("p (k e) -> p k e", e=4)
                        own.add(nc.vector.tensor_reduce(g1["m"][:, :], logits, AX.X, ALU.max))
                        own.sync()
                        nc.vector.tensor_tensor(gt["l"][:, :, :], logits, wide(g1["m"], 4), ALU.subtract).then_inc(s_mx, 1)
                        dve.wait_ge(s_ex, g + 1)
                        own.add(nc.vector.tensor_reduce(g1["s"][:, :], gt["e"][:, :, :], AX.X, ALU.add))
                        own.sync()
                        own.add(nc.vector.reciprocal(g1["r"][:, :], g1["s"][:, :]))
                        own.sync()
                        own.add(nc.vector.tensor_tensor(gt["g"][:, :, :], gt["e"][:, :, :], wide(g1["r"], 4), ALU.mult))
                        own.sync()
                        top_two(own, gt, g1, rev, 4)
                        nc.vector.tensor_tensor(g1["d"][:, :], g1["v2"][:, :], g1["v1"][:, :], ALU.subtract).then_inc(s_df, 1)
                        dve.wait_ge(s_ex2, g + 1)
                        two_weights(own, g1)
                        own.add(nc.vector.tensor_tensor(gt["g2"][:, :, :], gt["o1"][:, :, :], wide(g1["w1"], 4), ALU.mult))
                        own.add(nc.vector.tensor_tensor(gt["e"][:, :, :], gt["o2"][:, :, :], wide(g1["w2"], 4), ALU.mult))
                        own.sync()
                        nc.vector.tensor_tensor(cf[:, :, 0:4], gt["g2"][:, :, :], gt["e"][:, :, :], ALU.add).then_inc(s_cf, 1)
                        for n, (c0, c1) in enumerate(HALVES):
                            dve.wait_ge(s_cT, g * 2 + n + 1)
                            nc.vector.tensor_copy(cfT[:, c0:c1], psum[0:5, n, 0:c1 - c0]).then_inc(s_cTc, 1)
                        for n in (0, 2, 1, 3):
                            q, (c0, c1) = n // 2, HALVES[n % 2]
                            dve.wait_ge(s_gbr, g * 4 + n + 1)
                            dve.wait_ge(s_h2c, g * 6 + 2 * (q + 1) + n % 2 + 1)
                            nc.vector.tensor_tensor(h2[:, 1 + q, c0:c1], h2[:, 1 + q, c0:c1], psum[:, n, 0:c1 - c0], ALU.mult).then_inc(s_h2g, 1)
                        for k in range(G):
                            dve.wait_ge(s_y3, g * G + k + 1)
                            x = xr[:, ds(g * G + k, 1), :].squeeze(1)
                            nc.vector.tensor_tensor(x, psum[:, 4 + k % 4, 0:D], x, ALU.add).then_inc(s_x2, 1)
                        assert own.n == DENSE0_OWN, own.n

        early.close()
        out1 = sb("out1", [P, NT, NX])
        out2 = sb("out2", [P, NT, NX])
        wt1 = sb("wt1", [P, NT])
        wt2 = sb("wt2", [P, NT])
        rstd4 = sb("rstd4", [P, NT])
        nmr4 = sb("nmr4", [P, NT])

        with ExitStack() as ph4:
            agg = sb("agg", [P, NB, EA + 1], f32, ph4)
            rcount = sb("rcount", [P, NB], f32, ph4)
            s_own4 = sem("later_vector_own")
            s_one = sem("l1_onehot_ready")
            s_prd = sem("l1_products")
            s_add = sem("l1_added")
            s_row4 = [sem(f"l1_rows_loaded{u}") for u in range(STEP4)]
            s_it4 = sem("l1_tiles_loaded")
            s_hi = sem("l1_first_part")
            s_r1 = sem("l1_remainder")
            s_mid = sem("l1_second_part")
            s_lo = sem("l1_third_part")
            with ExitStack() as ph5:
                items4 = sb("items4", [4, IJ * P], i32, ph5)
                tile_bi = sb("tile_bi", [P, IJ * P], i32, ph5)
                tile_b = sb("tile_b", [P, IJ * P], f32, ph5)
                rows4 = sb("rows4", [P, STEP4, RUN, ER], f32, ph5)
                parts = sb("parts", [P, RING, RUN, 3 * EA + 2], bf16, ph5)
                hot4 = sb("hot4", [P, RING, RUN, P], bf16, ph5)
                with nc.Block() as block:

                    @block.sync
                    def _(sp):
                        sp.dma_start(tile_bi[:, :], item_d[1:2, :].partition_broadcast(P).squeeze(1)).then_inc(s_it4, 16)
                        sp.dma_start(items4[:, :], item_d).then_inc(s_it4, 16)
                        sp.wait_ge(s_it4, 32)
                        with sp.Fori(0, NI4 // STEP4) as it:
                            for half in range(2):
                                runs = nc.values_load_multi_w_load_instructions(
                                    items4[3:4, ds(it * STEP4 + half * RING, RING)], [mybir.EngineType.SP], min_val=0, max_val=NC // RUN - 1,
                                    skip_runtime_bounds_check_because="a run's number is clamped to the last")[1]
                                for k in range(RING):
                                    u = half * RING + k
                                    sp.wait_ge(s_prd, it * STEP4 + u + 1)
                                    sp.dma_start(rows4[:, u, :, :], edges_d[ds(runs[k] * (P * RUN), P * RUN), :].rearrange(
                                        "(p c) f -> p c f", c=RUN)).then_inc(s_row4[u], 16)
                        for u in range(HALF4):
                            sp.wait_ge(s_prd, NI4 + u + 1)
                            sp.dma_start(rows4[:, u, :, :], edges_d[EP - P * RUN:EP, :].rearrange("(p c) f -> p c f", c=RUN)).then_inc(s_row4[u], 16)

                    def whole(u):
                        return rows4[:, u:u + 2, :, 0:EA]

                    def part(u, n):
                        c0 = (0, EA + 1, 2 * EA + 1)[n]
                        return parts[:, u % RING:u % RING + 2, :, c0:c0 + EA]

                    @block.scalar
                    def _(act):
                        def first(it, u):
                            for v in (u, u + 1):
                                act.wait_ge(s_row4[v], it * 16 + 16)
                            act.wait_ge(s_prd, STEP4 - RING + it * STEP4 + u + 2)
                            alone(act)
                            nc.scalar.activation(part(u, 0), whole(u), ACT.Copy).then_inc(s_hi, 1)

                        first(0, 0)
                        with act.Fori(0, NI4 // STEP4) as it:
                            for u in range(0, STEP4, 2):
                                if u + 2 < STEP4:
                                    first(it, u + 2)
                                else:
                                    first(it + 1, 0)
                                act.wait_ge(s_r1, it * (STEP4 // 2) + u // 2 + 1)
                                nc.scalar.activation(part(u, 1), whole(u), ACT.Copy).then_inc(s_mid, 1)

                    @block.gpsimd
                    def _(pool):
                        pool.memset(parts[:, :, :, EA:EA + 1], 1.0).then_inc(s_lo, 1)

                        def remainder(n, u):
                            pool.wait_ge(s_hi, n + 1)
                            alone(pool)
                            pool.tensor_tensor(whole(u), whole(u), part(u, 0), ALU.subtract).then_inc(s_r1, 1)

                        remainder(0, 0)
                        with pool.Fori(0, NI4 // STEP4) as it:
                            for u in range(0, STEP4, 2):
                                n = it * (STEP4 // 2) + u // 2
                                remainder(n + 1, (u + 2) % STEP4)
                                pool.wait_ge(s_mid, n + 1)
                                alone(pool)
                                pool.tensor_tensor(part(u, 2), whole(u), part(u, 1), ALU.subtract).then_inc(s_lo, 1)

                    @block.tensor
                    def _(pe):
                        pe.sem_inc(s_prd, STEP4)
                        with pe.Fori(0, NI4 // STEP4) as it:
                            for u in range(STEP4):
                                if u % 2 == 0:
                                    pe.wait_ge(s_lo, it * (STEP4 // 2) + u // 2 + 2)
                                pe.wait_ge(s_one, it * STEP4 + u + 1)
                                pe.wait_ge(s_add, it * STEP4 + u + 1)
                                for c in range(RUN):
                                    for n in ((1, 2, 0) if c == RUN - 1 else (0, 1, 2)):
                                        c0, width = ((0, EA + 1), (EA + 1, EA), (2 * EA + 1, EA))[n]
                                        last = nc.tensor.matmul(psum[:, u % RING, 0:width], hot4[:, u % RING, c, :],
                                                                parts[:, u % RING, c, c0:c0 + width],
                                                                start=c == 0 and n == 0, stop=c == RUN - 1 and n == 0)
                                last.then_inc(s_prd, 1)

                    @block.vector
                    def _(dve):
                        dve.sem_inc(s_add, RING)
                        own = Chain(dve, s_own4)
                        own.add(nc.vector.memset(agg[:, :, :], 0.0))
                        dve.wait_ge(s_it4, 32)
                        own.add(nc.vector.tensor_scalar(tile_b[:, :], tile_bi[:, :], float(P), None, ALU.mult))
                        own.sync()

                        def onehots(it, u):
                            dve.wait_ge(s_row4[u], it * 16 + 16)
                            dve.wait_ge(s_prd, STEP4 - RING + it * STEP4 + u + 1)
                            alone(dve)
                            nc.vector.scalar_tensor_tensor(
                                hot4[:, u % RING, :, :], iota_r[:, :].unsqueeze(1).to_broadcast([P, RUN, P]), tile_b[:, ds(it * STEP4 + u, 1)],
                                rows4[:, u, :, EA + 1:EA + 2].to_broadcast([P, RUN, P]), ALU.add, ALU.is_equal).then_inc(s_one, 1)

                        for u in range(HALF4):
                            onehots(0, u)
                        with dve.Fori(0, NI4 // STEP4) as it:
                            for quarter in range(4):
                                tiles = nc.values_load_multi_w_load_instructions(
                                    items4[1:2, ds(it * STEP4 + quarter * HALF4, HALF4)], [mybir.EngineType.DVE], min_val=0, max_val=NB - 1,
                                    skip_runtime_bounds_check_because="a tile's number is a count of at most NB - 1 buckets")[1]
                                for k in range(HALF4):
                                    u = quarter * HALF4 + k
                                    if quarter < 3:
                                        onehots(it, u + HALF4)
                                    else:
                                        onehots(it + 1, k)
                                for k in range(HALF4):
                                    u = quarter * HALF4 + k
                                    dve.wait_ge(s_prd, STEP4 + it * STEP4 + u + 1)
                                    dve.wait_ge(s_add, RING + it * STEP4 + u)
                                    there = agg[:, ds(tiles[k], 1), :].squeeze(1)
                                    nc.vector.tensor_tensor(there, there, psum[:, u % RING, 0:EA + 1], ALU.add).then_inc(s_add, 1)
                        dve.wait_ge(s_add, RING + NI4)
                        nc.vector.tensor_scalar(rcount[:, :], agg[:, :, EA], 1.0, None, ALU.max).then_inc(s_own4, 1)
                        dve.wait_ge(s_own4, own.n + 1)
                        nc.vector.reciprocal(rcount[:, :], rcount[:, :]).then_inc(s_own4, 1)

            with ExitStack() as ph6:
                gw1 = sb("gw1", [P, 2, 4, P], f32, ph6)
                gw1e = sb("gw1e", [EA, 4, P], f32, ph6)
                gw1u = sb("gw1u", [P, 4, P], f32, ph6)
                u0 = sb("u0", [P, 1], f32, ph6)
                gb1 = sb("gb1", [P, 4], f32, ph6)
                hbias = sb("hbias", [P, 4], f32, ph6)
                gw2 = sb("gw2", [P, 4, D], f32, ph6)
                gb2 = sb("gb2", [1, D], f32, ph6)
                fg = sb("fg", [P, 2, NX], f32, ph6)
                fbg = sb("fbg", [1, NX], f32, ph6)
                rev5 = sb("rev5", [P, NX], f32, ph6)
                rev5_i = sb("rev5_i", [P, NX], i32, ph6)
                xs5 = sb("xs5", [P, G, D + EA], f32, ph6)
                xs6 = sb("xs6", [P, G, D], f32, ph6)
                xT5 = sb("xT5", [P, 2, G * P], f32, ph6)
                aT5 = sb("aT5", [EA, G * P], f32, ph6)
                h5 = sb("h5", [P, 4, G * P], f32, ph6)
                yT5 = sb("yT5", [P, 2, G * P], f32, ph6)
                ln5, ln6 = ({n: sb(f"ln{m}_" + n, s, f32, ph6) for n, s in
                             (("stats", [P, G, 6]), ("mv", [P, G, 2]), ("sd", [P, G]), ("rstd", [P, G]), ("nmr", [P, G]), ("nil", [P, 4]))}
                            for m in (5, 6))
                gt5 = {n: sb("gt5_" + n, [P, G, NX], f32, ph6) for n in ("g", "eq", "sc", "o1", "g2", "eq2", "sc2", "o2")}
                g5 = {n: sb("g5_" + n, [P, G], f32, ph6) for n in ("v1", "k1", "v2", "k2", "d", "x", "t", "w1", "w2")}
                s_w5 = sem("l1_weights")
                s_c5 = sem("l1_constants")
                s_own5 = sem("l1_dense_vector_own")
                s_u5 = sem("l1_global_product")
                s_v5 = sem("l1_variance")
                s_sd5 = sem("l1_deviation")
                s_ln5 = sem("l1_rstd")
                s_a5 = sem("l1_normalised")
                s_t5 = sem("l1_transposed")
                s_tc5 = sem("l1_columns")
                s_h5 = sem("l1_hidden_products")
                s_hc5 = sem("l1_hidden")
                s_o5 = sem("l1_node_products")
                s_x3 = sem("l1_rows_done")
                s_v6 = sem("moe_variance")
                s_sd6 = sem("moe_deviation")
                s_ln6 = sem("moe_rstd")
                s_y6 = sem("moe_normalised")
                s_t6 = sem("moe_transposed")
                s_tc6 = sem("moe_columns")
                s_lg6 = sem("moe_logits")
                s_gl6 = sem("moe_logits_copied")
                s_df6 = sem("moe_gate_gap")
                s_ex6 = sem("moe_gate_ratio")
                with nc.Block() as block:

                    @block.sync
                    def _(sp):
                        with nc.allow_non_contiguous_dma(reason="a few hundred biases"):
                            for dst, src in (
                                (gw1[:, :, :, :], a["g_W1"][0:D, :].rearrange("(c p) (m n) -> p c m n", p=P, n=P)),
                                (gw1e[:, :, :], a["g_W1"][D:D + EA, :].rearrange("p (m n) -> p m n", n=P)),
                                (gw1u[:, :, :], a["g_W1"][D + EA:D + EA + P, :].rearrange("p (m n) -> p m n", n=P)),
                                (u0[:, :], a["g_u"][0, :].unsqueeze(1)),
                                (gb1[:, :], a["g_b1"].rearrange("(m p) -> p m", p=P)),
                                (gw2[:, :, :], a["g_W2"].rearrange("(m p) n -> p m n", p=P)),
                                (gb2[:, :], a["g_b2"].unsqueeze(0)),
                                (fg[:, :, :], a["f_Wg"].rearrange("(c p) e -> p c e", p=P)),
                                (fbg[:, :], a["f_bg"].unsqueeze(0)),
                            ):
                                sp.dma_start(dst, src).then_inc(s_w5, 16)
                        sp.wait_ge(s_w5, 16 * 9)

                    @block.gpsimd
                    def _(pool):
                        pool.iota(rev5_i[:, :], pattern=[[-1, NX]], base=NX, channel_multiplier=0).then_inc(s_c5, 1)

                    @block.scalar
                    def _(act):
                        act.wait_ge(s_w5, 16 * 9)

                        def deviation(ln, g, s_v, s_sd):
                            act.wait_ge(s_v, g + 1)
                            nc.scalar.activation(ln["sd"][:, :], ln["mv"][:, :, 1], ACT.Sqrt, bias=eps[:, :]).then_inc(s_sd, 1)

                        def node_rows(g):
                            act.wait_ge(s_ln5, g + 1)
                            alone(act)
                            for k in range(G):
                                t = g * G + k
                                nc.scalar.activation(xs5[:, k, 0:D], xr[:, ds(t, 1), :].squeeze(1), ACT.Identity,
                                                     bias=ln5["nmr"][:, k:k + 1], scale=ln5["rstd"][:, k:k + 1])
                                nc.scalar.activation(xs5[:, k, D:D + EA], agg[:, ds(t, 1), 0:EA].squeeze(1), ACT.Copy,
                                                     scale=rcount[:, ds(t, 1)]).then_inc(s_a5, 1)

                        def hidden(g, ns):
                            for n in ns:
                                m, (c0, c1) = n // 2, HALVES[n % 2]
                                act.wait_ge(s_h5, g * 8 + n + 1)
                                nc.scalar.activation(h5[:, m, c0:c1], psum[:, 4 + n % 4, 0:c1 - c0], ACT.Relu,
                                                     bias=hbias[:, m:m + 1]).then_inc(s_hc5, 1)

                        def gate_rows(g):
                            act.wait_ge(s_ln6, g + 1)
                            alone(act)
                            for k in range(G):
                                nc.scalar.activation(xs6[:, k, :], xr[:, ds(g * G + k, 1), :].squeeze(1), ACT.Identity,
                                                     bias=ln6["nmr"][:, k:k + 1], scale=ln6["rstd"][:, k:k + 1]).then_inc(s_y6, 1)

                        def ratio(g):
                            act.wait_ge(s_df6, g + 1)
                            nc.scalar.activation(g5["x"][:, :], g5["d"][:, :], ACT.Exp).then_inc(s_ex6, 1)

                        deviation(ln5, 0, s_v5, s_sd5)
                        node_rows(0)
                        deviation(ln5, 1, s_v5, s_sd5)
                        hidden(0, range(8))
                        act.wait_ge(s_t5, G)
                        node_rows(1)
                        with act.Fori(0, NG - 2) as i:
                            g = i + 1
                            deviation(ln6, g - 1, s_v6, s_sd6)
                            hidden(g, range(2))
                            deviation(ln5, g + 1, s_v5, s_sd5)
                            hidden(g, range(2, 4))
                            gate_rows(g - 1)
                            hidden(g, range(4, 8))
                            act.wait_ge(s_t5, g * G + G)
                            node_rows(g + 1)
                            ratio(g - 1)
                        deviation(ln6, NG - 2, s_v6, s_sd6)
                        hidden(NG - 1, range(4))
                        gate_rows(NG - 2)
                        hidden(NG - 1, range(4, 8))
                        ratio(NG - 2)
                        deviation(ln6, NG - 1, s_v6, s_sd6)
                        gate_rows(NG - 1)
                        ratio(NG - 1)

                    @block.tensor
                    def _(pe):
                        pe.wait_ge(s_w5, 16 * 9)
                        for m in range(4):
                            last = nc.tensor.matmul(psum[:, 0, m:m + 1], gw1u[:, m, :], u0[:, :], start=True, stop=True)
                        last.then_inc(s_u5, 1)

                        def hidden(g):
                            for k in range(G):
                                pe.wait_ge(s_a5, g * G + k + 1)
                                if k >= 2:
                                    pe.wait_ge(s_tc5, g * G + k - 1)
                                for c in range(2):
                                    nc.tensor.transpose(psum[:, k % 2, c * P:(c + 1) * P], xs5[:, k, c * P:(c + 1) * P], ident[:, :])
                                nc.tensor.transpose(psum[0:EA, k % 2, 2 * P:3 * P], xs5[:, k, D:D + EA], ident[:, :]).then_inc(s_t5, 1)
                            pe.wait_ge(s_tc5, g * G + G)
                            for n in range(8):
                                m, (c0, c1) = n // 2, HALVES[n % 2]
                                if n >= 4:
                                    pe.wait_ge(s_hc5, g * 8 + n - 3)
                                for c in range(2):
                                    nc.tensor.matmul(psum[:, 4 + n % 4, 0:c1 - c0], gw1[:, c, m, :], xT5[:, c, c0:c1], start=c == 0, stop=False)
                                nc.tensor.matmul(psum[:, 4 + n % 4, 0:c1 - c0], gw1e[:, m, :], aT5[:, c0:c1], start=False, stop=True).then_inc(s_h5, 1)

                        def nodes(g):
                            pe.wait_ge(s_hc5, g * 8 + 8)
                            for k in range(G):
                                if k >= 4:
                                    pe.wait_ge(s_x3, g * G + k - 3)
                                for m in range(4):
                                    nc.tensor.matmul(psum[:, 4 + k % 4, 0:D], h5[:, m, k * P:(k + 1) * P], gw2[:, m, :], start=m == 0, stop=False)
                                nc.tensor.matmul(psum[:, 4 + k % 4, 0:D], ones[0:1, :], gb2[:, :], start=False, stop=True).then_inc(s_o5, 1)

                        def gates(g):
                            for k in range(G):
                                pe.wait_ge(s_y6, g * G + k + 1)
                                if k >= 2:
                                    pe.wait_ge(s_tc6, g * G + k - 1)
                                for c in range(2):
                                    last = nc.tensor.transpose(psum[:, k % 2, c * P:(c + 1) * P], xs6[:, k, c * P:(c + 1) * P], ident[:, :])
                                last.then_inc(s_t6, 1)
                            pe.wait_ge(s_tc6, g * G + G)
                            pe.wait_ge(s_gl6, g + 1)
                            for k in range(G):
                                for c in range(2):
                                    nc.tensor.matmul(psum[:, 2, k * NX:(k + 1) * NX], yT5[:, c, k * P:(k + 1) * P], fg[:, c, :], start=c == 0, stop=False)
                                last = nc.tensor.matmul(psum[:, 2, k * NX:(k + 1) * NX], ones[0:1, :], fbg[:, :], start=False, stop=True)
                            last.then_inc(s_lg6, 1)

                        pe.wait_ge(s_gl6, 1)
                        hidden(0)
                        nodes(0)
                        with pe.Fori(0, NG - 1) as i:
                            pe.wait_ge(s_x3, i * G + G)
                            hidden(i + 1)
                            gates(i)
                            nodes(i + 1)
                        gates(NG - 1)

                    @block.vector
                    def _(dve):
                        own = Chain(dve, s_own5)
                        dve.wait_ge(s_c5, 1)
                        own.add(nc.vector.tensor_copy(rev5[:, :], rev5_i[:, :]))
                        dve.wait_ge(s_u5, 1)
                        nc.vector.tensor_tensor(hbias[:, :], psum[:, 0, 0:4], gb1[:, :], ALU.add).then_inc(s_gl6, 1)

                        def node_columns(g):
                            for k in range(G):
                                dve.wait_ge(s_t5, g * G + k + 1)
                                at = slice(k * P, (k + 1) * P)
                                nc.vector.tensor_copy(xT5[:, :, at], psum[:, k % 2, 0:2 * P].rearrange("p (c n) -> p c n", c=2))
                                nc.vector.tensor_copy(aT5[:, at], psum[0:EA, k % 2, 2 * P:3 * P]).then_inc(s_tc5, 1)

                        def node_sums(g):
                            for k in range(G):
                                dve.wait_ge(s_o5, g * G + k + 1)
                                x = xr[:, ds(g * G + k, 1), :].squeeze(1)
                                nc.vector.tensor_tensor(x, psum[:, 4 + k % 4, 0:D], x, ALU.add).then_inc(s_x3, 1)

                        def keep_rstd(own, g):
                            dve.wait_ge(s_ln6, g + 1)
                            own.add(nc.vector.tensor_copy(rstd4[:, ds(g * G, G)], ln6["rstd"][:, :]))
                            own.add(nc.vector.tensor_copy(nmr4[:, ds(g * G, G)], ln6["nmr"][:, :]))

                        def gate_columns(g):
                            for k in range(G):
                                dve.wait_ge(s_t6, g * G + k + 1)
                                nc.vector.tensor_copy(yT5[:, :, k * P:(k + 1) * P],
                                                      psum[:, k % 2, 0:2 * P].rearrange("p (c n) -> p c n", c=2)).then_inc(s_tc6, 1)

                        def gates(own, g):
                            dve.wait_ge(s_lg6, g + 1)
                            nc.vector.tensor_copy(gt5["g"][:, :, :], psum[:, 2, 0:NX * G].rearrange("p (k e) -> p k e", e=NX)).then_inc(s_gl6, 1)
                            dve.wait_ge(s_gl6, g + 2)
                            top_two(own, gt5, g5, rev5, NX)
                            nc.vector.tensor_tensor(g5["d"][:, :], g5["v2"][:, :], g5["v1"][:, :], ALU.subtract).then_inc(s_df6, 1)
                            dve.wait_ge(s_ex6, g + 1)
                            two_weights(own, g5)
                            for to, of in ((wt1, "w1"), (wt2, "w2")):
                                own.add(nc.vector.tensor_copy(to[:, ds(g * G, G)], g5[of][:, :]))
                            for to, of in ((out1, "o1"), (out2, "o2")):
                                own.add(nc.vector.tensor_copy(to[:, ds(g * G, G), :], gt5[of][:, :, :]))
                            own.sync()

                        own.sync()
                        normalise(dve, own, xr, 0, ln5, s_v5, s_sd5, s_ln5)
                        node_columns(0)
                        dve.wait_ge(s_a5, G)
                        normalise(dve, own, xr, 1, ln5, s_v5, s_sd5, s_ln5)
                        node_sums(0)
                        first = own.n
                        def step(own, g, ahead):
                            node_columns(g)
                            dve.wait_ge(s_x3, g * G)
                            normalise(dve, own, xr, g - 1, ln6, s_v6, s_sd6, s_ln6)
                            keep_rstd(own, g - 1)
                            if ahead:
                                dve.wait_ge(s_a5, g * G + G)
                                normalise(dve, own, xr, g + 1, ln5, s_v5, s_sd5, s_ln5)
                            gate_columns(g - 1)
                            gates(own, g - 1)
                            node_sums(g)

                        with dve.Fori(0, NG - 2) as i:
                            own = Chain(dve, s_own5, first + i * DENSE1_OWN)
                            step(own, i + 1, True)
                            assert own.n == DENSE1_OWN, own.n
                        own = Chain(dve, s_own5, first + (NG - 2) * DENSE1_OWN)
                        step(own, NG - 1, False)
                        dve.wait_ge(s_x3, NG * G)
                        normalise(dve, own, xr, NG - 1, ln6, s_v6, s_sd6, s_ln6)
                        keep_rstd(own, NG - 1)
                        gate_columns(NG - 1)
                        gates(own, NG - 1)

        with ExitStack() as ph7:
            place_i = sb("place_i", [P, 2, NT], i32, ph7)
            etab = sb("etab", [1, NBLK + 2], i32, ph7)
            weights = ph7.enter_context(ExitStack())
            fw1 = sb("fw1", [P, NX, 2, HX], f32, weights)
            fw2 = sb("fw2", [P, NX, HX // P, D], f32, weights)
            fb1 = sb("fb1", [P, NX, HX // P], f32, weights)
            fb2 = sb("fb2", [P, NX, D], f32, weights)
            s_w7 = sem("moe_weights")
            s_n7 = sem("moe_counts")
            s_o7 = sem("moe_offsets")
            s_pl7 = sem("moe_places")
            s_st7 = sem("moe_staged")
            s_id7 = sem("moe_place_copied")
            s_dp = [sem(f"moe_slot_moved{k}") for k in range(G)]
            with ExitStack() as ph8:
                st8 = sb("st8", [P, G, D], f32, ph8)
                id8 = sb("id8", [P, 2, G], i32, ph8)
                both = sb("both", [P, NT, NX], f32, ph8)
                pos8 = sb("pos8", [P, NT, NX], f32, ph8)
                pl8 = sb("pl8", [P, 2, NT], f32, ph8)
                cnt8 = sb("cnt8", [P, NX], f32, ph8)
                nb8_i = sb("nb8_i", [P, NX], i32, ph8)
                nb8s = sb("nb8s", [P, NX], i32, ph8)
                nb8 = sb("nb8", [P, NX], f32, ph8)
                end8 = sb("end8", [P, NX], f32, ph8)
                bas8 = sb("bas8", [P, NX], f32, ph8)
                blk_f = sb("blk_f", [1, NBLK + 2], f32, ph8)
                ge8 = sb("ge8", [1, NBLK + 2, NX - 1], f32, ph8)
                with nc.Block() as block:

                    @block.sync
                    def _(sp):
                        for e in range(NX):
                            sp.dma_start(fw1[:, e, :, :], a["f_W1"][e].rearrange("(c p) n -> p c n", p=P)).then_inc(s_w7, 16)
                        for e in range(NX):
                            sp.dma_start(fw2[:, e, :, :], a["f_W2"][e].rearrange("(m p) n -> p m n", p=P)).then_inc(s_w7, 16)
                        with nc.allow_non_contiguous_dma(reason="the experts' biases by hidden unit"):
                            sp.dma_start(fb1[:, :, :], a["f_b1"].rearrange("e (m p) -> p e m", p=P)).then_inc(s_w7, 16)
                        sp.dma_start(fb2[:, :, :], a["f_b2"].partition_broadcast(P)).then_inc(s_w7, 16)
                        sp.wait_ge(s_w7, 16 * (2 * NX + 2))

                    @block.vector
                    def _(dve):
                        own = Chain(dve, s_own4, 4)
                        own.add(nc.vector.tensor_tensor(both[:, :, :], out1[:, :, :], out2[:, :, :], ALU.add))
                        dve.wait_ge(s_pl7, 1)
                        own.add(nc.vector.tensor_copy(blk_f[:, :], etab[:, :]))
                        own.sync()
                        nc.vector.tensor_reduce(cnt8[:, :], both[:, :, :].rearrange("p t e -> p e t"), AX.X, ALU.add).then_inc(s_n7, 1)
                        dve.wait_ge(s_o7, 1)
                        own.add(nc.vector.tensor_scalar(nb8_i[:, :], psum[:, 0, 0:NX], float(P - 1), None, ALU.add))
                        own.sync()
                        own.add(nc.vector.tensor_scalar(nb8s[:, :], nb8_i[:, :], 7, None, ALU.arith_shift_right))
                        own.sync()
                        own.add(nc.vector.tensor_copy(nb8[:, :], nb8s[:, :]))
                        own.sync()
                        own.add(nc.vector.tensor_tensor_scan(end8[:, :], nb8[:, :], nb8[:, :], 0.0, ALU.add, ALU.bypass))
                        own.sync()
                        own.add(nc.vector.tensor_tensor(bas8[:, :], end8[:, :], nb8[:, :], ALU.subtract))
                        own.sync()
                        own.add(nc.vector.tensor_scalar(bas8[:, :], bas8[:, :], float(P), -1.0, ALU.mult, ALU.add))
                        own.sync()
                        own.add(nc.vector.tensor_tensor(bas8[:, :], bas8[:, :], psum[:, 0, NX:2 * NX], ALU.add))
                        own.sync()
                        for e in range(NX):
                            own.add(nc.vector.tensor_tensor_scan(pos8[:, :, e], both[:, :, e], both[:, :, e], bas8[:, e:e + 1], ALU.add, ALU.bypass))
                        own.sync()
                        for n, o in enumerate((out1, out2)):
                            own.add(nc.vector.tensor_tensor(both[:, :, :], o[:, :, :], pos8[:, :, :], ALU.mult))
                            own.sync()
                            own.add(nc.vector.tensor_reduce(pl8[:, n, :], both[:, :, :], AX.X, ALU.add))
                            own.sync()
                        nc.vector.tensor_copy(place_i[:, :, :], pl8[:, :, :]).then_inc(s_pl7, 1)
                        own.add(nc.vector.tensor_tensor(ge8[:, :, :], end8[0:1, 0:NX - 1].unsqueeze(1).to_broadcast([1, NBLK + 2, NX - 1]),
                                                        blk_f[:, :].unsqueeze(2).to_broadcast([1, NBLK + 2, NX - 1]), ALU.is_le))
                        own.sync()
                        own.add(nc.vector.tensor_reduce(blk_f[:, :], ge8[:, :, :], AX.X, ALU.add))
                        own.sync()
                        own.add(nc.vector.tensor_copy(etab[:, :], blk_f[:, :]))
                        own.sync()

                    @block.tensor
                    def _(pe):
                        pe.wait_ge(s_n7, 1)
                        nc.tensor.matmul(psum[:, 0, 0:NX], ones[:, :], cnt8[:, :], start=True, stop=True)
                        nc.tensor.matmul(psum[:, 0, NX:2 * NX], upper[:, :], cnt8[:, :], start=True, stop=True).then_inc(s_o7, 1)

                    @block.scalar
                    def _(act):
                        def stage(t, k):
                            nc.scalar.activation(st8[:, k, :], xr[:, ds(t, 1), :].squeeze(1), ACT.Identity,
                                                 bias=nmr4[:, ds(t, 1)], scale=rstd4[:, ds(t, 1)]).then_inc(s_st7, 1)

                        for k in range(G):
                            stage(k, k)
                        with act.Fori(0, NG - 1) as g:
                            for k in range(G):
                                act.wait_ge(s_dp[k], g * 32 + 32)
                                alone(act)
                                stage(g * G + G + k, k)

                    @block.gpsimd
                    def _(pool):
                        pool.iota(etab[:, :], pattern=[[1, NBLK + 2]], base=0, channel_multiplier=0).then_inc(s_pl7, 1)
                        pool.wait_ge(s_pl7, 2)

                        def dispatch(g):
                            pool.wait_ge(s_id7, g + 1)
                            for k in range(G):
                                pool.wait_ge(s_st7, g * G + k + 1)
                                alone(pool)
                                for n in range(2):
                                    pool.indirect_dma_start(
                                        out=xd_d, out_offset=bass.IndirectOffsetOnAxis(ap=id8[:, n, k:k + 1], axis=0),
                                        in_=st8[:, k, :], in_offset=None).then_inc(s_dp[k], 16)

                        pool.tensor_copy(id8[:, :, :], place_i[:, :, 0:G]).then_inc(s_id7, 1)
                        with pool.Fori(0, NG - 1) as g:
                            dispatch(g)
                            for k in range(G):
                                pool.wait_ge(s_dp[k], g * 32 + 32)
                            alone(pool)
                            pool.tensor_copy(id8[:, :, :], place_i[:, :, ds(g * G + G, G)]).then_inc(s_id7, 1)
                        dispatch(NG - 1)
                        for k in range(G):
                            pool.wait_ge(s_dp[k], NG * 32)

            with ExitStack() as ph9:
                xb = sb("xb", [P, 2, D], f32, ph9)
                xbT = sb("xbT", [P, 2, 2, P], f32, ph9)
                hs = sb("hs", [P, HX], f32, ph9)
                hT = sb("hT", [P, HX // P, P], f32, ph9)
                yb = sb("yb", [P, 2, D], f32, ph9)
                s_in = [sem(f"block_loaded{u}") for u in range(2)]
                s_xt = sem("block_transposed")
                s_xc = sem("block_columns")
                s_m1 = sem("block_hidden_products")
                s_hsa = sem("block_hidden_half_a")
                s_hsd = sem("block_hidden_half_d")
                s_ht = sem("block_hidden_transposed")
                s_hta = sem("block_relu_a")
                s_htd = sem("block_relu_d")
                s_m2 = sem("block_products")
                s_yb = sem("block_rows")
                s_yo = [sem(f"block_stored{u}") for u in range(2)]
                M = HX // P
                with nc.Block() as block:

                    @block.sync
                    def _(sp):
                        for u in range(2):
                            sp.dma_start(xb[:, u, :], xd_d[u * P:(u + 1) * P, :]).then_inc(s_in[u], 16)
                        with sp.Fori(0, NBLK // 2) as it:
                            for u in range(2):
                                sp.wait_ge(s_xt, it * 2 + u + 1)
                                sp.dma_start(xb[:, u, :], xd_d[ds(it * (2 * P) + (u + 2) * P, P), :]).then_inc(s_in[u], 16)

                    @block.tensor
                    def _(pe):
                        def transpose_x(j, u, n):
                            pe.wait_ge(s_in[u], n)
                            if not isinstance(j, int) or j > 0:
                                pe.wait_ge(s_xc, j)
                            for c in range(2):
                                last = nc.tensor.transpose(psum[:, 0, c * P:(c + 1) * P], xb[:, u, c * P:(c + 1) * P], ident[:, :])
                            last.then_inc(s_xt, 1)

                        def hidden(j, u, e):
                            pe.wait_ge(s_xc, j + 1)
                            for half in range(2):
                                for c in range(2):
                                    last = nc.tensor.matmul(psum[:, 1 + half, :], xbT[:, u, c, :],
                                                            fw1[:, ds(e, 1), c, half * 512:(half + 1) * 512].squeeze(1), start=c == 0, stop=c == 1)
                                last.then_inc(s_m1, 1)

                        def expert(j):
                            return pe.value_load(etab[0:1, ds(j, 1)], min_val=0, max_val=NX - 1)

                        transpose_x(0, 0, 16)
                        transpose_x(1, 1, 16)
                        e0 = expert(0)
                        hidden(0, 0, e0)
                        pe.sem_inc(s_yb, 1)
                        with pe.Fori(0, NBLK // 2) as it:
                            for u in range(2):
                                j = it * 2 + u
                                pe.wait_ge(s_hsa, j + 1)
                                pe.wait_ge(s_hsd, j + 1)
                                for m in range(M):
                                    last = nc.tensor.transpose(psum[:, 3 + m // 4, m % 4 * P:(m % 4 + 1) * P], hs[:, m * P:(m + 1) * P], ident[:, :])
                                    if m % 4 == 3:
                                        last.then_inc(s_ht, 1)
                                transpose_x(j + 2, u, it * 16 + 32)
                                nxt = expert(j + 1)
                                hidden(j + 1, 1 - u, nxt)
                                now = expert(j)
                                pe.wait_ge(s_hta, j * 4 + 4)
                                pe.wait_ge(s_htd, j * 4 + 4)
                                pe.wait_ge(s_yb, j + 1)
                                for m in range(M):
                                    last = nc.tensor.matmul(psum[:, 5, 0:D], hT[:, m, :], fw2[:, ds(now, 1), m, :].squeeze(1), start=m == 0, stop=m == M - 1)
                                last.then_inc(s_m2, 1)

                    @block.scalar
                    def _(act):
                        def copy_hidden(j):
                            act.wait_ge(s_m1, 2 * j + 1)
                            nc.scalar.activation(hs[:, 0:512], psum[:, 1, :], ACT.Copy).then_inc(s_hsa, 1)

                        copy_hidden(0)
                        act.sem_inc(s_m2, 1)
                        with act.Fori(0, NBLK // 2) as it:
                            for u in range(2):
                                j = it * 2 + u
                                e = act.value_load(etab[0:1, ds(j, 1)], min_val=0, max_val=NX - 1)
                                act.wait_ge(s_ht, 2 * j + 1)
                                act.wait_ge(s_m2, j + 1)
                                alone(act)
                                for m in range(4):
                                    nc.scalar.activation(hT[:, m, :], psum[:, 3, m * P:(m + 1) * P], ACT.Relu,
                                                         bias=fb1[:, ds(e, 1), m]).then_inc(s_hta, 1)
                                act.wait_ge(s_ht, 2 * j + 2)
                                copy_hidden(j + 1)
                                act.wait_ge(s_yb, j + 2)
                                act.dma_start(yd_d[ds(it * (2 * P) + u * P, P), :], yb[:, u, :]).then_inc(s_yo[u], 16)
                        for u in range(2):
                            act.wait_ge(s_yo[u], 16 * (NBLK // 2) + 1)

                    @block.vector
                    def _(dve):
                        def columns(j, u):
                            dve.wait_ge(s_xt, j + 1)
                            nc.vector.tensor_copy(xbT[:, u, :, :].rearrange("p c n -> p (c n)"), psum[:, 0, 0:2 * P]).then_inc(s_xc, 1)

                        def copy_hidden(j):
                            dve.wait_ge(s_m1, 2 * j + 2)
                            nc.vector.tensor_copy(hs[:, 512:1024], psum[:, 2, :]).then_inc(s_hsd, 1)

                        columns(0, 0)
                        columns(1, 1)
                        copy_hidden(0)
                        for u in range(2):
                            dve.sem_inc(s_yo[u], 1)
                        with dve.Fori(0, NBLK // 2) as it:
                            for u in range(2):
                                j = it * 2 + u
                                e = dve.value_load(etab[0:1, ds(j, 1)], min_val=0, max_val=NX - 1)
                                dve.wait_ge(s_ht, 2 * j + 2)
                                dve.wait_ge(s_m2, j + 1)
                                alone(dve)
                                for m in range(4, M):
                                    nc.vector.tensor_scalar(hT[:, m, :], psum[:, 4, (m - 4) * P:(m - 3) * P], fb1[:, ds(e, 1), m], 0.0,
                                                            ALU.add, ALU.max).then_inc(s_htd, 1)
                                columns(j + 2, u)
                                copy_hidden(j + 1)
                                dve.wait_ge(s_m2, j + 2)
                                dve.wait_ge(s_yo[u], it * 16 + 1)
                                nc.vector.tensor_tensor(yb[:, u, :], psum[:, 5, 0:D], fb2[:, ds(e, 1), :].squeeze(1), ALU.add).then_inc(s_yb, 1)

            weights.close()
            with ExitStack() as ph10:
                yg = sb("yg", [P, G, 2, D], f32, ph10)
                id10 = sb("id10", [P, 2, G], i32, ph10)
                fin = sb("fin", [P, G, D], f32, ph10)
                s_p1 = sem("first_result_added")
                s_fin = sem("rows_finished")
                s_out = sem("rows_stored_out")
                s_out2 = sem("last_rows_stored_out")
                with nc.Block() as block:

                    @block.gpsimd
                    def _(pool):
                        pool.sem_inc(s_fin, 1)
                        with pool.Fori(0, NG) as g:
                            pool.wait_ge(s_fin, g * G + 1)
                            alone(pool)
                            pool.tensor_copy(id10[:, :, :], place_i[:, :, ds(g * G, G)]).then_inc(s_id7, 1)
                            pool.wait_ge(s_id7, NG + g + 1)
                            alone(pool)
                            for k in range(G):
                                for n in range(2):
                                    pool.indirect_dma_start(
                                        out=yg[:, k, n, :], out_offset=None, in_=yd_d,
                                        in_offset=bass.IndirectOffsetOnAxis(ap=id10[:, n, k:k + 1], axis=0)).then_inc(s_dp[k], 16)

                    @block.vector
                    def _(dve):
                        dve.sem_inc(s_out, 1)
                        with dve.Fori(0, NG) as g:
                            dve.wait_ge(s_out, g * 16 + 1)
                            for k in range(G):
                                t = g * G + k
                                dve.wait_ge(s_dp[k], DISPATCHED + g * 32 + 32)
                                alone(dve)
                                nc.vector.scalar_tensor_tensor(fin[:, k, :], yg[:, k, 0, :], wt1[:, ds(t, 1)], xr[:, ds(t, 1), :].squeeze(1),
                                                               ALU.mult, ALU.add).then_inc(s_p1, 1)
                                dve.wait_ge(s_p1, t + 1)
                                alone(dve)
                                nc.vector.scalar_tensor_tensor(fin[:, k, :], yg[:, k, 1, :], wt2[:, ds(t, 1)], fin[:, k, :],
                                                               ALU.mult, ALU.add).then_inc(s_fin, 1)

                    @block.sync
                    def _(sp):
                        y = out["y"]
                        with sp.Fori(0, NG - 1) as g:
                            sp.wait_ge(s_fin, g * G + G + 1)
                            sp.dma_start(y[ds(g * (G * P), G * P), :].rearrange("(t p) d -> p t d", p=P), fin[:, :, :]).then_inc(s_out, 16)
                        sp.wait_ge(s_fin, NT + 1)
                        first = (NG - 1) * G * P
                        sp.dma_start(y[first:first + (G - 1) * P, :].rearrange("(t p) d -> p t d", p=P), fin[:, 0:G - 1, :]).then_inc(s_out2, 16)
                        sp.dma_start(y[first + (G - 1) * P:N, :], fin[0:N - first - (G - 1) * P, G - 1, :]).then_inc(s_out2, 16)
                        sp.wait_ge(s_out, 16 * (NG - 1) + 1)
                        sp.wait_ge(s_out2, 32)


def kernel(**inputs):
    import numpy as _np
    import concourse.bacc as _bacc
    from concourse import mybir as _mybir
    from concourse.bass_utils import run_bass_kernel_spmd as _run

    given = {name: _np.asarray(v) for name, v in inputs.items()}
    arrays = {
        "x": _np.pad(given["x"], ((0, NP - N), (0, 0))),
        "src": _np.pad(given["src"], (0, EP - E), constant_values=PAD_KEY),
        "dst": _np.pad(given["dst"], (0, EP - E), constant_values=PAD_KEY),
        "w": _np.pad(given["edge_weight"], (0, EP - E)),
        "attr": _np.pad(given["edge_attr_64"], ((0, EP - E), (0, 0))),
        "w_self": given["L0_gnn_w_self"].transpose(1, 0),
        "w_neigh": given["L0_gnn_w_neigh"].transpose(1, 0),
        "f_Wg": given["L1_ffn_Wg"].transpose(1, 0),
        "f_W1": given["L1_ffn_W1"].transpose(0, 2, 1),
        "f_W2": given["L1_ffn_W2"].transpose(0, 2, 1),
    }
    for name in ("sW1", "sb1", "sW2", "sb2", "sW3", "sb3", "eW1", "eb1", "eW2", "eb2", "eW3", "eb3", "gW", "gb"):
        arrays[name] = given["L0_ffn_" + name]
    for name in ("u", "W1", "b1", "W2", "b2"):
        arrays["g_" + name] = given["L1_gnn_" + name]
    for name in ("bg", "b1", "b2"):
        arrays["f_" + name] = given["L1_ffn_" + name]

    nc = _bacc.Bacc("TRN2", target_bir_lowering=False, num_devices=1)
    laid, aps = {}, {}
    for name, v in arrays.items():
        v = _np.ascontiguousarray(v)
        laid[f"in_{name}_dram"] = v
        aps[name] = nc.dram_tensor(f"in_{name}_dram", v.shape, _mybir.dt.from_np(v.dtype), kind="ExternalInput").ap()
    y = nc.dram_tensor("out_y_dram", (N, D), _mybir.dt.from_np(_np.dtype("float32")), kind="ExternalOutput").ap()
    build(nc, aps, {"y": y})
    r = _run(nc, [laid], core_ids=[0])
    return r.results[0]["out_y_dram"]
```

```python
import concourse.bass as bass
from concourse import mybir
from contextlib import ExitStack

P = 128
D = 256
N = 6250
NT = -(-N // P)
NP = NT * P
G = 7
NG = NT // G
E = 100000
RUN = 4
NC = -(-E // (P * RUN)) * RUN
EP = NC * P
PAD_KEY = NP
NB = NT + 1
STEP = 16
NI = -(-(-(-E // P) + NT - 1) // STEP) * STEP
STEP4 = 16
LO_DVE = (4, 10)
HALF4 = 4
NI4 = -(-(-(-E // (P * RUN)) + NT - 1) // STEP4) * STEP4
IJ = -(-NI // P)
EA = 64
ER = EA + 2
RING = 8
NX = 8
HX = 1024
NBLK = (2 * NP + NX * (P - 1)) // P
NBLK += NBLK % 2
SPARE = NBLK + 2 - 2 * NP // P
CAP = NP + P
DISPATCHED = 32 * NG
FIN0 = G + 1
assert NG % 2 == 1
LN_EPS = 1e-5

f32 = mybir.dt.float32
i32 = mybir.dt.int32
bf16 = mybir.dt.bfloat16
ALU = mybir.AluOpType
ACT = mybir.ActivationFunctionType
AX = mybir.AxisListType
ds = bass.ds


class Chain:

    def __init__(self, engine, sem, base=0):
        self.engine, self.sem, self.base, self.n = engine, sem, base, 0

    def add(self, instruction):
        self.n += 1
        instruction.then_inc(self.sem, 1)

    def sync(self):
        self.engine.wait_ge(self.sem, self.base + self.n)


def wide(v, n):
    return v[:, :].unsqueeze(2).to_broadcast([P, G, n])


LN_OWN = 2 * G + 2
DENSE0_OWN = 59
XN_PARTS = (range(0, 4), range(4, G))
assert NB % 5 == 0
DENSE1_OWN = 47
HALVES = ((0, 4 * P), (4 * P, G * P))
SC = 28
assert NC % (2 * SC) == 0


def build(nc, a, out):
    ctx = ExitStack()

    def sb(name, shape, dt=f32, scope=None):
        return (scope or ctx).enter_context(nc.sbuf_tensor(name, shape, dt))

    def sem(name):
        return ctx.enter_context(nc.semaphore(name))

    def dram(name, shape, dt=f32):
        return nc.dram_tensor(name, shape, dt, kind="Internal").ap()

    with ctx:
        xn_d = dram("xn_rows", [NP, D])
        edges_d = dram("sorted_edges", [EP, ER])
        item_d = dram("item_rows", [4, IJ * P], i32)
        xd_d = dram("dispatched", [NX * CAP + SPARE * P, D])
        hx_d = dram("hidden_parts", [NG * P, 4 * G * P])
        yd_d = dram("expert_rows", [NBLK * P, D])
        psum = ctx.enter_context(nc.psum_tensor("psum", [P, 8, 512], f32))

        ident = sb("ident", [P, P])
        iota_r = sb("iota_r", [P, P])
        upper = sb("upper", [P, P])
        ones = sb("ones", [P, P])
        xr = sb("xr", [P, NT, D])
        rstd = sb("rstd", [P, NT])
        nmr = sb("nmr", [P, NT])
        sd = sb("sd", [P, G])
        eps = sb("eps", [P, 1])
        early = ctx.enter_context(ExitStack())
        pos_i = sb("pos_i", [P, NC], i32, early)
        acc = sb("acc", [P, NB, D], f32, early)

        s_const = sem("constants")
        s_x = sem("x_loaded")
        s_dst = sem("dst_loaded")
        s_src = sem("src_loaded")
        s_own = sem("vector_own")
        s_sgn = sem("source_counts")
        s_var = sem("variance_ready")
        s_sd = sem("deviation_ready")
        s_ln = sem("rstd_ready")
        s_xn = sem("xn_ready")
        s_xst = [sem(f"xn_stored{h}") for h in range(2)]
        s_cum = sem("counts_ready")
        s_off = sem("offsets_in_psum")
        s_tab = sem("tables_ready")
        s_tabT = sem("tables_transposed")
        s_row = sem("rows_ready")
        s_rst = sem("item_tables_moved")
        s_cidx = sem("chunk_indices")
        s_pg = sem("item_rows_gathered")
        s_pf = sem("item_rows_ready")
        s_pt = sem("item_rows_transposed")
        s_pe = sem("item_columns_ready")
        s_z = sem("zero_ready")
        s_xdz = sem("dispatch_zeroed")

        s_turn = sem("turns")

        def alone(engine):
            engine.sem_inc(s_turn, 1)

        def normalise(dve, own, x, g, ln, s_var, s_sd, s_rstd):
            nc.vector.memset(ln["nil"][:, 2:3], 0.0)
            for k in range(G):
                own.add(nc.vector.bn_stats(ln["stats"][:, k, :], x[:, ds(g * G + k, 1), :].squeeze(1)))
            own.sync()
            nc.vector.memset(ln["nil"][:, 0:1], 0.0)
            for k in range(G):
                own.add(nc.vector.bn_aggr(ln["mv"][:, k, :], ln["stats"][:, k, :]))
            own.sync()
            nc.vector.memset(ln["nil"][:, 1:2], 0.0).then_inc(s_var, 1)
            dve.wait_ge(s_sd, g + 1)
            own.add(nc.vector.reciprocal(ln["rstd"][:, :], ln["sd"][:, :]))
            own.sync()
            nc.vector.scalar_tensor_tensor(ln["nmr"][:, :], ln["mv"][:, :, 0], -1.0, ln["rstd"][:, :],
                                           ALU.mult, ALU.mult).then_inc(s_rstd, 1)

        def top_two(own, gt, g1, rev, n):
            for v, o, eq, sc, key, src in (("v1", "o1", "eq", "sc", "k1", "g"), ("v2", "o2", "eq2", "sc2", "k2", "g2")):
                if src == "g2":
                    own.add(nc.vector.scalar_tensor_tensor(gt["g2"][:, :, :], gt["o1"][:, :, :], -1e30, gt["g"][:, :, :], ALU.mult, ALU.add))
                    own.sync()
                own.add(nc.vector.tensor_reduce(g1[v][:, :], gt[src][:, :, :], AX.X, ALU.max))
                own.sync()
                own.add(nc.vector.tensor_tensor(gt[eq][:, :, :], gt[src][:, :, :], wide(g1[v], n), ALU.is_equal))
                own.sync()
                own.add(nc.vector.tensor_tensor(gt[sc][:, :, :], gt[eq][:, :, :], rev[:, 0:n].unsqueeze(1).to_broadcast([P, G, n]), ALU.mult))
                own.sync()
                own.add(nc.vector.tensor_reduce(g1[key][:, :], gt[sc][:, :, :], AX.X, ALU.max))
                own.sync()
                own.add(nc.vector.tensor_tensor(gt[o][:, :, :], gt[sc][:, :, :], wide(g1[key], n), ALU.is_equal))
                own.sync()

        def two_weights(own, g1):
            own.add(nc.vector.tensor_scalar(g1["t"][:, :], g1["x"][:, :], 1.0, None, ALU.add))
            own.sync()
            own.add(nc.vector.reciprocal(g1["w1"][:, :], g1["t"][:, :]))
            own.sync()
            own.add(nc.vector.tensor_tensor(g1["w2"][:, :], g1["x"][:, :], g1["w1"][:, :], ALU.mult))
            own.sync()

        with ExitStack() as ph:
            items = sb("items", [4, IJ * P], i32, ph)
            it_src = sb("it_src", [P, IJ * P], i32, ph)
            it_rel = sb("it_rel", [P, IJ * P], f32, ph)
            it_w = sb("it_w", [P, IJ * P], f32, ph)
            kb = sb("kb", [P, NC], f32, ph)
            base = sb("base", [P, NB + 2], f32, ph)
            bnum = sb("bnum", [P, NB + 2], f32, ph)
            with ExitStack() as ph1:
                iota_i = sb("iota_i", [P, P], i32, ph1)
                dst_i = sb("dst_i", [P, NC], i32, ph1)
                src_i = sb("src_i", [P, NC], i32, ph1)
                dst_f = sb("dst_f", [P, NC], f32, ph1)
                src_f = sb("src_f", [P, NC], f32, ph1)
                junk = sb("junk", [P, NC], f32, ph1)
                junk2 = sb("junk2", [P, NC], f32, ph1)
                nil = sb("nil", [P, 4], f32, ph1)
                thr = sb("thr", [P, NB], f32, ph1)
                thr_h = sb("thr_h", [P, NB], f32, ph1)
                thr_i = sb("thr_i", [P, NB + 2], i32, ph1)
                item_i = sb("item_i", [P, IJ], i32, ph1)
                item_f = sb("item_f", [P, IJ], f32, ph1)
                cum = sb("cum", [P, 2, NB + 1], f32, ph1)
                cnt = sb("cnt", [P, NB], f32, ph1)
                starts = sb("starts", [P, 2, NB + 1], f32, ph1)
                st_i = sb("st_i", [P, 2, NB + 1], i32, ph1)
                up_i = sb("up_i", [P, 2, NB + 1], i32, ph1)
                c0_i = sb("c0_i", [P, 2, NB + 1], i32, ph1)
                c1_i = sb("c1_i", [P, 2, NB + 1], i32, ph1)
                ni = sb("ni", [P, 2, NB], f32, ph1)
                nz = sb("nz", [P, 2, NB], f32, ph1)
                iend = sb("iend", [P, 2, NB], f32, ph1)
                dif = sb("dif", [P, 2, NB], f32, ph1)
                ddif = sb("ddif", [P, 2, NT], f32, ph1)
                geq = sb("geq", [P, IJ, NT], f32, ph1)
                prod = sb("prod", [P, IJ, NT], f32, ph1)
                tab = sb("tab", [P, 4, IJ], f32, ph1)
                cidx = sb("cidx", [P, IJ], i32, ph1)
                tabT = sb("tabT", [4 * IJ, P], i32, ph1)
                t128 = sb("t128", [P, IJ], f32, ph1)
                row_i = sb("row_i", [P, IJ, 2, P], i32, ph1)
                row_w = sb("row_w", [P, IJ, P], f32, ph1)
                row_f = sb("row_f", [P, IJ, 2, P], f32, ph1)
                stats = sb("stats", [P, G, 6], f32, ph1)
                mv = sb("mv", [P, G, 2], f32, ph1)
                xn_st = sb("xn_st", [P, G, D], f32, ph1)
                zero = sb("zero", [P, D], f32, ph1)

                with nc.Block() as block:

                    @block.sync
                    def _(sp):
                        sp.dma_start(dst_i[:, :], a["dst"].rearrange("(p c) -> p c", p=P)).then_inc(s_dst, 16)
                        sp.dma_start(src_i[:, :], a["src"].rearrange("(p c) -> p c", p=P)).then_inc(s_src, 16)
                        sp.dma_start(xr[:, :, :], a["x"].rearrange("(t p) d -> p t d", p=P)).then_inc(s_x, 16)
                        sp.wait_ge(s_row, 1)
                        sp.dma_start(item_d.rearrange("k (j p) -> (k j) p", p=P), tabT[:, :]).then_inc(s_rst, 16)
                        sp.wait_ge(s_rst, 16)
                        sp.dma_start(items[:, :], item_d).then_inc(s_rst, 16)
                        with sp.Fori(0, NG) as g:
                            for h, tiles in enumerate(XN_PARTS):
                                sp.wait_ge(s_xn, g * G + tiles[-1] + 1)
                                sp.dma_start(
                                    xn_d[ds(g * (G * P) + tiles[0] * P, len(tiles) * P), :].rearrange("(t p) d -> p t d", p=P),
                                    xn_st[:, tiles[0]:tiles[-1] + 1, :]).then_inc(s_xst[h], 16)
                        for h in range(2):
                            sp.wait_ge(s_xst[h], 16 * NG + 1)
                        sp.wait_ge(s_rst, 32)

                    @block.gpsimd
                    def _(pool):
                        own = Chain(pool, s_const)
                        own.add(pool.memset(ident[:, :], 0.0))
                        own.add(pool.memset(ones[:, :], 1.0))
                        own.add(pool.iota(iota_i[:, :], pattern=[[1, P]], base=0, channel_multiplier=0))
                        own.add(pool.iota(thr_i[:, :], pattern=[[P, NB + 2]], base=0, channel_multiplier=0))
                        own.add(pool.memset(eps[:, :], LN_EPS))
                        own.add(pool.iota(item_i[:, :], pattern=[[P, IJ]], base=0, channel_multiplier=1))
                        own.sync()
                        own.add(pool.affine_select(out=ident[:, :], in_=ident[:, :], compare_op=ALU.not_equal,
                                                   fill=1.0, base=0, pattern=[[-1, P]], channel_multiplier=1))
                        own.add(pool.affine_select(out=upper[:, :], in_=ones[:, :], compare_op=ALU.is_gt,
                                                   fill=0.0, base=0, pattern=[[1, P]], channel_multiplier=-1))
                        own.add(pool.memset(acc[:, :, :], 0.0))
                        pool.wait_ge(s_cidx, 1)
                        for j in range(IJ):
                            off = bass.IndirectOffsetOnAxis(ap=cidx[:, j:j + 1], axis=0)
                            for n, name in enumerate(("src", "dst")):
                                pool.indirect_dma_start(
                                    out=row_i[:, j, n, :], out_offset=None,
                                    in_=a[name].rearrange("(c p) -> c p", p=P), in_offset=off).then_inc(s_pg, 16)
                            pool.indirect_dma_start(
                                out=row_w[:, j, :], out_offset=None,
                                in_=a["w"].rearrange("(c p) -> c p", p=P), in_offset=off).then_inc(s_pg, 16)

                    @block.scalar
                    def _(act):
                        for h in range(2):
                            act.sem_inc(s_xst[h], 1)
                        act.wait_ge(s_z, 1)
                        act.dma_start(xd_d[NX * CAP:NX * CAP + SPARE * P, :].rearrange("(p r) d -> p r d", p=P),
                                      zero[:, :].unsqueeze(1).to_broadcast([P, SPARE, D])).then_inc(s_xdz, 16)
                        act.wait_ge(s_sgn, 1)
                        with act.Fori(0, NB // 5) as it:
                            for k in range(5):
                                act.wait_ge(s_sgn, it * 5 + k + 1)
                                alone(act)
                                nc.scalar.activation(junk2[:, :], src_f[:, :], ACT.Sign, scale=-1.0, bias=thr_h[:, ds(it * 5 + k, 1)],
                                                     accum_out=cum[:, 1, ds(it * 5 + k + 1, 1)]).then_inc(s_sgn, 1)

                        def deviation(g):
                            act.wait_ge(s_var, g + 1)
                            nc.scalar.activation(sd[:, :], mv[:, :, 1], ACT.Sqrt, bias=eps[:, :]).then_inc(s_sd, 1)

                        def rows(g):
                            act.wait_ge(s_ln, g + 1)
                            for h, tiles in enumerate(XN_PARTS):
                                act.wait_ge(s_xst[h], 16 * g + 1)
                                alone(act)
                                for k in tiles:
                                    t = g * G + k
                                    nc.scalar.activation(xn_st[:, k, :], xr[:, ds(t, 1), :], ACT.Identity,
                                                         bias=nmr[:, ds(t, 1)], scale=rstd[:, ds(t, 1)]).then_inc(s_xn, 1)

                        deviation(0)
                        with act.Fori(0, NG - 1) as g:
                            deviation(g + 1)
                            rows(g)
                        rows(NG - 1)
                        act.wait_ge(s_xdz, 16)

                    @block.vector
                    def _(dve):
                        own = Chain(dve, s_own)
                        nc.vector.memset(zero[:, :], 0.0).then_inc(s_z, 1)
                        dve.wait_ge(s_const, 8)
                        own.add(nc.vector.tensor_copy(iota_r[:, :], iota_i[:, :]))
                        own.add(nc.vector.tensor_copy(thr[:, :], thr_i[:, 1:NB + 1]))
                        own.add(nc.vector.tensor_copy(item_f[:, :], item_i[:, :]))
                        own.add(nc.vector.memset(cum[:, :, 0:1], 0.0))
                        dve.wait_ge(s_dst, 16)
                        own.add(nc.vector.tensor_copy(dst_f[:, :], dst_i[:, :]))
                        dve.wait_ge(s_src, 16)
                        own.add(nc.vector.tensor_copy(src_f[:, :], src_i[:, :]))
                        own.add(nc.vector.tensor_scalar(thr_h[:, :], thr_i[:, 1:NB + 1], -0.5, None, ALU.add))
                        own.sync()
                        nc.vector.memset(nil[:, 2:3], 0.0).then_inc(s_sgn, 1)
                        with dve.Fori(0, NB) as b:
                            dve.wait_ge(s_own, own.n + b)
                            nc.vector.tensor_scalar(junk[:, :], dst_f[:, :], thr[:, ds(b, 1)], None,
                                                    ALU.is_lt, ALU.add, accum_out=cum[:, 0, ds(b + 1, 1)]).then_inc(s_own, 1)
                        own.n += NB
                        dve.wait_ge(s_sgn, NB + 1)
                        own.add(nc.vector.tensor_scalar(cum[:, 1, 1:NB + 1], cum[:, 1, 1:NB + 1], float(NC), 0.5, ALU.add, ALU.mult))
                        own.sync()
                        own.add(nc.vector.tensor_tensor(cnt[:, :], cum[:, 1, 1:NB + 1], cum[:, 1, 0:NB], ALU.subtract))
                        own.sync()
                        nc.vector.memset(t128[:, :], 0.0).then_inc(s_cum, 1)
                        dve.wait_ge(s_off, 1)
                        own.add(nc.vector.tensor_copy(starts[:, :, :], psum[:, 0, 0:2 * (NB + 1)].rearrange("p (k b) -> p k b", k=2)))
                        own.sync()
                        own.add(nc.vector.tensor_copy(st_i[:, :, :], starts[:, :, :]))
                        for k, size in enumerate((P, P * RUN)):
                            own.add(nc.vector.tensor_scalar(up_i[:, k, :], starts[:, k, :], float(size - 1), None, ALU.add))
                        own.add(nc.vector.tensor_tensor(base[:, 0:NB], psum[:, 1, 0:NB], starts[:, 1, 0:NB], ALU.add))
                        own.sync()
                        for k, size in enumerate((P, P * RUN)):
                            shift = size.bit_length() - 1
                            own.add(nc.vector.tensor_scalar(c0_i[:, k, :], st_i[:, k, :], shift, None, ALU.arith_shift_right))
                            own.add(nc.vector.tensor_scalar(c1_i[:, k, :], up_i[:, k, :], shift, None, ALU.arith_shift_right))
                        own.add(nc.vector.tensor_tensor(nz[:, :, :], starts[:, :, 1:NB + 1], starts[:, :, 0:NB], ALU.is_gt))
                        own.add(nc.vector.tensor_scalar(base[:, 0:NB], base[:, 0:NB], 1.0, None, ALU.subtract))
                        own.sync()
                        own.add(nc.vector.tensor_tensor(ni[:, :, :], c1_i[:, :, 1:NB + 1], c0_i[:, :, 0:NB], ALU.subtract))
                        own.sync()
                        own.add(nc.vector.tensor_tensor(ni[:, :, :], ni[:, :, :], nz[:, :, :], ALU.mult))
                        own.sync()
                        for k in range(2):
                            own.add(nc.vector.tensor_tensor_scan(iend[:, k, :], ni[:, k, :], ni[:, k, :], 0.0, ALU.add, ALU.bypass))
                        own.sync()
                        own.add(nc.vector.tensor_tensor(dif[:, :, :], ni[:, :, :], iend[:, :, :], ALU.subtract))
                        own.sync()
                        own.add(nc.vector.tensor_tensor(dif[:, :, :], dif[:, :, :], c0_i[:, :, 0:NB], ALU.add))
                        own.sync()
                        own.add(nc.vector.tensor_tensor(ddif[:, :, :], dif[:, :, 1:NB], dif[:, :, 0:NT], ALU.subtract))
                        own.sync()
                        for k in range(2):
                            own.add(nc.vector.tensor_tensor(geq[:, :, :], iend[:, k, 0:NT].unsqueeze(1).to_broadcast([P, IJ, NT]),
                                                            item_f[:, :].unsqueeze(2).to_broadcast([P, IJ, NT]), ALU.is_le))
                            own.sync()
                            own.add(nc.vector.tensor_reduce(tab[:, k, :], geq[:, :, :], AX.X, ALU.add))
                            own.add(nc.vector.tensor_tensor(prod[:, :, :], geq[:, :, :],
                                                            ddif[:, k, :].unsqueeze(1).to_broadcast([P, IJ, NT]), ALU.mult))
                            own.sync()
                            own.add(nc.vector.tensor_reduce(tab[:, 2 + k, :], prod[:, :, :], AX.X, ALU.add))
                            own.sync()
                            own.add(nc.vector.tensor_tensor(tab[:, 2 + k, :], tab[:, 2 + k, :], item_f[:, :], ALU.add))
                            own.sync()
                            own.add(nc.vector.tensor_scalar(tab[:, 2 + k, :], tab[:, 2 + k, :], float(NC // (RUN if k else 1) - 1), None, ALU.min))
                            own.sync()
                        nc.vector.tensor_copy(cidx[:, :], tab[:, 2, :]).then_inc(s_cidx, 1)
                        nc.vector.tensor_scalar(t128[:, :], tab[:, 0, :], float(P), None, ALU.mult).then_inc(s_tab, 1)
                        dve.wait_ge(s_tabT, 1)
                        nc.vector.tensor_copy(tabT[:, :], psum[0:4 * IJ, 2, 0:P]).then_inc(s_row, 1)
                        own.add(nc.vector.memset(base[:, NB:NB + 2], 0.0))
                        own.add(nc.vector.tensor_scalar(dst_i[:, :], src_i[:, :], 7, None, ALU.arith_shift_right))
                        own.sync()
                        own.add(nc.vector.tensor_copy(kb[:, :], dst_i[:, :]))
                        own.add(nc.vector.tensor_scalar(bnum[:, :], thr_i[:, :], 1.0 / P, None, ALU.mult))
                        dve.wait_ge(s_x, 16)
                        n1 = own.n
                        with dve.Fori(0, NG) as g:
                            own = Chain(dve, s_own, g * LN_OWN + n1)
                            own.sync()
                            nc.vector.memset(nil[:, 2:3], 0.0)
                            for k in range(G):
                                own.add(nc.vector.bn_stats(stats[:, k, :], xr[:, ds(g * G + k, 1), :].squeeze(1)))
                            own.sync()
                            nc.vector.memset(nil[:, 0:1], 0.0)
                            for k in range(G):
                                own.add(nc.vector.bn_aggr(mv[:, k, :], stats[:, k, :]))
                            own.sync()
                            nc.vector.memset(nil[:, 1:2], 0.0).then_inc(s_var, 1)
                            dve.wait_ge(s_sd, g + 1)
                            alone(dve)
                            own.add(nc.vector.reciprocal(rstd[:, ds(g * G, G)], sd[:, :]))
                            own.sync()
                            alone(dve)
                            own.add(nc.vector.scalar_tensor_tensor(nmr[:, ds(g * G, G)], mv[:, :, 0], -1.0, rstd[:, ds(g * G, G)], ALU.mult, ALU.mult))
                            own.sync()
                            nc.vector.memset(nil[:, 3:4], 0.0).then_inc(s_ln, 1)
                            assert own.n == LN_OWN, own.n
                        own = Chain(dve, s_own, n1 + NG * LN_OWN)
                        own.sync()
                        dve.wait_ge(s_pg, 3 * 16 * IJ)
                        own.add(nc.vector.tensor_copy(row_f[:, :, :, :], row_i[:, :, :, :]))
                        own.sync()
                        nc.vector.tensor_tensor(row_f[:, :, 1, :], row_f[:, :, 1, :], t128[:, :].unsqueeze(2).to_broadcast([P, IJ, P]),
                                                ALU.subtract).then_inc(s_pf, 1)
                        for j in range(IJ):
                            dve.wait_ge(s_pt, j + 1)
                            nc.vector.tensor_scalar(it_src[:, j * P:(j + 1) * P], psum[:, 3 + j % 2, 0:P], float(NP - 1), None,
                                                    ALU.min).then_inc(s_pe, 1)
                            nc.vector.tensor_copy(it_rel[:, j * P:(j + 1) * P], psum[:, 3 + j % 2, P:2 * P]).then_inc(s_pe, 1)
                            nc.vector.tensor_copy(it_w[:, j * P:(j + 1) * P], psum[:, 3 + j % 2, 2 * P:3 * P]).then_inc(s_pe, 1)

                    @block.tensor
                    def _(pe):
                        pe.wait_ge(s_const, 8)
                        pe.wait_ge(s_cum, 1)
                        nc.tensor.matmul(psum[:, 0, 0:2 * (NB + 1)], ones[:, :], cum[:, :, :].rearrange("p k b -> p (k b)"),
                                         start=True, stop=True)
                        nc.tensor.matmul(psum[:, 1, 0:NB], upper[:, :], cnt[:, :], start=True, stop=True).then_inc(s_off, 1)
                        pe.wait_ge(s_tab, 1)
                        nc.tensor.transpose(psum[0:4 * IJ, 2, 0:P], tab[:, :, :].rearrange("p k j -> p (k j)"), ident[:, :]).then_inc(s_tabT, 1)
                        pe.wait_ge(s_pf, 1)
                        for j in range(IJ):
                            if j >= 2:
                                pe.wait_ge(s_pe, 3 * (j - 1))
                            nc.tensor.transpose(psum[:, 3 + j % 2, 0:P], row_f[:, j, 0, :], ident[:, :])
                            nc.tensor.transpose(psum[:, 3 + j % 2, P:2 * P], row_f[:, j, 1, :], ident[:, :])
                            nc.tensor.transpose(psum[:, 3 + j % 2, 2 * P:3 * P], row_w[:, j, :], ident[:, :]).then_inc(s_pt, 1)

            s_hot = sem("l0_onehot_ready")
            s_mm = sem("l0_products")
            s_acc = sem("l0_added")
            s_gat = [sem(f"l0_gathered{u}") for u in range(RING)]
            s_idx = sem("l0_indices_ready")
            s_rank = sem("ranked")
            with ExitStack() as ph2:
                idx = sb("idx", [P, 2, RING], i32, ph2)
                rows = sb("rows", [P, RING, D], f32, ph2)
                hot = sb("hot", [P, RING, P], f32, ph2)
                mask = sb("mask", [P, NC], f32, ph2)
                rank = sb("rank", [P, NC], f32, ph2)
                pos = sb("pos", [P, NC], f32, ph2)
                with nc.Block() as block:

                    @block.scalar
                    def _(act):
                        for h in range(2):
                            nc.scalar.activation(idx[:, h, :], it_src[:, h * RING:(h + 1) * RING], ACT.Copy).then_inc(s_idx, 1)
                        with act.Fori(0, NI // STEP - 1) as it:
                            for h in range(2):
                                act.wait_ge(s_mm, RING + it * STEP + (h + 1) * RING)
                                nc.scalar.activation(idx[:, h, :], it_src[:, ds((it + 1) * STEP + h * RING, RING)],
                                                     ACT.Copy).then_inc(s_idx, 1)

                    @block.gpsimd
                    def _(pool):
                        with pool.Fori(0, NI // STEP) as it:
                            for u in range(STEP):
                                if u % RING == 0:
                                    pool.wait_ge(s_idx, it * 2 + u // RING + 1)
                                pool.wait_ge(s_mm, it * STEP + u + 1)
                                alone(pool)
                                pool.indirect_dma_start(
                                    out=rows[:, u % RING, :], out_offset=None, in_=xn_d,
                                    in_offset=bass.IndirectOffsetOnAxis(ap=idx[:, u // RING, u % RING:u % RING + 1], axis=0),
                                ).then_inc(s_gat[u % RING], 16)

                    @block.tensor
                    def _(pe):
                        pe.sem_inc(s_mm, RING)
                        with pe.Fori(0, NI // STEP) as it:
                            for u in range(STEP):
                                pe.wait_ge(s_hot, it * STEP + u + 1)
                                pe.wait_ge(s_gat[u % RING], it * (16 * STEP // RING) + 16 * (u // RING + 1))
                                pe.wait_ge(s_acc, it * STEP + u + 1)
                                nc.tensor.matmul(psum[:, u % RING, 0:D], hot[:, u % RING, :], rows[:, u % RING, :],
                                                 start=True, stop=True).then_inc(s_mm, 1)

                    @block.vector
                    def _(dve):
                        dve.sem_inc(s_acc, RING)
                        nc.vector.memset(pos[:, :], 0.0).then_inc(s_rank, 1)
                        with dve.Fori(0, NI // STEP) as it:

                            def onehot(u):
                                dve.wait_ge(s_mm, it * STEP + u + 1)
                                nc.vector.tensor_scalar(hot[:, u % RING, :], iota_r[:, :], it_rel[:, ds(it * STEP + u, 1)],
                                                        it_w[:, ds(it * STEP + u, 1)], ALU.is_equal, ALU.mult).then_inc(s_hot, 1)

                            for u in range(RING):
                                onehot(u)
                            dve.wait_ge(s_rank, it * 3 + 1)
                            nc.vector.tensor_scalar(mask[:, :], kb[:, :], bnum[:, ds(it, 1)], None, ALU.is_equal).then_inc(s_rank, 1)
                            dve.wait_ge(s_rank, it * 3 + 2)
                            nc.vector.tensor_tensor_scan(rank[:, :], mask[:, :], mask[:, :], base[:, ds(it, 1)],
                                                         ALU.add, ALU.bypass).then_inc(s_rank, 1)
                            dve.wait_ge(s_rank, it * 3 + 3)
                            alone(dve)
                            nc.vector.copy_predicated(pos[:, :], mask[:, :].bitcast(i32), rank[:, :]).then_inc(s_rank, 1)
                            for half in range(2):
                                tiles = nc.values_load_multi_w_load_instructions(
                                    items[0:1, ds(it * STEP + half * RING, RING)], [mybir.EngineType.DVE], min_val=0, max_val=NB - 1,
                                    skip_runtime_bounds_check_because="a tile's number is a count of at most NB - 1 buckets")[1]
                                for k in range(RING):
                                    u = half * RING + k
                                    dve.wait_ge(s_mm, RING + it * STEP + u + 1)
                                    dve.wait_ge(s_acc, RING + it * STEP + u)
                                    there = acc[:, ds(tiles[k], 1), :].squeeze(1)
                                    nc.vector.tensor_tensor(there, there, psum[:, u % RING, 0:D], ALU.add).then_inc(s_acc, 1)
                                    if half == 0:
                                        onehot(u + RING)
                        dve.wait_ge(s_rank, 3 * (NI // STEP) + 1)
                        nc.vector.tensor_copy(pos_i[:, :], pos[:, :]).then_inc(s_rank, 1)

        s_v5 = sem("l1_variance")
        s_sd5 = sem("l1_deviation")
        s_ln5 = sem("l1_rstd")
        s_a5 = sem("l1_rows")
        s_t5 = sem("l1_transposed")
        s_tc5 = sem("l1_columns")
        s_h5 = sem("l1_hidden_products")
        s_hc5 = sem("l1_hidden")
        s_hx = sem("l1_part_moved")
        with ExitStack() as ph3:
            stage = sb("stage", [P, 2, SC, ER], f32, ph3)
            sidx = sb("sidx", [P, 2, SC], i32, ph3)
            src3 = sb("src3", [P, NC], i32, ph3)
            w_self = sb("w_self", [P, 2, D], f32, ph3)
            w_neigh = sb("w_neigh", [P, 2, D], f32, ph3)
            w1 = sb("w1", [P, 2, 6, P], f32, ph3)
            b1 = sb("b1", [P, 6], f32, ph3)
            w2s = sb("w2s", [P, 2, P], f32, ph3)
            w2e = sb("w2e", [P, 4, P // 2], f32, ph3)
            b2 = sb("b2", [P, 3], f32, ph3)
            w3 = sb("w3", [P, 3, D], f32, ph3)
            b3 = sb("b3", [5, D], f32, ph3)
            gw = sb("gw", [P, 2, 4], f32, ph3)
            gb = sb("gb", [1, 4], f32, ph3)
            pair = sb("pair", [4, 2, P], f32, ph3)
            rev = sb("rev", [P, 8], f32, ph3)
            rev_i = sb("rev_i", [P, 8], i32, ph3)
            xs = sb("xs", [P, G, 2 * D], f32, ph3)
            tT = sb("tT", [P, 2, 4, P], f32, ph3)
            sq = sb("sq", [P, D], f32, ph3)
            ss = sb("ss", [P, G], f32, ph3)
            nrm = sb("nrm", [P, G], f32, ph3)
            rn = sb("rn", [P, G], f32, ph3)
            ln = {n: sb("ln_" + n, s, f32, ph3) for n, s in
                  (("stats", [P, G, 6]), ("mv", [P, G, 2]), ("sd", [P, G]), ("rstd", [P, G]), ("nmr", [P, G]), ("nil", [P, 4]))}
            yT = sb("yT", [P, 2, G * P], f32, ph3)
            h1 = sb("h1", [P, 6, G * P], f32, ph3)
            h2 = sb("h2", [P, 3, G * P], f32, ph3)
            gt = {n: sb("gt_" + n, [P, G, 4], f32, ph3) for n in ("l", "e", "g", "eq", "sc", "o1", "g2", "eq2", "sc2", "o2")}
            g1 = {n: sb("g1_" + n, [P, G], f32, ph3) for n in ("m", "s", "r", "v1", "k1", "v2", "k2", "d", "x", "t", "w1", "w2")}
            cf = sb("cf", [P, G, 5], f32, ph3)
            cfT = sb("cfT", [5, G * P], f32, ph3)

            gw1 = sb("gw1", [P, 2, 4, P], f32, ph3)
            s_w3 = sem("weights")
            s_att = [sem(f"attributes_loaded{h}") for h in range(2)]
            s_side = sem("scatter_sides_ready")
            s_own3 = sem("l0_vector_own")
            s_sca = [sem(f"scattered{h}") for h in range(2)]
            s_c3 = sem("l0_constants")
            s_a = sem("l0_normalised")
            s_t1 = sem("l0_transposed")
            s_t1c = sem("l0_columns")
            s_gnn = sem("l0_gnn_products")
            s_ss = sem("l0_squares")
            s_nrm = sem("l0_norms")
            s_v3 = sem("l0_variance")
            s_sd3 = sem("l0_deviation")
            s_ln3 = sem("l0_rstd")
            s_y = sem("l0_ffn_rows")
            s_t2 = sem("l0_ffn_transposed")
            s_yT = sem("l0_ffn_columns")
            s_h1 = sem("l0_hidden1_products")
            s_h1c = sem("l0_hidden1")
            s_h2 = sem("l0_hidden2_products")
            s_h2c = sem("l0_hidden2")
            s_lg = sem("l0_logits")
            s_mx = sem("l0_shifted")
            s_ex = sem("l0_exponentials")
            s_df = sem("l0_gate_gap")
            s_ex2 = sem("l0_gate_ratio")
            s_cf = sem("l0_coefficients")
            s_cT = sem("l0_coefficients_transposed")
            s_cTc = sem("l0_coefficient_columns")
            s_gbr = sem("l0_gates_spread")
            s_h2g = sem("l0_hidden2_gated")
            s_y3 = sem("l0_ffn_products")
            s_x2 = sem("l0_rows_done")

            with nc.Block() as block:

                @block.sync
                def _(sp):
                    attr = a["attr"].rearrange("(p c) f -> p c f", p=P)
                    for h in range(2):
                        sp.dma_start(stage[:, h, :, 0:EA], attr[:, h * SC:(h + 1) * SC, :]).then_inc(s_att[h], 16)
                    sp.dma_start(src3[:, :], a["src"].rearrange("(p c) -> p c", p=P)).then_inc(s_src, 16)
                    for dst, src in (
                        (gw1[:, :, :, :], a["g_W1"][0:D, :].rearrange("(c p) (m n) -> p c m n", p=P, n=P)),
                        (w_self[:, :, :], a["w_self"].rearrange("(c p) n -> p c n", p=P)),
                        (w_neigh[:, :, :], a["w_neigh"].rearrange("(c p) n -> p c n", p=P)),
                        (w1[:, :, 0:2, :], a["sW1"].rearrange("(c p) (m n) -> p c m n", p=P, n=P)),
                        (w2s[:, :, :], a["sW2"].rearrange("(c p) n -> p c n", p=P)),
                        (w2e[:, :, :], a["eW2"].rearrange("e p n -> p e n")),
                        (w3[:, 0, :], a["sW3"]),
                        (w3[:, 1:3, :], a["eW3"].rearrange("(q e) k n -> (e k) q n", q=2)),
                        (b3[0:4, :], a["eb3"]),
                        (b3[4:5, :], a["sb3"].unsqueeze(0)),
                        (gw[:, :, :], a["gW"].rearrange("(c p) n -> p c n", p=P)),
                        (gb[:, :], a["gb"].unsqueeze(0)),
                        (b1[:, 0:2], a["sb1"].rearrange("(m p) -> p m", p=P)),
                        (b1[:, 2:6], a["eb1"].rearrange("e p -> p e")),
                        (b2[:, 0:1], a["sb2"].unsqueeze(1)),
                        (b2[:, 1:3], a["eb2"].rearrange("(q e) k -> (e k) q", q=2)),
                    ):
                        with nc.allow_non_contiguous_dma(reason="a few hundred biases"):
                            sp.dma_start(dst, src).then_inc(s_w3, 16)
                    for c in range(2):
                        sp.dma_start(w1[:, c, 2:6, :], a["eW1"][:, c * P:(c + 1) * P, :].rearrange("e p n -> p e n")).then_inc(s_w3, 16)
                    with sp.Fori(0, NC // SC // 2 - 1) as it:
                        for h in range(2):
                            sp.wait_ge(s_sca[h], (it + 1) * (16 * SC))
                            sp.dma_start(stage[:, h, :, 0:EA], attr[:, ds((it + 1) * (2 * SC) + h * SC, SC), :]).then_inc(s_att[h], 16)

                @block.gpsimd
                def _(pool):
                    own = Chain(pool, s_c3)
                    own.add(pool.iota(rev_i[:, :], pattern=[[-1, 8]], base=8, channel_multiplier=0))
                    own.add(pool.memset(pair[:, :, :], 0.0))
                    own.add(pool.memset(stage[:, :, :, EA:EA + 1], 1.0))
                    own.add(pool.memset(cf[:, :, 4:5], 1.0))
                    own.sync()
                    for m in range(4):
                        own.add(pool.affine_select(out=pair[:, m // 2, m % 2 * (P // 2):(m % 2 + 1) * (P // 2)],
                                                   in_=pair[:, m // 2, m % 2 * (P // 2):(m % 2 + 1) * (P // 2)],
                                                   compare_op=ALU.not_equal, fill=1.0, base=-m,
                                                   pattern=[[0, P // 2]], channel_multiplier=1))
                    own.sync()
                    pool.wait_ge(s_src, 32)
                    with pool.Fori(0, NC // SC // 2) as it:
                        for h in range(2):
                            pool.wait_ge(s_att[h], it * 16 + 16)
                            alone(pool)
                            at = ds(it * (2 * SC) + h * SC, SC)
                            pool.tensor_copy(sidx[:, h, :], pos_i[:, at]).then_inc(s_side, 1)
                            pool.tensor_copy(stage[:, h, :, EA + 1], src3[:, at]).then_inc(s_side, 1)
                            pool.wait_ge(s_side, it * 4 + 2 * h + 2)
                            alone(pool)
                            for c in range(SC):
                                pool.indirect_dma_start(
                                    out=edges_d, out_offset=bass.IndirectOffsetOnAxis(ap=sidx[:, h, c:c + 1], axis=0),
                                    in_=stage[:, h, c, :], in_offset=None).then_inc(s_sca[h], 16)
                    for h in range(2):
                        pool.wait_ge(s_sca[h], 16 * SC * (NC // SC // 2))

                @block.scalar
                def _(act):
                    act.wait_ge(s_w3, 16 * 18)
                    act.wait_ge(s_c3, 8)
                    act.sem_inc(s_t2, 1)
                    act.sem_inc(s_hx, 1)
                    act.sem_inc(s_ss, 1)
                    with act.Fori(0, NG) as g:
                        act.wait_ge(s_t2, g * G + 1)
                        alone(act)
                        for k in range(G):
                            t = g * G + k
                            nc.scalar.activation(xs[:, k, 0:D], xr[:, ds(t, 1), :].squeeze(1), ACT.Identity,
                                                 bias=nmr[:, ds(t, 1)], scale=rstd[:, ds(t, 1)])
                            nc.scalar.activation(xs[:, k, D:2 * D], acc[:, ds(t, 1), :].squeeze(1), ACT.Copy).then_inc(s_a, 1)
                        for k in range(G):
                            act.wait_ge(s_gnn, g * G + min(k | 1, G - 1) + 1)
                            act.wait_ge(s_ss, g * G + k + 1)
                            nc.scalar.activation(sq[:, :], psum[:, k // 2, k % 2 * D:(k % 2 + 1) * D], ACT.Square,
                                                 accum_out=ss[:, k:k + 1]).then_inc(s_ss, 1)
                        act.wait_ge(s_ss, g * G + G + 1)
                        nc.scalar.activation(nrm[:, :], ss[:, :], ACT.Sqrt).then_inc(s_nrm, 1)
                        act.wait_ge(s_v3, g + 1)
                        nc.scalar.activation(ln["sd"][:, :], ln["mv"][:, :, 1], ACT.Sqrt, bias=eps[:, :]).then_inc(s_sd3, 1)
                        act.wait_ge(s_ln3, g + 1)
                        alone(act)
                        for k in range(G):
                            nc.scalar.activation(xs[:, k, 0:D], xr[:, ds(g * G + k, 1), :].squeeze(1), ACT.Identity,
                                                 bias=ln["nmr"][:, k:k + 1], scale=ln["rstd"][:, k:k + 1]).then_inc(s_y, 1)
                        act.wait_ge(s_mx, g + 1)
                        nc.scalar.activation(gt["e"][:, :, :], gt["l"][:, :, :], ACT.Exp).then_inc(s_ex, 1)
                        act.wait_ge(s_hx, g * 16 + 1)
                        for n in range(12):
                            m, (c0, c1) = n // 2, HALVES[n % 2]
                            act.wait_ge(s_h1, g * 12 + n + 1)
                            nc.scalar.activation(h1[:, m, c0:c1], psum[:, 4 + n % 4, 0:c1 - c0], ACT.Relu,
                                                 bias=b1[:, m:m + 1]).then_inc(s_h1c, 1)
                        act.wait_ge(s_df, g + 1)
                        nc.scalar.activation(g1["x"][:, :], g1["d"][:, :], ACT.Exp).then_inc(s_ex2, 1)
                        for n in range(6):
                            m, (c0, c1) = n // 2, HALVES[n % 2]
                            act.wait_ge(s_h2, g * 6 + n + 1)
                            nc.scalar.activation(h2[:, m, c0:c1], psum[:, 4 + n % 4, 0:c1 - c0], ACT.Relu,
                                                 bias=b2[:, m:m + 1]).then_inc(s_h2c, 1)
                        act.wait_ge(s_v5, g + 1)
                        nc.scalar.activation(ln["sd"][:, :], ln["mv"][:, :, 1], ACT.Sqrt, bias=eps[:, :]).then_inc(s_sd5, 1)
                        act.wait_ge(s_ln5, g + 1)
                        alone(act)
                        for k in range(G):
                            nc.scalar.activation(xs[:, k, 0:D], xr[:, ds(g * G + k, 1), :].squeeze(1), ACT.Identity,
                                                 bias=ln["nmr"][:, k:k + 1], scale=ln["rstd"][:, k:k + 1]).then_inc(s_a5, 1)
                        for n in range(8):
                            m, (c0, c1) = n // 2, HALVES[n % 2]
                            act.wait_ge(s_h5, g * 8 + n + 1)
                            nc.scalar.activation(h1[:, m, c0:c1], psum[:, 4 + n % 4, 0:c1 - c0], ACT.Copy).then_inc(s_hc5, 1)
                        act.wait_ge(s_hc5, g * 8 + 8 + 1)
                        act.dma_start(hx_d[ds(g * P, P), :], h1[:, 0:4, :].rearrange("p m n -> p (m n)")).then_inc(s_hx, 16)
                    act.wait_ge(s_hx, NG * 16 + 1)

                @block.tensor
                def _(pe):
                    pe.wait_ge(s_w3, 16 * 18)
                    pe.wait_ge(s_c3, 8)
                    pe.sem_inc(s_x2, 1)
                    pe.sem_inc(s_hc5, 1)
                    with pe.Fori(0, NG) as g:

                        def products(k):
                            pe.wait_ge(s_t1c, g * G + k + 1)
                            for c in range(4):
                                w = (w_self if c < 2 else w_neigh)[:, c % 2, :]
                                last = nc.tensor.matmul(psum[:, k // 2, k % 2 * D:(k % 2 + 1) * D], tT[:, k % 2, c, :], w,
                                                        start=c == 0, stop=c == 3)
                            last.then_inc(s_gnn, 1)

                        pe.wait_ge(s_x2, g * G + 1)
                        pe.wait_ge(s_hc5, g * 8 + 1)
                        for k in range(G):
                            pe.wait_ge(s_a, g * G + k + 1)
                            if k >= 2:
                                pe.wait_ge(s_t1c, g * G + k - 1)
                            for c in range(4):
                                last = nc.tensor.transpose(psum[:, 4 + k % 2, c * P:(c + 1) * P], xs[:, k, c * P:(c + 1) * P], ident[:, :])
                            last.then_inc(s_t1, 1)
                            if k:
                                products(k - 1)
                        products(G - 1)
                        for k in range(G):
                            pe.wait_ge(s_y, g * G + k + 1)
                            if k >= 2:
                                pe.wait_ge(s_yT, g * G + k - 1)
                            for c in range(2):
                                last = nc.tensor.transpose(psum[:, 4 + k % 2, c * P:(c + 1) * P], xs[:, k, c * P:(c + 1) * P], ident[:, :])
                            last.then_inc(s_t2, 1)
                        pe.wait_ge(s_yT, g * G + G)
                        for k in range(G):
                            for c in range(2):
                                nc.tensor.matmul(psum[:, 6, k * 4:k * 4 + 4], yT[:, c, k * P:(k + 1) * P], gw[:, c, :],
                                                 start=c == 0, stop=False)
                            last = nc.tensor.matmul(psum[:, 6, k * 4:k * 4 + 4], ones[0:1, :], gb[:, :], start=False, stop=True)
                        last.then_inc(s_lg, 1)
                        for n in range(12):
                            m, (c0, c1) = n // 2, HALVES[n % 2]
                            if n >= 4:
                                pe.wait_ge(s_h1c, g * 12 + n - 3)
                            if n == 2:
                                pe.wait_ge(s_mx, g + 1)
                            for c in range(2):
                                last = nc.tensor.matmul(psum[:, 4 + n % 4, 0:c1 - c0], w1[:, c, m, :], yT[:, c, c0:c1],
                                                        start=c == 0, stop=c == 1)
                            last.then_inc(s_h1, 1)
                        for n in range(6):
                            m, (c0, c1) = n // 2, HALVES[n % 2]
                            pe.wait_ge(s_h1c, g * 12 + 12)
                            if n >= 4:
                                pe.wait_ge(s_h2c, g * 6 + n - 3)
                            for c in range(2):
                                if m == 0:
                                    last = nc.tensor.matmul(psum[:, 4 + n % 4, 0:c1 - c0], w2s[:, c, :], h1[:, c, c0:c1],
                                                            start=c == 0, stop=c == 1)
                                else:
                                    e = 2 * (m - 1) + c
                                    last = nc.tensor.matmul(psum[c * (P // 2):(c + 1) * (P // 2), 4 + n % 4, 0:c1 - c0],
                                                            w2e[:, e, :], h1[:, 2 + e, c0:c1], start=True, stop=True)
                            last.then_inc(s_h2, 1)
                        pe.wait_ge(s_cf, g + 1)
                        for n, (c0, c1) in enumerate(HALVES):
                            for k in range(c0 // P, c1 // P):
                                last = nc.tensor.transpose(psum[0:5, n, k * P - c0:(k + 1) * P - c0], cf[:, k, :], ident[:, :])
                            last.then_inc(s_cT, 1)
                        pe.wait_ge(s_cTc, g * 2 + 2)
                        for n in range(4):
                            q, (c0, c1) = n // 2, HALVES[n % 2]
                            nc.tensor.matmul(psum[:, n, 0:c1 - c0], pair[:, q, :], cfT[0:4, c0:c1], start=True, stop=True).then_inc(s_gbr, 1)
                        for k in range(G):
                            if k == 0:
                                pe.wait_ge(s_h2c, g * 6 + 6)
                            pe.wait_ge(s_h2g, g * 4 + (3 if k < 4 else 4))
                            if k >= 4:
                                pe.wait_ge(s_x2, g * G + k - 2)
                            for m in range(3):
                                nc.tensor.matmul(psum[:, 4 + k % 4, 0:D], h2[:, m, k * P:(k + 1) * P], w3[:, m, :], start=m == 0, stop=False)
                            nc.tensor.matmul(psum[:, 4 + k % 4, 0:D], cfT[:, k * P:(k + 1) * P], b3[:, :], start=False, stop=True).then_inc(s_y3, 1)
                        for k in range(G):
                            pe.wait_ge(s_a5, g * G + k + 1)
                            if k >= 2:
                                pe.wait_ge(s_tc5, g * G + k - 1)
                            for c in range(2):
                                last = nc.tensor.transpose(psum[:, k % 2, c * P:(c + 1) * P], xs[:, k, c * P:(c + 1) * P], ident[:, :])
                            last.then_inc(s_t5, 1)
                        pe.wait_ge(s_tc5, g * G + G)
                        for n in range(8):
                            m, (c0, c1) = n // 2, HALVES[n % 2]
                            if n >= 4:
                                pe.wait_ge(s_hc5, g * 8 + n - 3 + 1)
                            for c in range(2):
                                last = nc.tensor.matmul(psum[:, 4 + n % 4, 0:c1 - c0], gw1[:, c, m, :], yT[:, c, c0:c1], start=c == 0, stop=c == 1)
                            last.then_inc(s_h5, 1)

                @block.vector
                def _(dve):
                    dve.wait_ge(s_c3, 8)
                    nc.vector.tensor_copy(rev[:, :], rev_i[:, :]).then_inc(s_own3, 1)
                    with dve.Fori(0, NG) as g:
                        own = Chain(dve, s_own3, 1 + g * DENSE0_OWN)
                        for k in range(G):
                            dve.wait_ge(s_t1, g * G + k + 1)
                            if k >= 2:
                                dve.wait_ge(s_gnn, g * G + k - 1)
                            nc.vector.tensor_copy(tT[:, k % 2, :, :].rearrange("p c n -> p (c n)"), psum[:, 4 + k % 2, :]).then_inc(s_t1c, 1)
                        dve.wait_ge(s_nrm, g + 1)
                        own.add(nc.vector.tensor_scalar(nrm[:, :], nrm[:, :], 1e-12, None, ALU.max))
                        own.sync()
                        own.add(nc.vector.reciprocal(rn[:, :], nrm[:, :]))
                        own.sync()
                        for k in range(G):
                            x = xr[:, ds(g * G + k, 1), :].squeeze(1)
                            own.add(nc.vector.scalar_tensor_tensor(x, psum[:, k // 2, k % 2 * D:(k % 2 + 1) * D], rn[:, k:k + 1], x,
                                                                   ALU.mult, ALU.add))
                        own.sync()
                        normalise(dve, own, xr, g, ln, s_v3, s_sd3, s_ln3)
                        for k in range(G):
                            dve.wait_ge(s_t2, g * G + k + 2)
                            nc.vector.tensor_copy(yT[:, :, k * P:(k + 1) * P],
                                                  psum[:, 4 + k % 2, 0:2 * P].rearrange("p (c n) -> p c n", c=2)).then_inc(s_yT, 1)
                        dve.wait_ge(s_lg, g + 1)
                        logits = psum[:, 6, 0:4 * G].rearrange("p (k e) -> p k e", e=4)
                        own.add(nc.vector.tensor_reduce(g1["m"][:, :], logits, AX.X, ALU.max))
                        own.sync()
                        nc.vector.tensor_tensor(gt["l"][:, :, :], logits, wide(g1["m"], 4), ALU.subtract).then_inc(s_mx, 1)
                        dve.wait_ge(s_ex, g + 1)
                        own.add(nc.vector.tensor_reduce(g1["s"][:, :], gt["e"][:, :, :], AX.X, ALU.add))
                        own.sync()
                        own.add(nc.vector.reciprocal(g1["r"][:, :], g1["s"][:, :]))
                        own.sync()
                        own.add(nc.vector.tensor_tensor(gt["g"][:, :, :], gt["e"][:, :, :], wide(g1["r"], 4), ALU.mult))
                        own.sync()
                        top_two(own, gt, g1, rev, 4)
                        nc.vector.tensor_tensor(g1["d"][:, :], g1["v2"][:, :], g1["v1"][:, :], ALU.subtract).then_inc(s_df, 1)
                        dve.wait_ge(s_ex2, g + 1)
                        two_weights(own, g1)
                        own.add(nc.vector.tensor_tensor(gt["g2"][:, :, :], gt["o1"][:, :, :], wide(g1["w1"], 4), ALU.mult))
                        own.add(nc.vector.tensor_tensor(gt["e"][:, :, :], gt["o2"][:, :, :], wide(g1["w2"], 4), ALU.mult))
                        own.sync()
                        nc.vector.tensor_tensor(cf[:, :, 0:4], gt["g2"][:, :, :], gt["e"][:, :, :], ALU.add).then_inc(s_cf, 1)
                        for n, (c0, c1) in enumerate(HALVES):
                            dve.wait_ge(s_cT, g * 2 + n + 1)
                            nc.vector.tensor_copy(cfT[:, c0:c1], psum[0:5, n, 0:c1 - c0]).then_inc(s_cTc, 1)
                        for n in (0, 2, 1, 3):
                            q, (c0, c1) = n // 2, HALVES[n % 2]
                            dve.wait_ge(s_gbr, g * 4 + n + 1)
                            dve.wait_ge(s_h2c, g * 6 + 2 * (q + 1) + n % 2 + 1)
                            nc.vector.tensor_tensor(h2[:, 1 + q, c0:c1], h2[:, 1 + q, c0:c1], psum[:, n, 0:c1 - c0], ALU.mult).then_inc(s_h2g, 1)
                        for k in range(G):
                            dve.wait_ge(s_y3, g * G + k + 1)
                            x = xr[:, ds(g * G + k, 1), :].squeeze(1)
                            nc.vector.tensor_tensor(x, psum[:, 4 + k % 4, 0:D], x, ALU.add).then_inc(s_x2, 1)
                        dve.wait_ge(s_x2, g * G + G + 1)
                        normalise(dve, own, xr, g, ln, s_v5, s_sd5, s_ln5)
                        for k in range(G):
                            dve.wait_ge(s_t5, g * G + k + 1)
                            nc.vector.tensor_copy(yT[:, :, k * P:(k + 1) * P],
                                                  psum[:, k % 2, 0:2 * P].rearrange("p (c n) -> p c n", c=2)).then_inc(s_tc5, 1)
                        assert own.n == DENSE0_OWN, own.n

        early.close()
        wt1 = sb("wt1", [P, NT])
        wt2 = sb("wt2", [P, NT])
        place_i = sb("place_i", [P, 2, NT], i32)
        run0 = sb("run0", [P, NX])
        run6 = sb("run6", [P, NX])
        weights = ctx.enter_context(ExitStack())
        fw1 = sb("fw1", [P, NX, 2, HX], f32, weights)
        fb1 = sb("fb1", [P, NX, HX // P], f32, weights)
        fb2 = sb("fb2", [P, NX, D], f32, weights)
        s_w7 = sem("moe_weights")
        s_n7 = sem("moe_counts")
        s_o7 = sem("moe_offsets")
        s_pl7 = sem("moe_places")
        s_free = sem("moe_dispatch_done")
        s_pad = sem("moe_filled")
        s_id7 = sem("moe_place_copied")
        s_dp = [sem(f"moe_slot_moved{k}") for k in range(G)]

        with ExitStack() as ph4:
            agg = sb("agg", [P, NB, EA + 1], f32, ph4)
            rcount = sb("rcount", [P, NB], f32, ph4)
            s_own4 = sem("later_vector_own")
            s_one = sem("l1_onehot_ready")
            s_prd = sem("l1_products")
            s_add = sem("l1_added")
            s_row4 = [sem(f"l1_rows_loaded{u}") for u in range(STEP4)]
            s_hi = sem("l1_first_part")
            s_r1 = sem("l1_remainder")
            s_mid = sem("l1_second_part")
            s_lo = sem("l1_third_part")
            with ExitStack() as ph5:
                items4 = sb("items4", [4, IJ * P], i32, ph5)
                tile_bi = sb("tile_bi", [P, IJ * P], i32, ph5)
                tile_b = sb("tile_b", [P, IJ * P], f32, ph5)
                rows4 = sb("rows4", [P, STEP4, RUN, ER], f32, ph5)
                parts = sb("parts", [P, STEP4, RUN, 3 * EA + 2], bf16, ph5)
                hot4 = sb("hot4", [P, RING, RUN, P], bf16, ph5)
                with nc.Block() as block:

                    @block.sync
                    def _(sp):
                        sp.dma_start(tile_bi[:, :], item_d[1:2, :].partition_broadcast(P).squeeze(1)).then_inc(s_rst, 16)
                        sp.dma_start(items4[:, :], item_d).then_inc(s_rst, 16)
                        sp.wait_ge(s_rst, 64)
                        with sp.Fori(0, NI4 // STEP4) as it:
                            for half in range(2):
                                runs = nc.values_load_multi_w_load_instructions(
                                    items4[3:4, ds(it * STEP4 + half * RING, RING)], [mybir.EngineType.SP], min_val=0, max_val=NC // RUN - 1,
                                    skip_runtime_bounds_check_because="a run's number is clamped to the last")[1]
                                for k in range(RING):
                                    u = half * RING + k
                                    sp.wait_ge(s_prd, it * STEP4 + u + 1)
                                    sp.dma_start(rows4[:, u, :, :], edges_d[ds(runs[k] * (P * RUN), P * RUN), :].rearrange(
                                        "(p c) f -> p c f", c=RUN)).then_inc(s_row4[u], 16)
                        for u in range(HALF4):
                            sp.wait_ge(s_prd, NI4 + u + 1)
                            sp.dma_start(rows4[:, u, :, :], edges_d[EP - P * RUN:EP, :].rearrange("(p c) f -> p c f", c=RUN)).then_inc(s_row4[u], 16)

                    def whole(u):
                        return rows4[:, u:u + 2, :, 0:EA]

                    def part(u, n):
                        c0 = (0, EA + 1, 2 * EA + 1)[n]
                        return parts[:, u:u + 2, :, c0:c0 + EA]

                    @block.scalar
                    def _(act):
                        def first(it, u):
                            for v in (u, u + 1):
                                act.wait_ge(s_row4[v], it * 16 + 16)
                            alone(act)
                            nc.scalar.activation(part(u, 0), whole(u), ACT.Copy).then_inc(s_hi, 1)

                        first(0, 0)
                        with act.Fori(0, NI4 // STEP4) as it:
                            for u in range(0, STEP4, 2):
                                if u + 2 < STEP4:
                                    first(it, u + 2)
                                else:
                                    first(it + 1, 0)
                                act.wait_ge(s_r1, it * (STEP4 // 2) + u // 2 + 1)
                                nc.scalar.activation(part(u, 1), whole(u), ACT.Copy).then_inc(s_mid, 1)

                    @block.gpsimd
                    def _(pool):
                        pool.memset(parts[:, :, :, EA:EA + 1], 1.0).then_inc(s_lo, 1)

                        def remainder(n, u):
                            pool.wait_ge(s_hi, n + 1)
                            alone(pool)
                            pool.tensor_tensor(whole(u), whole(u), part(u, 0), ALU.subtract).then_inc(s_r1, 1)

                        remainder(0, 0)
                        with pool.Fori(0, NI4 // STEP4) as it:
                            for u in range(0, STEP4, 2):
                                n = it * (STEP4 // 2) + u // 2
                                remainder(n + 1, (u + 2) % STEP4)
                                if u in LO_DVE:
                                    continue
                                pool.wait_ge(s_mid, n + 1)
                                alone(pool)
                                pool.tensor_tensor(part(u, 2), whole(u), part(u, 1), ALU.subtract).then_inc(s_lo, 1)

                    @block.tensor
                    def _(pe):
                        pe.sem_inc(s_prd, STEP4)
                        with pe.Fori(0, NI4 // STEP4) as it:
                            for u in range(STEP4):
                                if u % 2 == 0 and u not in LO_DVE:
                                    pe.wait_ge(s_lo, it * (STEP4 // 2 - len(LO_DVE)) + u // 2 + 2 - sum(v < u for v in LO_DVE))
                                pe.wait_ge(s_one, it * (STEP4 + len(LO_DVE)) + u + 1 + sum(v <= u for v in LO_DVE))
                                pe.wait_ge(s_add, it * STEP4 + u + 1)
                                for c in range(RUN):
                                    for n in ((1, 2, 0) if c == RUN - 1 else (0, 1, 2)):
                                        c0, width = ((0, EA + 1), (EA + 1, EA), (2 * EA + 1, EA))[n]
                                        last = nc.tensor.matmul(psum[:, u % RING, 0:width], hot4[:, u % RING, c, :],
                                                                parts[:, u, c, c0:c0 + width],
                                                                start=c == 0 and n == 0, stop=c == RUN - 1 and n == 0)
                                last.then_inc(s_prd, 1)

                    @block.vector
                    def _(dve):
                        dve.sem_inc(s_add, RING)
                        own = Chain(dve, s_own4)
                        own.add(nc.vector.memset(agg[:, :, :], 0.0))
                        dve.wait_ge(s_rst, 64)
                        own.add(nc.vector.tensor_scalar(tile_b[:, :], tile_bi[:, :], float(P), None, ALU.mult))
                        own.sync()

                        def onehots(it, u):
                            if u in LO_DVE:
                                dve.wait_ge(s_mid, it * (STEP4 // 2) + u // 2 + 1)
                                alone(dve)
                                nc.vector.tensor_tensor(part(u, 2), whole(u), part(u, 1), ALU.subtract).then_inc(s_one, 1)
                            dve.wait_ge(s_row4[u], it * 16 + 16)
                            dve.wait_ge(s_prd, STEP4 - RING + it * STEP4 + u + 1)
                            alone(dve)
                            nc.vector.scalar_tensor_tensor(
                                hot4[:, u % RING, :, :], iota_r[:, :].unsqueeze(1).to_broadcast([P, RUN, P]), tile_b[:, ds(it * STEP4 + u, 1)],
                                rows4[:, u, :, EA + 1:EA + 2].to_broadcast([P, RUN, P]), ALU.add, ALU.is_equal).then_inc(s_one, 1)

                        for u in range(HALF4):
                            onehots(0, u)
                        with dve.Fori(0, NI4 // STEP4) as it:
                            for quarter in range(4):
                                tiles = nc.values_load_multi_w_load_instructions(
                                    items4[1:2, ds(it * STEP4 + quarter * HALF4, HALF4)], [mybir.EngineType.DVE], min_val=0, max_val=NB - 1,
                                    skip_runtime_bounds_check_because="a tile's number is a count of at most NB - 1 buckets")[1]
                                for k in range(HALF4):
                                    u = quarter * HALF4 + k
                                    if quarter < 3:
                                        onehots(it, u + HALF4)
                                    else:
                                        onehots(it + 1, k)
                                    dve.wait_ge(s_prd, STEP4 + it * STEP4 + u + 1)
                                    dve.wait_ge(s_add, RING + it * STEP4 + u)
                                    there = agg[:, ds(tiles[k], 1), :].squeeze(1)
                                    nc.vector.tensor_tensor(there, there, psum[:, u % RING, 0:EA + 1], ALU.add).then_inc(s_add, 1)
                        dve.wait_ge(s_add, RING + NI4)
                        nc.vector.tensor_scalar(rcount[:, :], agg[:, :, EA], 1.0, None, ALU.max).then_inc(s_own4, 1)
                        dve.wait_ge(s_own4, own.n + 1)
                        nc.vector.reciprocal(rcount[:, :], rcount[:, :]).then_inc(s_own4, 1)

            with ExitStack() as ph6:
                gw1e = sb("gw1e", [EA, 4, P], f32, ph6)
                gw1u = sb("gw1u", [P, 4, P], f32, ph6)
                u0 = sb("u0", [P, 1], f32, ph6)
                gb1 = sb("gb1", [P, 4], f32, ph6)
                hbias = sb("hbias", [P, 4], f32, ph6)
                gw2 = sb("gw2", [P, 4, D], f32, ph6)
                gb2 = sb("gb2", [P, D], f32, ph6)
                fg = sb("fg", [P, 2, NX], f32, ph6)
                fbg = sb("fbg", [P, NX], f32, ph6)
                rev5 = sb("rev5", [P, NX], f32, ph6)
                rev5_i = sb("rev5_i", [P, NX], i32, ph6)
                xs5 = sb("xs5", [P, G, EA], f32, ph6)
                xs6 = sb("xs6", [P, G, D], f32, ph6)
                hx5 = sb("hx5", [P, 4, G * P], f32, ph6)
                aT5 = sb("aT5", [EA, G * P], f32, ph6)
                h5 = sb("h5", [P, 4, G * P], f32, ph6)
                yT5 = sb("yT5", [P, 2, G * P], f32, ph6)
                ln6 = {n: sb("ln6_" + n, s, f32, ph6) for n, s in
                       (("stats", [P, G, 6]), ("mv", [P, G, 2]), ("sd", [P, G]), ("rstd", [P, G]), ("nmr", [P, G]), ("nil", [P, 4]))}
                gt5 = {n: sb("gt5_" + n, [P, G, NX], f32, ph6) for n in ("g", "eq", "sc", "o1", "g2", "eq2", "sc2", "o2")}
                both6 = sb("both6", [P, G, NX], f32, ph6)
                cnt6 = sb("cnt6", [P, NX], f32, ph6)
                bas6 = sb("bas6", [P, NX], f32, ph6)
                pos6 = sb("pos6", [P, G, NX], f32, ph6)
                sel6 = sb("sel6", [P, 2, G, NX], f32, ph6)
                pl6 = sb("pl6", [P, 2, G], f32, ph6)
                id6 = sb("id6", [P, 2, G], i32, ph6)
                run_i = sb("run_i", [P, NX], i32, ph6)
                g5 = {n: sb("g5_" + n, [P, G], f32, ph6) for n in ("v1", "k1", "v2", "k2", "d", "x", "t", "w1", "w2")}
                s_c5 = sem("l1_constants")
                s_own5 = sem("l1_dense_vector_own")
                s_u5 = sem("l1_global_product")
                s_hadd = sem("l1_parts_added")
                s_o5 = sem("l1_node_products")
                s_x3 = sem("l1_rows_done")
                s_v6 = sem("moe_variance")
                s_sd6 = sem("moe_deviation")
                s_ln6 = sem("moe_rstd")
                s_y6 = sem("moe_normalised")
                s_t6 = sem("moe_transposed")
                s_tc6 = sem("moe_columns")
                s_lg6 = sem("moe_logits")
                s_gl6 = sem("moe_logits_copied")
                s_df6 = sem("moe_gate_gap")
                s_ex6 = sem("moe_gate_ratio")
                with nc.Block() as block:

                    @block.sync
                    def _(sp):
                        with nc.allow_non_contiguous_dma(reason="a few hundred biases"):
                            for dst, src in (
                                (gw1e[:, :, :], a["g_W1"][D:D + EA, :].rearrange("p (m n) -> p m n", n=P)),
                                (gw1u[:, :, :], a["g_W1"][D + EA:D + EA + P, :].rearrange("p (m n) -> p m n", n=P)),
                                (u0[:, :], a["g_u"][0, :].unsqueeze(1)),
                                (gb1[:, :], a["g_b1"].rearrange("(m p) -> p m", p=P)),
                                (gw2[:, :, :], a["g_W2"].rearrange("(m p) n -> p m n", p=P)),
                                (gb2[:, :], a["g_b2"].partition_broadcast(P)),
                                (fg[:, :, :], a["f_Wg"].rearrange("(c p) e -> p c e", p=P)),
                                (fbg[:, :], a["f_bg"].partition_broadcast(P)),
                            ):
                                sp.dma_start(dst, src).then_inc(s_w3, 16)
                        sp.dma_start(hx5[:, :, :].rearrange("p m n -> p (m n)"), hx_d[0:P, :]).then_inc(s_hx, 16)
                        for e in range(NX):
                            sp.dma_start(fw1[:, e, :, :], a["f_W1"][e].rearrange("(c p) n -> p c n", p=P)).then_inc(s_w7, 16)
                        with nc.allow_non_contiguous_dma(reason="the experts' biases by hidden unit"):
                            sp.dma_start(fb1[:, :, :], a["f_b1"].rearrange("e (m p) -> p e m", p=P)).then_inc(s_w7, 16)
                        sp.dma_start(fb2[:, :, :], a["f_b2"].partition_broadcast(P)).then_inc(s_w7, 16)
                        with sp.Fori(0, NG - 1) as g:
                            sp.wait_ge(s_hadd, g * 8 + 8)
                            sp.dma_start(hx5[:, :, :].rearrange("p m n -> p (m n)"), hx_d[ds((g + 1) * P, P), :]).then_inc(s_hx, 16)
                        sp.wait_ge(s_w3, 16 * (18 + 8))
                        sp.wait_ge(s_w7, 16 * (NX + 2))

                    @block.gpsimd
                    def _(pool):
                        pool.iota(rev5_i[:, :], pattern=[[-1, NX]], base=NX, channel_multiplier=0).then_inc(s_c5, 1)
                        pool.iota(run_i[:, :], pattern=[[CAP, NX]], base=-1, channel_multiplier=0).then_inc(s_c5, 1)
                        pool.sem_inc(s_free, 1)

                        def bias(g):
                            x = xr[:, ds(g * G, G), :]
                            pool.tensor_tensor(x, x, gb2[:, :].unsqueeze(1).to_broadcast([P, G, D]), ALU.add).then_inc(s_c5, 1)

                        pool.wait_ge(s_w3, 16 * (18 + 8))
                        bias(0)
                        bias(1)

                        def dispatch(g):
                            pool.wait_ge(s_pl7, g + 1)
                            alone(pool)
                            for k in range(G):
                                for n in range(2):
                                    pool.indirect_dma_start(
                                        out=xd_d, out_offset=bass.IndirectOffsetOnAxis(ap=id6[:, n, k:k + 1], axis=0),
                                        in_=xs6[:, k, :], in_offset=None).then_inc(s_dp[k], 16)
                            for k in range(G):
                                pool.wait_ge(s_dp[k], g * 32 + 32)
                            pool.sem_inc(s_free, 1)

                        with pool.Fori(0, NG - 2) as g:
                            dispatch(g)
                            bias(g + 2)
                        dispatch(NG - 2)
                        dispatch(NG - 1)

                    @block.scalar
                    def _(act):
                        act.wait_ge(s_w3, 16 * (18 + 8))

                        def deviation(ln, g, s_v, s_sd):
                            act.wait_ge(s_v, g + 1)
                            nc.scalar.activation(ln["sd"][:, :], ln["mv"][:, :, 1], ACT.Sqrt, bias=eps[:, :]).then_inc(s_sd, 1)

                        def node_rows(g):
                            for k in range(G):
                                t = g * G + k
                                nc.scalar.activation(xs5[:, k, :], agg[:, ds(t, 1), 0:EA].squeeze(1), ACT.Copy,
                                                     scale=rcount[:, ds(t, 1)]).then_inc(s_a5, 1)

                        def hidden(g, ns):
                            for n in ns:
                                m, (c0, c1) = n // 2, HALVES[n % 2]
                                act.wait_ge(s_hadd, g * 8 + n + 1)
                                nc.scalar.activation(h5[:, m, c0:c1], h5[:, m, c0:c1], ACT.Relu,
                                                     bias=hbias[:, m:m + 1]).then_inc(s_hc5, 1)

                        def gate_rows(g):
                            act.wait_ge(s_ln6, g + 1)
                            act.wait_ge(s_free, g + 1)
                            alone(act)
                            for k in range(G):
                                nc.scalar.activation(xs6[:, k, :], xr[:, ds(g * G + k, 1), :].squeeze(1), ACT.Identity,
                                                     bias=ln6["nmr"][:, k:k + 1], scale=ln6["rstd"][:, k:k + 1]).then_inc(s_y6, 1)

                        def ratio(g):
                            act.wait_ge(s_df6, g + 1)
                            nc.scalar.activation(g5["x"][:, :], g5["d"][:, :], ACT.Exp).then_inc(s_ex6, 1)

                        node_rows(0)
                        hidden(0, range(8))
                        act.wait_ge(s_t5, NG * G + G)
                        node_rows(1)
                        with act.Fori(0, NG - 2) as i:
                            g = i + 1
                            deviation(ln6, g - 1, s_v6, s_sd6)
                            gate_rows(g - 1)
                            hidden(g, range(8))
                            act.wait_ge(s_t5, NG * G + g * G + G)
                            alone(act)
                            node_rows(g + 1)
                            ratio(g - 1)
                        deviation(ln6, NG - 2, s_v6, s_sd6)
                        gate_rows(NG - 2)
                        hidden(NG - 1, range(8))
                        ratio(NG - 2)
                        deviation(ln6, NG - 1, s_v6, s_sd6)
                        gate_rows(NG - 1)
                        ratio(NG - 1)

                    @block.tensor
                    def _(pe):
                        pe.wait_ge(s_w3, 16 * (18 + 8))
                        for m in range(4):
                            last = nc.tensor.matmul(psum[:, 0, m:m + 1], gw1u[:, m, :], u0[:, :], start=True, stop=True)
                        last.then_inc(s_u5, 1)

                        def hidden(g):
                            for k in range(G):
                                pe.wait_ge(s_a5, NG * G + g * G + k + 1)
                                if k >= 2:
                                    pe.wait_ge(s_tc5, NG * G + g * G + k - 1)
                                alone(pe)
                                nc.tensor.transpose(psum[0:EA, k % 2, 0:P], xs5[:, k, :], ident[:, :]).then_inc(s_t5, 1)
                            pe.wait_ge(s_tc5, NG * G + g * G + G)
                            for n in range(8):
                                m, (c0, c1) = n // 2, HALVES[n % 2]
                                if n >= 4:
                                    pe.wait_ge(s_hadd, g * 8 + n - 3)
                                nc.tensor.matmul(psum[:, 4 + n % 4, 0:c1 - c0], gw1e[:, m, :], aT5[:, c0:c1], start=True, stop=True).then_inc(s_h5, 1)

                        def counts(g):
                            pe.wait_ge(s_n7, g + 1)
                            nc.tensor.matmul(psum[:, 3, 0:NX], ones[:, :], cnt6[:, :], start=True, stop=True)
                            nc.tensor.matmul(psum[:, 3, NX:2 * NX], upper[:, :], cnt6[:, :], start=True, stop=True).then_inc(s_o7, 1)

                        def nodes(g, before=None):
                            pe.wait_ge(s_hc5, NG * 8 + g * 8 + 8 + 1)
                            for k in range(G):
                                if k == 4 and before is not None:
                                    counts(before)
                                if k >= 4:
                                    pe.wait_ge(s_x3, g * G + k - 3)
                                for m in range(4):
                                    last = nc.tensor.matmul(psum[:, 4 + k % 4, 0:D], h5[:, m, k * P:(k + 1) * P], gw2[:, m, :], start=m == 0, stop=m == 3)
                                last.then_inc(s_o5, 1)

                        def gates(g):
                            for k in range(G):
                                pe.wait_ge(s_y6, g * G + k + 1)
                                if k >= 2:
                                    pe.wait_ge(s_tc6, g * G + k - 1)
                                for c in range(2):
                                    last = nc.tensor.transpose(psum[:, k % 2, c * P:(c + 1) * P], xs6[:, k, c * P:(c + 1) * P], ident[:, :])
                                last.then_inc(s_t6, 1)
                            pe.wait_ge(s_tc6, g * G + G)
                            pe.wait_ge(s_gl6, g + 1)
                            for k in range(G):
                                for c in range(2):
                                    last = nc.tensor.matmul(psum[:, 2, k * NX:(k + 1) * NX], yT5[:, c, k * P:(k + 1) * P], fg[:, c, :],
                                                            start=c == 0, stop=c == 1)
                            last.then_inc(s_lg6, 1)

                        pe.wait_ge(s_gl6, 1)
                        hidden(0)
                        nodes(0)
                        with pe.Fori(0, NG - 1) as i:
                            pe.wait_ge(s_x3, i * G + G)
                            hidden(i + 1)
                            gates(i)
                            nodes(i + 1, i)
                        gates(NG - 1)
                        counts(NG - 1)

                    @block.vector
                    def _(dve):
                        own = Chain(dve, s_own5)
                        dve.wait_ge(s_c5, 2)
                        own.add(nc.vector.tensor_copy(rev5[:, :], rev5_i[:, :]))
                        own.add(nc.vector.tensor_copy(run0[:, :], run_i[:, :]))
                        own.add(nc.vector.tensor_copy(run6[:, :], run_i[:, :]))
                        dve.wait_ge(s_u5, 1)
                        nc.vector.tensor_tensor(hbias[:, :], psum[:, 0, 0:4], gb1[:, :], ALU.add).then_inc(s_gl6, 1)

                        def node_columns(g):
                            for k in range(G):
                                dve.wait_ge(s_t5, NG * G + g * G + k + 1)
                                nc.vector.tensor_copy(aT5[:, k * P:(k + 1) * P], psum[0:EA, k % 2, 0:P]).then_inc(s_tc5, 1)

                        def add_parts(g):
                            dve.wait_ge(s_hx, NG * 16 + g * 16 + 16 + 1)
                            for n in range(8):
                                m, (c0, c1) = n // 2, HALVES[n % 2]
                                dve.wait_ge(s_h5, NG * 8 + g * 8 + n + 1)
                                nc.vector.tensor_tensor(h5[:, m, c0:c1], psum[:, 4 + n % 4, 0:c1 - c0], hx5[:, m, c0:c1], ALU.add).then_inc(s_hadd, 1)

                        def node_sums(g, ks=range(G)):
                            dve.wait_ge(s_c5, g + 3)
                            for k in ks:
                                dve.wait_ge(s_o5, g * G + k + 1)
                                x = xr[:, ds(g * G + k, 1), :].squeeze(1)
                                nc.vector.tensor_tensor(x, psum[:, 4 + k % 4, 0:D], x, ALU.add).then_inc(s_x3, 1)

                        def gate_columns(g):
                            for k in range(G):
                                dve.wait_ge(s_t6, g * G + k + 1)
                                nc.vector.tensor_copy(yT5[:, :, k * P:(k + 1) * P],
                                                      psum[:, k % 2, 0:2 * P].rearrange("p (c n) -> p c n", c=2)).then_inc(s_tc6, 1)

                        def gates(own, g):
                            dve.wait_ge(s_lg6, g + 1)
                            nc.vector.tensor_tensor(gt5["g"][:, :, :], psum[:, 2, 0:NX * G].rearrange("p (k e) -> p k e", e=NX),
                                                    fbg[:, :].unsqueeze(1).to_broadcast([P, G, NX]), ALU.add).then_inc(s_gl6, 1)
                            dve.wait_ge(s_gl6, g + 2)
                            top_two(own, gt5, g5, rev5, NX)
                            nc.vector.tensor_tensor(g5["d"][:, :], g5["v2"][:, :], g5["v1"][:, :], ALU.subtract).then_inc(s_df6, 1)
                            dve.wait_ge(s_ex6, g + 1)
                            two_weights(own, g5)
                            for to, of in ((wt1, "w1"), (wt2, "w2")):
                                own.add(nc.vector.tensor_copy(to[:, ds(g * G, G)], g5[of][:, :]))
                            own.add(nc.vector.tensor_tensor(both6[:, :, :], gt5["o1"][:, :, :], gt5["o2"][:, :, :], ALU.add))
                            own.sync()
                            nc.vector.tensor_reduce(cnt6[:, :], both6[:, :, :].rearrange("p t e -> p e t"), AX.X, ALU.add).then_inc(s_n7, 1)

                        def places(own, g):
                            dve.wait_ge(s_o7, g + 1)
                            own.add(nc.vector.tensor_tensor(bas6[:, :], psum[:, 3, NX:2 * NX], run6[:, :], ALU.add))
                            own.sync()
                            own.add(nc.vector.tensor_tensor(run6[:, :], psum[:, 3, 0:NX], run6[:, :], ALU.add))
                            for e in range(NX):
                                own.add(nc.vector.tensor_tensor_scan(pos6[:, :, e], both6[:, :, e], both6[:, :, e], bas6[:, e:e + 1], ALU.add, ALU.bypass))
                            own.sync()
                            for n, of in enumerate(("o1", "o2")):
                                own.add(nc.vector.tensor_tensor(sel6[:, n, :, :], gt5[of][:, :, :], pos6[:, :, :], ALU.mult))
                            own.sync()
                            for n in range(2):
                                own.add(nc.vector.tensor_reduce(pl6[:, n, :], sel6[:, n, :, :], AX.X, ALU.add))
                            own.sync()
                            own.add(nc.vector.tensor_copy(place_i[:, :, ds(g * G, G)], pl6[:, :, :]))
                            nc.vector.tensor_copy(id6[:, :, :], pl6[:, :, :]).then_inc(s_pl7, 1)
                            own.sync()

                        own.sync()
                        node_columns(0)
                        add_parts(0)
                        node_sums(0)
                        first = own.n
                        def step(own, g):
                            node_columns(g)
                            dve.wait_ge(s_x3, g * G)
                            normalise(dve, own, xr, g - 1, ln6, s_v6, s_sd6, s_ln6)
                            add_parts(g)
                            gate_columns(g - 1)
                            gates(own, g - 1)
                            node_sums(g, range(4))
                            places(own, g - 1)
                            node_sums(g, range(4, G))

                        with dve.Fori(0, NG - 2) as i:
                            own = Chain(dve, s_own5, first + i * DENSE1_OWN)
                            step(own, i + 1)
                            assert own.n == DENSE1_OWN, own.n
                        own = Chain(dve, s_own5, first + (NG - 2) * DENSE1_OWN)
                        step(own, NG - 1)
                        dve.wait_ge(s_x3, NG * G)
                        normalise(dve, own, xr, NG - 1, ln6, s_v6, s_sd6, s_ln6)
                        gate_columns(NG - 1)
                        gates(own, NG - 1)
                        places(own, NG - 1)

        with ExitStack() as ph7:
            etab = sb("etab", [1, NBLK + 2], i32, weights)
            rtab = sb("rtab", [1, NBLK + 2], i32, weights)
            fw2 = sb("fw2", [P, NX, HX // P, D], f32, weights)
            with ExitStack() as ph8:
                zero8 = sb("zero8", [P, D], f32, ph8)
                part_i = sb("part_i", [P, NX], i32, ph8)
                part_f = sb("part_f", [P, NX], f32, ph8)
                pad_f = sb("pad_f", [P, NX], f32, ph8)
                pad_i = sb("pad_i", [P, NX], i32, ph8)
                nb_f = sb("nb_f", [P, NX], f32, ph8)
                nb_i = sb("nb_i", [P, NX], i32, ph8)
                nb_s = sb("nb_s", [P, NX], i32, ph8)
                end8 = sb("end8", [P, NX], f32, ph8)
                jump8 = sb("jump8", [P, NX], f32, ph8)
                blk_i = sb("blk_i", [1, NBLK + 2], i32, ph8)
                blk_f = sb("blk_f", [1, NBLK + 2], f32, ph8)
                row_b = sb("row_b", [1, NBLK + 2], f32, ph8)
                ge8 = sb("ge8", [1, NBLK + 2, NX], f32, ph8)
                far_f = sb("far_f", [P, 2, NT], f32, ph8)
                near_f = sb("near_f", [P, 2, NT], f32, ph8)
                back_f = sb("back_f", [P, NX, 2, NT], f32, ph8)
                with nc.Block() as block:

                    @block.sync
                    def _(sp):
                        for e in range(NX):
                            sp.dma_start(fw2[:, e, :, :], a["f_W2"][e].rearrange("(m p) n -> p m n", p=P)).then_inc(s_w7, 16)

                    @block.vector
                    def _(dve):
                        own = Chain(dve, s_own4, 4)
                        nc.vector.memset(zero8[:, :], 0.0).then_inc(s_n7, 1)
                        dve.wait_ge(s_c5, NG + 4)
                        own.add(nc.vector.tensor_copy(blk_f[:, :], blk_i[:, :]))
                        own.add(nc.vector.tensor_scalar(part_f[:, :], part_i[:, :], 1.0, None, ALU.add))
                        own.sync()
                        own.add(nc.vector.tensor_tensor(pad_f[:, :], part_f[:, :], run6[:, :], ALU.add))
                        own.sync()
                        nc.vector.tensor_copy(pad_i[:, :], pad_f[:, :]).then_inc(s_pl7, 1)
                        own.add(nc.vector.tensor_tensor(nb_f[:, :], run6[:, :], run0[:, :], ALU.subtract))
                        own.sync()
                        own.add(nc.vector.tensor_scalar(nb_i[:, :], nb_f[:, :], float(P - 1), None, ALU.add))
                        own.sync()
                        own.add(nc.vector.tensor_scalar(nb_s[:, :], nb_i[:, :], 7, None, ALU.arith_shift_right))
                        own.sync()
                        own.add(nc.vector.tensor_copy(nb_f[:, :], nb_s[:, :]))
                        own.sync()
                        own.add(nc.vector.tensor_tensor_scan(end8[:, :], nb_f[:, :], nb_f[:, :], 0.0, ALU.add, ALU.bypass))
                        own.add(nc.vector.tensor_scalar(jump8[:, :], nb_f[:, :], -float(P), float(CAP), ALU.mult, ALU.add))
                        own.sync()
                        own.add(nc.vector.tensor_tensor(ge8[:, :, :], end8[0:1, :].unsqueeze(1).to_broadcast([1, NBLK + 2, NX]),
                                                        blk_f[:, :].unsqueeze(2).to_broadcast([1, NBLK + 2, NX]), ALU.is_le))
                        own.sync()
                        own.add(nc.vector.tensor_reduce(row_b[:, :], ge8[:, :, 0:NX - 1], AX.X, ALU.add))
                        own.sync()
                        own.add(nc.vector.tensor_copy(etab[:, :], row_b[:, :]))
                        own.add(nc.vector.tensor_tensor(ge8[:, :, :], ge8[:, :, :], jump8[0:1, :].unsqueeze(1).to_broadcast([1, NBLK + 2, NX]), ALU.mult))
                        own.sync()
                        own.add(nc.vector.tensor_reduce(row_b[:, :], ge8[:, :, :], AX.X, ALU.add))
                        own.sync()
                        own.add(nc.vector.scalar_tensor_tensor(row_b[:, :], blk_f[:, :], float(P), row_b[:, :], ALU.mult, ALU.add))
                        own.sync()
                        own.add(nc.vector.tensor_copy(rtab[:, :], row_b[:, :]))
                        own.add(nc.vector.tensor_copy(far_f[:, :, :], place_i[:, :, :]))
                        own.add(nc.vector.tensor_copy(near_f[:, :, :], place_i[:, :, :]))
                        own.sync()
                        for e in range(1, NX):
                            own.add(nc.vector.tensor_scalar(back_f[:, e, :, :], far_f[:, :, :], float(e * CAP), jump8[:, e - 1:e], ALU.is_ge, ALU.mult))
                        own.sync()
                        for e in range(1, NX):
                            own.add(nc.vector.tensor_tensor(near_f[:, :, :], near_f[:, :, :], back_f[:, e, :, :], ALU.subtract))
                            own.sync()
                        own.add(nc.vector.tensor_copy(place_i[:, :, :], near_f[:, :, :]))
                        own.sync()

                    @block.gpsimd
                    def _(pool):
                        pool.iota(blk_i[:, :], pattern=[[1, NBLK + 2]], base=0, channel_multiplier=0).then_inc(s_c5, 1)
                        pool.iota(part_i[:, :], pattern=[[0, NX]], base=0, channel_multiplier=1).then_inc(s_c5, 1)
                        pool.wait_ge(s_n7, NG + 1)
                        pool.wait_ge(s_pl7, NG + 1)
                        for e in range(NX):
                            pool.indirect_dma_start(out=xd_d, out_offset=bass.IndirectOffsetOnAxis(ap=pad_i[:, e:e + 1], axis=0),
                                                    in_=zero8[:, :], in_offset=None).then_inc(s_pad, 16)
                        pool.wait_ge(s_pad, 16 * NX)

            with ExitStack() as ph9:
                xb = sb("xb", [P, 2, D], f32, ph9)
                xbT = sb("xbT", [P, 2, 2, P], f32, ph9)
                hs = sb("hs", [P, HX], f32, ph9)
                hT = sb("hT", [P, HX // P, P], f32, ph9)
                yb = sb("yb", [P, 2, D], f32, ph9)
                s_in = [sem(f"block_loaded{u}") for u in range(2)]
                s_xt = sem("block_transposed")
                s_xc = sem("block_columns")
                s_m1 = sem("block_hidden_products")
                s_hsa = sem("block_hidden_half_a")
                s_hsd = sem("block_hidden_half_d")
                s_ht = sem("block_hidden_transposed")
                s_hta = sem("block_relu_a")
                s_htd = sem("block_relu_d")
                s_m2 = sem("block_products")
                s_yb = sem("block_rows")
                s_yo = [sem(f"block_stored{u}") for u in range(2)]
                M = HX // P
                with nc.Block() as block:

                    @block.sync
                    def _(sp):
                        for u in range(2):
                            first = sp.value_load(rtab[0:1, u:u + 1], min_val=0, max_val=NX * CAP + (SPARE - 1) * P)
                            sp.dma_start(xb[:, u, :], xd_d[ds(first, P), :]).then_inc(s_in[u], 16)
                        with sp.Fori(0, NBLK // 2) as it:
                            for u in range(2):
                                first = sp.value_load(rtab[0:1, ds(it * 2 + u + 2, 1)], min_val=0, max_val=NX * CAP + (SPARE - 1) * P)
                                sp.wait_ge(s_xt, it * 2 + u + 1)
                                sp.dma_start(xb[:, u, :], xd_d[ds(first, P), :]).then_inc(s_in[u], 16)

                    @block.tensor
                    def _(pe):
                        def transpose_x(j, u, n):
                            pe.wait_ge(s_in[u], n)
                            if not isinstance(j, int) or j > 0:
                                pe.wait_ge(s_xc, j)
                            for c in range(2):
                                last = nc.tensor.transpose(psum[:, 0, c * P:(c + 1) * P], xb[:, u, c * P:(c + 1) * P], ident[:, :])
                            last.then_inc(s_xt, 1)

                        def hidden(j, u, e):
                            pe.wait_ge(s_xc, j + 1)
                            for half in range(2):
                                for c in range(2):
                                    last = nc.tensor.matmul(psum[:, 1 + half, :], xbT[:, u, c, :],
                                                            fw1[:, ds(e, 1), c, half * 512:(half + 1) * 512].squeeze(1), start=c == 0, stop=c == 1)
                                last.then_inc(s_m1, 1)

                        def expert(j):
                            return pe.value_load(etab[0:1, ds(j, 1)], min_val=0, max_val=NX - 1)

                        transpose_x(0, 0, 16)
                        transpose_x(1, 1, 16)
                        e0 = expert(0)
                        hidden(0, 0, e0)
                        pe.wait_ge(s_w7, 16 * (2 * NX + 2))
                        pe.sem_inc(s_yb, 1)
                        with pe.Fori(0, NBLK // 2) as it:
                            for u in range(2):
                                j = it * 2 + u
                                pe.wait_ge(s_hsa, j + 1)
                                pe.wait_ge(s_hsd, j + 1)
                                for m in range(M):
                                    last = nc.tensor.transpose(psum[:, 3 + m // 4, m % 4 * P:(m % 4 + 1) * P], hs[:, m * P:(m + 1) * P], ident[:, :])
                                    if m % 4 == 3:
                                        last.then_inc(s_ht, 1)
                                transpose_x(j + 2, u, it * 16 + 32)
                                nxt = expert(j + 1)
                                hidden(j + 1, 1 - u, nxt)
                                now = expert(j)
                                pe.wait_ge(s_hta, j * 4 + 4)
                                pe.wait_ge(s_htd, j * 4 + 4)
                                pe.wait_ge(s_yb, j + 1)
                                for m in range(M):
                                    last = nc.tensor.matmul(psum[:, 5, 0:D], hT[:, m, :], fw2[:, ds(now, 1), m, :].squeeze(1), start=m == 0, stop=m == M - 1)
                                last.then_inc(s_m2, 1)

                    @block.scalar
                    def _(act):
                        def copy_hidden(j):
                            act.wait_ge(s_m1, 2 * j + 1)
                            nc.scalar.activation(hs[:, 0:512], psum[:, 1, :], ACT.Copy).then_inc(s_hsa, 1)

                        copy_hidden(0)
                        act.sem_inc(s_m2, 1)
                        with act.Fori(0, NBLK // 2) as it:
                            for u in range(2):
                                j = it * 2 + u
                                e = act.value_load(etab[0:1, ds(j, 1)], min_val=0, max_val=NX - 1)
                                act.wait_ge(s_ht, 2 * j + 1)
                                act.wait_ge(s_m2, j + 1)
                                alone(act)
                                for m in range(4):
                                    nc.scalar.activation(hT[:, m, :], psum[:, 3, m * P:(m + 1) * P], ACT.Relu,
                                                         bias=fb1[:, ds(e, 1), m]).then_inc(s_hta, 1)
                                act.wait_ge(s_ht, 2 * j + 2)
                                copy_hidden(j + 1)
                                act.wait_ge(s_yb, j + 2)
                                act.dma_start(yd_d[ds(it * (2 * P) + u * P, P), :], yb[:, u, :]).then_inc(s_yo[u], 16)
                        for u in range(2):
                            act.wait_ge(s_yo[u], 16 * (NBLK // 2) + 1)

                    @block.vector
                    def _(dve):
                        def columns(j, u):
                            dve.wait_ge(s_xt, j + 1)
                            nc.vector.tensor_copy(xbT[:, u, :, :].rearrange("p c n -> p (c n)"), psum[:, 0, 0:2 * P]).then_inc(s_xc, 1)

                        def copy_hidden(j):
                            dve.wait_ge(s_m1, 2 * j + 2)
                            nc.vector.tensor_copy(hs[:, 512:1024], psum[:, 2, :]).then_inc(s_hsd, 1)

                        columns(0, 0)
                        columns(1, 1)
                        copy_hidden(0)
                        for u in range(2):
                            dve.sem_inc(s_yo[u], 1)
                        with dve.Fori(0, NBLK // 2) as it:
                            for u in range(2):
                                j = it * 2 + u
                                e = dve.value_load(etab[0:1, ds(j, 1)], min_val=0, max_val=NX - 1)
                                dve.wait_ge(s_ht, 2 * j + 2)
                                dve.wait_ge(s_m2, j + 1)
                                alone(dve)
                                for m in range(4, M):
                                    nc.vector.tensor_scalar(hT[:, m, :], psum[:, 4, (m - 4) * P:(m - 3) * P], fb1[:, ds(e, 1), m], 0.0,
                                                            ALU.add, ALU.max).then_inc(s_htd, 1)
                                columns(j + 2, u)
                                copy_hidden(j + 1)
                                dve.wait_ge(s_m2, j + 2)
                                dve.wait_ge(s_yo[u], it * 16 + 1)
                                nc.vector.tensor_tensor(yb[:, u, :], psum[:, 5, 0:D], fb2[:, ds(e, 1), :].squeeze(1), ALU.add).then_inc(s_yb, 1)

            weights.close()
            with ExitStack() as ph10:
                yg = sb("yg", [P, G, 2, D], f32, ph10)
                id10 = sb("id10", [P, 2, 2, G], i32, ph10)
                fin = sb("fin", [P, G, D], f32, ph10)
                s_p1 = sem("first_result_added")
                s_fin = sem("rows_finished")
                s_out = sem("rows_stored_out")
                with nc.Block() as block:

                    @block.gpsimd
                    def _(pool):
                        pool.sem_inc(s_fin, FIN0)

                        def gather(g, half):
                            pool.wait_ge(s_fin, FIN0 - G + g * G)
                            alone(pool)
                            pool.tensor_copy(id10[:, half, :, :], place_i[:, :, ds(g * G, G)]).then_inc(s_id7, 1)
                            pool.wait_ge(s_id7, g + 1)
                            for k in range(G):
                                pool.wait_ge(s_fin, FIN0 - G + g * G + k + 1)
                                alone(pool)
                                for n in range(2):
                                    pool.indirect_dma_start(
                                        out=yg[:, k, n, :], out_offset=None, in_=yd_d,
                                        in_offset=bass.IndirectOffsetOnAxis(ap=id10[:, half, n, k:k + 1], axis=0)).then_inc(s_dp[k], 16)

                        with pool.Fori(0, NG // 2) as it:
                            gather(it * 2, 0)
                            gather(it * 2 + 1, 1)
                        gather(NG - 1, 0)

                    @block.vector
                    def _(dve):
                        dve.sem_inc(s_out, 1)
                        with dve.Fori(0, NG) as g:
                            dve.wait_ge(s_out, g * 16 + 1)
                            for k in range(G):
                                t = g * G + k
                                dve.wait_ge(s_dp[k], DISPATCHED + g * 32 + 32)
                                alone(dve)
                                nc.vector.scalar_tensor_tensor(fin[:, k, :], yg[:, k, 0, :], wt1[:, ds(t, 1)], xr[:, ds(t, 1), :].squeeze(1),
                                                               ALU.mult, ALU.add).then_inc(s_p1, 1)
                                dve.wait_ge(s_p1, t + 1)
                                alone(dve)
                                nc.vector.scalar_tensor_tensor(fin[:, k, :], yg[:, k, 1, :], wt2[:, ds(t, 1)], fin[:, k, :],
                                                               ALU.mult, ALU.add).then_inc(s_fin, 1)

                    @block.sync
                    def _(sp):
                        y = out["y"]
                        with sp.Fori(0, NG - 1) as g:
                            sp.wait_ge(s_fin, FIN0 + g * G + G)
                            sp.dma_start(y[ds(g * (G * P), G * P), :].rearrange("(t p) d -> p t d", p=P), fin[:, :, :]).then_inc(s_out, 16)
                        sp.wait_ge(s_fin, FIN0 + NT)
                        first = (NG - 1) * G * P
                        sp.dma_start(y[first:first + (G - 1) * P, :].rearrange("(t p) d -> p t d", p=P), fin[:, 0:G - 1, :]).then_inc(s_out, 16)
                        sp.dma_start(y[first + (G - 1) * P:N, :], fin[0:N - first - (G - 1) * P, G - 1, :]).then_inc(s_out, 16)
                        sp.wait_ge(s_out, 16 * (NG + 1) + 1)


def kernel(**inputs):
    import numpy as _np
    import concourse.bacc as _bacc
    from concourse import mybir as _mybir
    from concourse.bass_utils import run_bass_kernel_spmd as _run

    given = {name: _np.asarray(v) for name, v in inputs.items()}
    arrays = {
        "x": _np.pad(given["x"], ((0, NP - N), (0, 0))),
        "src": _np.pad(given["src"], (0, EP - E), constant_values=PAD_KEY),
        "dst": _np.pad(given["dst"], (0, EP - E), constant_values=PAD_KEY),
        "w": _np.pad(given["edge_weight"], (0, EP - E)),
        "attr": _np.pad(given["edge_attr_64"], ((0, EP - E), (0, 0))),
        "w_self": given["L0_gnn_w_self"].transpose(1, 0),
        "w_neigh": given["L0_gnn_w_neigh"].transpose(1, 0),
        "f_Wg": given["L1_ffn_Wg"].transpose(1, 0),
        "f_W1": given["L1_ffn_W1"].transpose(0, 2, 1),
        "f_W2": given["L1_ffn_W2"].transpose(0, 2, 1),
    }
    for name in ("sW1", "sb1", "sW2", "sb2", "sW3", "sb3", "eW1", "eb1", "eW2", "eb2", "eW3", "eb3", "gW", "gb"):
        arrays[name] = given["L0_ffn_" + name]
    for name in ("u", "W1", "b1", "W2", "b2"):
        arrays["g_" + name] = given["L1_gnn_" + name]
    for name in ("bg", "b1", "b2"):
        arrays["f_" + name] = given["L1_ffn_" + name]

    nc = _bacc.Bacc("TRN2", target_bir_lowering=False, num_devices=1)
    laid, aps = {}, {}
    for name, v in arrays.items():
        v = _np.ascontiguousarray(v)
        laid[f"in_{name}_dram"] = v
        aps[name] = nc.dram_tensor(f"in_{name}_dram", v.shape, _mybir.dt.from_np(v.dtype), kind="ExternalInput").ap()
    y = nc.dram_tensor("out_y_dram", (N, D), _mybir.dt.from_np(_np.dtype("float32")), kind="ExternalOutput").ap()
    build(nc, aps, {"y": y})
    r = _run(nc, [laid], core_ids=[0])
    return r.results[0]["out_y_dram"]
```
